# Optimizing a Trainium2 kernel written in Bass

```python
import numpy as np
import jax
import jax.numpy as jnp

def _softmax(x, axis=-1):
    return jax.nn.softmax(x, axis=axis)

def _gelu(x):
    return jax.nn.gelu(x, approximate=True)

def _silu(x):
    return jax.nn.silu(x)

def _sigmoid(x):
    return jax.nn.sigmoid(x)

def _layernorm(x, axis=-1, eps=1e-05):
    m = jnp.mean(x, axis=axis, keepdims=True)
    v = jnp.var(x, axis=axis, keepdims=True)
    return (x - m) / jnp.sqrt(v + eps)

def _scatter_add(tgt, idx, src, axis=0):
    return tgt.at[idx].add(src)

def _segment_sum(src, seg, n):
    return jax.ops.segment_sum(src, seg, n)
kernel_name = 'mk_flamingo_gated_d1_seqx_r8_244991'

def setup_inputs(seed: int=0):
    np.random.seed(seed)
    _w = jnp.asarray

    def _rec_inputs():
        import jax
        import jax.numpy as jnp
        _rk = jax.random.key(seed)
        x = 7.22e-05 + 1 * jax.random.normal(jax.random.fold_in(_rk, 1), (2, 512, 128), jnp.float32)
        _lenS = 512 - jax.random.randint(jax.random.fold_in(_rk, 7), (2,), 0, max(1, 512 // 4) + 1, jnp.int32)
        _lenS2 = 154 - jax.random.randint(jax.random.fold_in(_rk, 8), (2,), 0, max(1, 154 // 4) + 1, jnp.int32)
        _ctx_768P = jax.random.normal(jax.random.fold_in(_rk, 11), (2, 16, 96), jnp.float32)
        _ctx_768c = jax.random.dirichlet(jax.random.fold_in(_rk, 511), 0.3 * jnp.ones((16,), jnp.float32), (2, 154))
        _ctx_768t = jnp.einsum('bsk,bkd->bsd', _ctx_768c, _ctx_768P)
        _ctx_768t = _ctx_768t * jax.lax.rsqrt(jnp.mean(jnp.square(_ctx_768t)) + 1e-12) * 0.953939
        ctx_768 = -0.000191848 + 0.999787 * (_ctx_768t + 0.3 * jax.random.normal(jax.random.fold_in(_rk, 611), (2, 154, 96), jnp.float32))
        _g = jax.random.normal(jax.random.fold_in(_rk, 9001), (2, 1), jnp.float32)
        _g = jnp.sign(_g) * jnp.maximum(jnp.abs(_g), 1.0) + (_g == 0) * 1.0
        g_xattn = _g[0]
        g_ffn = _g[1]
        return (x, ctx_768, g_xattn, g_ffn)
    x, ctx_768, g_xattn, g_ffn = _rec_inputs()

    def _L0_xattn_setup():
        import jax, jax.numpy as jnp
        import numpy as np
        NUM_HEADS = 16
        CLAMP = 10000.0
        key = jax.random.key(seed)
        ks = jax.random.split(key, 8)
        B, Nq, Nkv, Cq, Ckv = (4, 256, 256, 128, 96)
        s_q = 1.0 / np.sqrt(Cq)
        s_kv = 1.0 / np.sqrt(Ckv)
        return {'query': jax.random.normal(ks[0], (B, Nq, Cq), jnp.float32), 'key_value': jax.random.normal(ks[1], (B, Nkv, Ckv), jnp.float32), 'Wq': jax.random.normal(ks[2], (Cq, Cq), jnp.float32) * s_q, 'bq': jnp.zeros((Cq,), jnp.float32), 'Wk': jax.random.normal(ks[3], (Ckv, Cq), jnp.float32) * s_kv, 'bk': jnp.zeros((Cq,), jnp.float32), 'Wv': jax.random.normal(ks[4], (Ckv, Cq), jnp.float32) * s_kv, 'bv': jnp.zeros((Cq,), jnp.float32), 'Wo': jax.random.normal(ks[5], (Cq, Cq), jnp.float32) * s_q, 'bo': jnp.zeros((Cq,), jnp.float32)}
    _L0_xattn_all = _L0_xattn_setup()
    _L0_xattn_in = {k: v for k, v in _L0_xattn_all.items() if k in ('Wq', 'bq', 'Wk', 'bk', 'Wv', 'bv', 'Wo', 'bo')}
    del _L0_xattn_all

    def _L0_ffn_setup():
        import jax, jax.numpy as jnp
        import numpy as np
        NUM_EXPERTS = 8
        N_EMBD = 128
        D_FF = 4 * N_EMBD
        B, S = (4, 256)
        key = jax.random.key(seed)
        ks = jax.random.split(key, 6)
        x = jax.random.normal(ks[0], (B, S, N_EMBD), dtype=jnp.float32)
        gate_w = jax.random.normal(ks[1], (N_EMBD, NUM_EXPERTS), dtype=jnp.float32) * 0.02
        w1 = jax.random.normal(ks[2], (NUM_EXPERTS, N_EMBD, D_FF), dtype=jnp.float32) * 0.02
        b1 = jnp.zeros((NUM_EXPERTS, D_FF), dtype=jnp.float32)
        w2 = jax.random.normal(ks[3], (NUM_EXPERTS, D_FF, N_EMBD), dtype=jnp.float32) * 0.02
        b2 = jnp.zeros((NUM_EXPERTS, N_EMBD), dtype=jnp.float32)
        return {'x': x, 'gate_w': gate_w, 'w1': w1, 'b1': b1, 'w2': w2, 'b2': b2}
    _L0_ffn_all = _L0_ffn_setup()
    _L0_ffn_in = {k: v for k, v in _L0_ffn_all.items() if k in ('gate_w', 'w1', 'b1', 'w2', 'b2')}
    del _L0_ffn_all
    return {'x': x, 'ctx_768': ctx_768, 'g_xattn': g_xattn, 'g_ffn': g_ffn, 'L0_xattn_Wq': _L0_xattn_in['Wq'], 'L0_xattn_bq': _L0_xattn_in['bq'], 'L0_xattn_Wk': _L0_xattn_in['Wk'], 'L0_xattn_bk': _L0_xattn_in['bk'], 'L0_xattn_Wv': _L0_xattn_in['Wv'], 'L0_xattn_bv': _L0_xattn_in['bv'], 'L0_xattn_Wo': _L0_xattn_in['Wo'], 'L0_xattn_bo': _L0_xattn_in['bo'], 'L0_ffn_gate_w': _L0_ffn_in['gate_w'], 'L0_ffn_w1': _L0_ffn_in['w1'], 'L0_ffn_b1': _L0_ffn_in['b1'], 'L0_ffn_w2': _L0_ffn_in['w2'], 'L0_ffn_b2': _L0_ffn_in['b2']}

def reference(x, ctx_768, g_xattn, g_ffn, L0_xattn_Wq, L0_xattn_bq, L0_xattn_Wk, L0_xattn_bk, L0_xattn_Wv, L0_xattn_bv, L0_xattn_Wo, L0_xattn_bo, L0_ffn_gate_w, L0_ffn_w1, L0_ffn_b1, L0_ffn_w2, L0_ffn_b2):
    import jax
    import jax.numpy as jnp

    def _L0_xattn_ref(query, key_value, Wq, bq, Wk, bk, Wv, bv, Wo, bo):
        import jax, jax.numpy as jnp
        import numpy as np
        NUM_HEADS = 16
        CLAMP = 10000.0
        B, Nq, Cq = query.shape
        Nkv = key_value.shape[1]
        H = NUM_HEADS
        D = Cq // H
        scale = D ** (-0.5)
        q = (query @ Wq + bq).reshape(B, Nq, H, D).transpose(0, 2, 1, 3)
        k = (key_value @ Wk + bk).reshape(B, Nkv, H, D).transpose(0, 2, 1, 3)
        v = (key_value @ Wv + bv).reshape(B, Nkv, H, D).transpose(0, 2, 1, 3)
        attn = jnp.einsum('bhqd,bhkd->bhqk', q, k) * scale
        attn = jnp.clip(attn, -CLAMP, CLAMP)
        attn = jax.nn.softmax(attn, axis=-1)
        attn = jnp.where(jnp.any(jnp.isnan(attn)), jnp.asarray(1.0 / Nkv, attn.dtype), attn)
        x = jnp.einsum('bhqk,bhkd->bqhd', attn, v).reshape(B, Nq, Cq)
        return x @ Wo + bo

    def _L0_ffn_ref(x, gate_w, w1, b1, w2, b2):
        import jax, jax.numpy as jnp
        import numpy as np
        NUM_EXPERTS = 8
        N_EMBD = 128
        D_FF = 4 * N_EMBD
        B, S = (4, 256)
        Bb, Ss, D = x.shape
        x_flat = x.reshape(-1, D)
        router_logits = x_flat @ gate_w
        router_probs = jax.nn.softmax(router_logits, axis=-1)
        expert_idx = jnp.argmax(router_probs, axis=-1)
        expert_w = jnp.take_along_axis(router_probs, expert_idx[:, None], axis=1)[:, 0]
        out = jnp.zeros_like(x_flat)
        for e in range(NUM_EXPERTS):
            h = jax.nn.gelu(x_flat @ w1[e] + b1[e], approximate=False)
            y = h @ w2[e] + b2[e]
            sel = expert_idx == e
            out = out + jnp.where(sel, expert_w, 0.0)[:, None] * y
        return out.reshape(Bb, Ss, D)
    x = x + jnp.tanh(g_xattn[0]) * _L0_xattn_ref(_layernorm(x, axis=-1), ctx_768, L0_xattn_Wq, L0_xattn_bq, L0_xattn_Wk, L0_xattn_bk, L0_xattn_Wv, L0_xattn_bv, L0_xattn_Wo, L0_xattn_bo)
    x = x + jnp.tanh(g_ffn[0]) * _L0_ffn_ref(_layernorm(x, axis=-1), L0_ffn_gate_w, L0_ffn_w1, L0_ffn_b1, L0_ffn_w2, L0_ffn_b2)
    return x

_drawn_inputs = setup_inputs


def setup_inputs(seed=0):
    import zlib

    import numpy as np

    out = dict(_drawn_inputs(seed))
    spreads = {'L0_xattn_bq': (0.0, 0.492),
     'L0_xattn_bk': (0.0, 0.8),
     'L0_xattn_bv': (0.0, 0.1),
     'L0_xattn_bo': (0.0, 0.1),
     'L0_ffn_b1': (0.0, 0.8),
     'L0_ffn_b2': (0.0, 0.52)}
    factors = {'L0_ffn_gate_w': 3.443, 'L0_ffn_w1': 6.788, 'L0_ffn_w2': 6.158}
    for name, (base, spread) in spreads.items():
        noise = np.random.default_rng([zlib.crc32(name.encode()), seed]).standard_normal(out[name].shape)
        drawn = base * np.exp(spread * noise) if base else spread * noise
        out[name] = jnp.asarray(drawn.astype(out[name].dtype))
    for name, factor in factors.items():
        out[name] = (out[name] * factor).astype(out[name].dtype)
    return out
```

```python
from contextlib import ExitStack

import concourse.bass as bass
from concourse import mybir

F32 = mybir.dt.float32
BF16 = mybir.dt.bfloat16
I32 = mybir.dt.int32
ALU = mybir.AluOpType
ACT = mybir.ActivationFunctionType
AX = mybir.AxisListType

P = 128
NB, NQ, C = 2, 512, 128
NK, CK = 154, 96
H, D = 16, 8
T = NB * NQ // P
TB = NQ // P
KL = NK - P
G, J = 4, 4
PR = H // 2
RB = 3
NBLK = T + 7
ROW = 2 * C + 4
STK = 96
NC = 6
QPART = (0, 0, 0, 1, 1, 2)
KPART = (0, 1, 2, 0, 1, 0)
KW = NB * C + NB * C // 2
U, UT = 4, 2
UQ = UT * P
AHEAD = 8
CH = 5 * G
E, FF = 8, 512
FC = FF // P
SCALE = float(D) ** -0.5
EPS = 1e-5


def plan():
    steps = [("ctxT", 0, 0), ("xT", 0, 0), ("k", 0, 0), ("q", 0, 0), ("kT", 0, 0), ("qT", 0, 0), ("kLT", 0, 0)]
    first = [("max", 0, k) for k in range(5 * UT)]
    steps += first[:4] + [("xT", 1, 0)] + first[4:] + [("q", 1, 0), ("shift", 0, 0), ("v", 0, 0), ("qT", 1, 0)]
    at = {}

    def put(when, *step):
        at.setdefault(when, []).append(step)

    for u in range(U):
        t0 = CH * u
        if u + 1 < U:
            for k in range(5 * UT):
                put(t0 + PLAN["max0"] + k * PLAN["maxn"] // 8, "max", u + 1, k)
            put(t0 + PLAN["shift"], "shift", u + 1, 0)
        if u + 2 < U:
            put(t0 + PLAN["q"], "q", u + 2, 0)
            put(t0 + PLAN["qT"], "qT", u + 2, 0)
        if u == 0:
            put(t0 + PLAN["kT"], "kT", 1, 0)
        for g in range(G):
            full = 4 * ((5 * g + 4) // 4) + 3
            when = t0 + full + PLAN["pv"]
            put(when, "pv", u, g)
            put(when + PLAN["turn"], "turn", u, g)
        when += PLAN["turn"]
        for kind in ("back", "out", "normedT", "route"):
            when += PLAN[kind]
            put(when, kind, u, 0)
    for n in range(max(at) + 1):
        if n < U * CH:
            steps.append(("score", n // CH, n % CH))
        steps += at.get(n, [])
    return steps


PLAN = {"max0": 1, "maxn": 12, "shift": 16, "q": 3, "qT": 8, "kT": 4, "pv": 4, "turn": 4, "back": 5, "out": 3,
        "normedT": 5, "route": 3}
WIDE = ("ctxT", "xT", "kT", "qT", "shift")
RING = ("k", "q", "kLT", "v", "max", "turn", "back", "out", "normedT", "route")


class Wide:

    def __init__(self, place, before):
        self.place, self.before, self.turn = place, before, None


def fillings(steps):
    last, count, open_, of = [0, 0], 0, None, {}
    held = [0, 0]

    def new():
        place = min((n for n in range(2) if open_ is None or n != open_[0].place), key=lambda n: held[n])
        return Wide(place, last[place])

    for s in steps:
        if s[0] in WIDE:
            w = new()
            count += 1
            w.turn = count
            last[w.place] = held[w.place] = count
            of[s] = [w]
        elif s[0] == "score":
            if open_ is None:
                open_ = [new(), 0]
                held[open_[0].place] = 10 ** 6
            of[s] = [(open_[0], open_[1])]
            open_[1] += 1
            if open_[1] == 4:
                count += 1
                open_[0].turn = count
                last[open_[0].place] = held[open_[0].place] = count
                open_ = None
    assert open_ is None
    return of


def program(nc, a, out):
    ctx = ExitStack()
    with ctx:
        def sb(name, shape, dt=F32):
            return ctx.enter_context(nc.sbuf_tensor(name, shape, dt))

        def sem(name):
            return ctx.enter_context(nc.semaphore(name))

        x = sb("x_sb", [P, T, C])
        xb = sb("x_plus_bias", [P, T, C])
        xn = sb("x_normed", [P, T, C])
        xnT = sb("x_normed_T", [P, T * P])
        cx = sb("context", [P, 3, CK])
        cxT = sb("context_T", [CK, NB * P])
        cxL = sb("context_left_T", [CK, NB, J, 32])
        wq = sb("wq", [C, C]); wk = sb("wk", [CK, C]); wv = sb("wv", [CK, C])
        wo = sb("wo", [C, C])
        bias = sb("bias_rows", [P, 4, C])
        gates = sb("gates", [P, 2]); tg = sb("tanh_gates", [P, 2])
        zf = sb("zeros_f", [P, P]); zb = sb("zeros_b", [P, P], BF16)
        idf = sb("ident_f", [P, P]); idb = sb("ident_b", [P, P], BF16)
        lmask = sb("left_mask", [P, J])
        st = sb("bn_stats", [P, T, 6]); mv = sb("mean_var", [P, T, 2])
        ve = sb("var_eps", [P, T]); rstd = sb("rstd", [P, T]); mhalf = sb("minus_half", [P, T])
        warm = sb("warm", [P, 2])
        q = sb("q_f", [P, 2, UT, C]); qr = sb("q_rest", [P, 2, UT, C])
        qs = sb("q_stack", [P, T, PR, 8, 16], BF16)
        qT = sb("q_stack_T", [P, PR, T * P], BF16)
        k = sb("k_f", [P, KW]); kr = sb("k_rest", [P, KW]); kp = sb("k_parts", [P, 3, KW], BF16)
        kl = sb("k_left_f", [P, NB, C])
        ks = sb("k_stack", [P, NB * PR, 2, P], BF16)
        ksL = sb("k_left_stack", [P, NB * G, P], BF16)
        kT = sb("k_stack_T", [P, NB, H, P], BF16)
        kLT = sb("k_left_stack_T", [P, NB, G, P], BF16)
        v = sb("v_main", [P, NB, H, 32]); vL = sb("v_left", [P, NB, G, J, 32])
        vLf = sb("v_left_f", [P, NB, C])
        mm = sb("max_main", [P, T, H]); ml = sb("max_left", [P, T, H]); mx = sb("max", [P, T, H])
        ms = sb("shift_parts", [P, T, P], BF16)
        NPT = 6
        pt = sb("probs_T", [P, NPT, 4, UQ])
        oT = sb("o_T", [P, 2, UQ])
        ot = sb("o_tokens", [P, 2, UT, C]); rc = sb("sum_reciprocal", [P, 2, UT, J])
        onT = sb("o_normed_T", [P, 2, UQ])
        row = sb("row", [P, T, ROW])
        xn2, x2 = row[:, :, 0:C], row[:, :, C:2 * C]
        rows = nc.dram_tensor("rows", (T * P, ROW), F32, kind="Internal").ap()
        st2 = sb("bn_stats2", [P, T, 6]); mv2 = sb("mean_var2", [P, T, 2])
        ve2 = sb("var_eps2", [P, T]); rstd2 = sb("rstd2", [P, T])
        xn2T = sb("x2_normed_T", [P, 2, UQ])
        gw = sb("gate_w", [C, E]); lg = sb("logits", [P, T, E])
        lmax = sb("logit_max", [P, T]); ld = sb("logit_diff", [P, T, E]); le = sb("logit_exp", [P, T, E])
        ls = sb("exp_sum", [P, T]); lr = sb("exp_sum_recip", [P, T])
        eq = sb("is_max", [P, T, E]); em = sb("best", [P, T])
        oh = sb("one_hot", [P, T, E], BF16)
        iota_i = sb("iota_i", [P, P], I32); io = sb("iota", [P, P]); ip = sb("iota_p", [P, 1]); ip_i = sb("iota_p_i", [P, 1], I32)
        rev = sb("rev", [P, E]); first = sb("first", [P, E])
        hi128 = sb("multiples_of_128", [P, NBLK + 1]); one8 = sb("ones8", [P, E])
        io_t = sb("iota_t", [P, T]); tri = sb("before", [P, P], BF16); ones = sb("ones", [P, P], BF16)
        nbk = sb("blocks_gt", [P, E, T]); nb = sb("blocks", [P, E]); end = sb("block_end", [P, E])
        base = sb("slot_base", [P, E]); sl = sb("slot_of_expert", [P, T, E]); slot = sb("slot", [P, T])
        ge = sb("block_ge", [P, T, NBLK + 1]); hs = sb("block_number", [P, T]); lo = sb("slot_in_block", [P, T])
        olo = sb("slot_one_hot", [P, T, P], BF16); rhs = sb("block_one_hot", [P, T, 3, NBLK], BF16)
        inv = sb("slot_tokens", [P, 3, NBLK]); gi = sb("gather_index", [P, NBLK], I32)
        tokf = sb("slot_token", [P, NBLK]); sif = sb("scatter_f", [P, NBLK]); si = sb("scatter_index", [P, NBLK], I32)
        bge = sb("block_past", [P, NBLK, E]); bef = sb("block_expert_f", [P, NBLK]); be = sb("block_expert", [P, NBLK], I32)
        w1 = sb("w1", [C, E, FF]); w2 = sb("w2", [P, E, FC, C]); b1r = sb("b1_rows", [E * FC, P])
        b1 = sb("b1_T", [P, E * FC]); b2 = sb("b2", [P, E, C])
        xg = qT[:].rearrange("p r q -> p (r q)").bitcast(F32)[:, 0:NBLK * ROW].rearrange("p (i c) -> p i c", i=NBLK)
        xgT = sb("gathered_T", [P, 2, P]); 
        old = qs[:].rearrange("p t r c m -> p (t r c m)").bitcast(F32)
        w1c, hb, hT = (old[:, 2 * FF * n:2 * FF * (n + 1)].rearrange("p (s f) -> p s f", s=2) for n in range(3))
        yo = old[:, 6 * FF:7 * FF].rearrange("p (s f) -> p s f", s=4)
        yb = old[:, 7 * FF:7 * FF + 2 * C].rearrange("p (s f) -> p s f", s=2)

        ring = [ctx.enter_context(nc.psum_tensor(f"ring{i}", [P, 512], F32)) for i in range(RB)]
        pa = [ctx.enter_context(nc.psum_tensor(f"wide{i}", [P, 1024], F32)) for i in range(2)]
        pv = ctx.enter_context(nc.psum_tensor("pv", [P, 512], F32))
        turned = [pv, ring[2]]

        wk_in = sem("wk_in"); wv_in = sem("wv_in"); bk_in = sem("bk_in"); bq_in = sem("bq_in"); bv_in = sem("bv_in")
        bo_in = sem("bo_in"); act_warm = sem("act_warm"); wide_full = sem("wide_full"); wide_free = sem("wide_free")
        cleared_cx = sem("cleared_cx"); cleared_half = sem("cleared_half"); cleared_ksL = sem("cleared_ksL")
        cleared_ks = sem("cleared_ks"); cleared_qs = sem("cleared_qs"); 
        cleared_v = sem("cleared_v"); shift_spread = sem("shift_spread"); cleared_ms = sem("cleared_ms"); cleared_row = sem("cleared_row")
        qs_base = sem("qs_base"); qs_equal = sem("qs_equal"); kparts_ready = sem("kparts_ready")
        ksL_ready = sem("ksL_ready"); ones_ready = sem("ones_ready")
        x_in = [sem(f"x_in{i}") for i in range(2)]
        cx_in = sem("cx_in"); wq_in = sem("wq_in"); wkv_in = sem("wkv_in")
        wo_in = sem("wo_in"); bias_in = sem("bias_in"); gates_in = sem("gates_in")
        zeros = sem("zeros"); ident = sem("ident"); cleared = sem("cleared")
        sel_ready = sem("sel_ready"); mask_step = sem("mask_step")
        gates_ready = sem("gates_ready")
        dv = sem("dve_chain"); pl = sem("pool_chain")
        aggr = sem("aggr"); rstd_ready = sem("rstd_ready"); xn_ready = sem("xn_ready")
        xT_ps = sem("xT_ps"); xT_ready = sem("xT_ready"); q_ps = sem("q_ps"); q_read = sem("q_read")
        qbase = sem("q_base"); qs_ready = sem("qs_ready"); qsT_ps = sem("qsT_ps"); qT_ready = sem("qT_ready")
        cT_ps = sem("cT_ps"); cT_ready = sem("cT_ready"); kv_ps = sem("kv_ps"); kv_read = sem("kv_read")
        v_ready = sem("v_ready"); ks_ready = [sem(f"ks_ready{b}") for b in range(NB)]; ksT_ps = sem("ksT_ps"); kT_ready = sem("kT_ready")
        ring_full = sem("ring_full"); ring_free = sem("ring_free")
        score_full = sem("score_full"); probs_ready = sem("probs_ready")
        shift_ready = sem("shift_ready"); mT_ready = sem("mT_ready")
        pv_full = sem("pv_full"); oT_ready = sem("oT_ready"); sum_done = sem("sum_done")
        xb_ready = sem("xb_ready"); on_ready = sem("on_ready"); x2_ready = sem("x2_ready")
        out_done = sem("out_done"); onT_ready = sem("onT_ready"); gw_in = sem("gw_in"); b1_in = sem("b1_in")
        b2_in = sem("b2_in"); w1_in = sem("w1_in"); w2_in = sem("w2_in"); rows_out = sem("rows_out")
        weight_ready = sem("weight_ready"); aggr2 = sem("aggr2"); rstd2_ready = sem("rstd2_ready")
        xn2_ready = sem("xn2_ready"); ld_ready = sem("ld_ready"); le_ready = sem("le_ready")
        oh_ready = sem("oh_ready"); rank_ps = sem("rank_ps"); iotas = sem("iotas"); consts2 = sem("consts2")
        olo_ready = sem("olo_ready"); inv_ps = sem("inv_ps"); index_ready = sem("index_ready")
        expert_ready = sem("expert_ready"); b1_ps = sem("b1_ps"); b1_ready = sem("b1_ready")
        gathered = [sem(f"gathered{i}") for i in range(NBLK)]
        xgT_ps = sem("xgT_ps"); xgT_ready = sem("xgT_ready"); w1c_ready = sem("w1c_ready")
        h_ps = sem("h_ps"); hb_ready = sem("hb_ready"); hidden_ready = sem("hidden_ready")
        scattered = [sem(f"scattered{i}") for i in range(4)]; y_ps = sem("y_ps"); y_read = sem("y_read"); yo_ready = sem("yo_ready")

        steps = plan()
        ringed = [s for s in steps if s[0] in RING]
        fills = fillings(steps)
        exps = {}
        for s in steps:
            if s[0] == "score" and fills[s][0][1] == 3:
                exps[fills[s][0][0]] = len(exps)
        turn_of = {n: w.turn for w, n in exps.items()}
        at_ring = {s: n for n, s in enumerate(ringed)}
        freed = [sum(x[0] != "out" for x in ringed[:n + 1]) for n in range(len(ringed))]
        units = [(u, g) for u in range(U) for g in range(G)]

        def wide_of(u, g):
            return turn_of[(5 * (G * u + g) + 4) // 4]

        block = ctx.enter_context(nc.Block())

        def stack_k(copy, b, c):
            for par in range(2):
                src = kp[:, KPART[c], b * C:(b + 1) * C].rearrange("p (n m) -> p n m", m=2 * D)
                own = slice(D * par, D * par + D)
                o = ks[:, b * PR:(b + 1) * PR, par, 16 * c:16 * c + 16]
                copy(o[:, :, own], src[:, :, own]).then_inc(ks_ready[b], 1)

        @block.sync
        def _(sp):
            xv = a["x"].rearrange("b (t p) c -> p (b t) c", p=P)
            sp.dma_start(x[:, 0:TB, :], xv[:, 0:TB, :]).then_inc(x_in[0], 16)
            sp.dma_start(wk[:], a["L0_xattn_Wk"]).then_inc(wk_in, 16)
            sp.dma_start(wq[:], a["L0_xattn_Wq"]).then_inc(wq_in, 16)
            sp.dma_start(bias[:, 1, :], a["L0_xattn_bk"].partition_broadcast(P)).then_inc(bk_in, 16)
            sp.dma_start(bias[:, 0, :], a["L0_xattn_bq"].partition_broadcast(P)).then_inc(bq_in, 16)
            sp.dma_start(x[:, TB:T, :], xv[:, TB:T, :]).then_inc(x_in[1], 16)
            sp.dma_start(wv[:], a["L0_xattn_Wv"]).then_inc(wv_in, 16)
            sp.dma_start(bias[:, 2, :], a["L0_xattn_bv"].partition_broadcast(P)).then_inc(bv_in, 16)
            sp.dma_start(gates[:, 0:1], a["g_xattn"].partition_broadcast(P)).then_inc(gates_in, 16)
            sp.dma_start(gates[:, 1:2], a["g_ffn"].partition_broadcast(P)).then_inc(gates_in, 16)
            sp.dma_start(bias[:, 3, :], a["L0_xattn_bo"].partition_broadcast(P)).then_inc(bo_in, 16)
            sp.dma_start(wo[:], a["L0_xattn_Wo"]).then_inc(wo_in, 16)
            sp.dma_start(gw[:], a["L0_ffn_gate_w"]).then_inc(gw_in, 16)
            sp.dma_start(b1r[:], a["L0_ffn_b1"].rearrange("e (c p) -> (e c) p", p=P)).then_inc(b1_in, 16)
            sp.dma_start(b2[:], a["L0_ffn_b2"].partition_broadcast(P)).then_inc(b2_in, 16)
            w1v = a["L0_ffn_w1"].rearrange("e d f -> d e f")
            w2v = a["L0_ffn_w2"].rearrange("e (c p) n -> p e c n", p=P)
            for h in range(2):
                es = slice(h * E // 2, (h + 1) * E // 2)
                sp.dma_start(w1[:, es, :], w1v[:, es, :]).then_inc(w1_in, 16)
                for e in range(h * E // 2, (h + 1) * E // 2):
                    sp.dma_start(w2[:, e], w2v[:, e]).then_inc(w2_in, 16)
            rv = rows.rearrange("(t p) c -> p t c", p=P)
            for u in range(U):
                sp.wait_ge(weight_ready, u + 1)
                sp.dma_start(rv[:, UT * u:UT * u + UT, :], row[:, UT * u:UT * u + UT, :]).then_inc(rows_out, 16)

        @block.scalar
        def _(act):
            cv = a["ctx_768"]
            act.dma_start(cx[:, 0:2, :], cv[:, 0:P, :].rearrange("b p c -> p b c")).then_inc(cx_in, 16)
            for b in range(NB):
                act.dma_start(cx[KL * b:KL * b + KL, 2, :], cv[b, P:NK, :]).then_inc(cx_in, 16)
            act.wait_ge(zeros, 1)
            nc.scalar.activation(warm[:, 0:1], zf[:, 0:1], ACT.Exp).then_inc(act_warm, 1)
            pvs = 0
            for s in steps:
                kind, u, n = s
                if kind in WIDE:
                    w = fills[s][0]
                    bank = pa[w.place]
                    act.wait_ge(wide_full, w.turn)
                if kind == "ctxT":
                    nc.scalar.activation(cxT[:], bank[0:CK, 0:NB * P], ACT.Copy).then_inc(cT_ready, 1)
                    act.wait_ge(cleared_cx, 1)
                    src = bank[0:CK, 256:256 + NB * KL].rearrange("c (b k) -> c b k", b=NB)
                    for b in range(NB):
                        last = nc.scalar.activation(cxL[:, b, :, 0:KL], src[:, b].unsqueeze(1).to_broadcast([CK, J, KL]),
                                                    ACT.Copy)
                        if b == 0:
                            last.then_inc(cT_ready, 1)
                    last.then_inc(wide_free, 1)
                elif kind == "xT":
                    nc.scalar.activation(xnT[:, u * 512:(u + 1) * 512], bank[:, 0:512], ACT.Copy).then_inc(wide_free, 1)
                elif kind == "kT":
                    nc.scalar.activation(kT[:, u].rearrange("p h q -> p (h q)"), bank[:].bitcast(BF16),
                                         ACT.Copy).then_inc(wide_free, 1)
                elif kind == "qT":
                    src = bank[0:STK].bitcast(BF16).rearrange("p (t r q) -> p r t q", t=UT, r=PR)
                    o = qT[0:STK, :, UQ * u:UQ * u + UQ].rearrange("p r (t q) -> p r t q", t=UT)
                    for t in range(UT):
                        last = nc.scalar.activation(o[:, :, t, :], src[:, :, t, :], ACT.Copy)
                    last.then_inc(wide_free, 1)
                elif kind == "shift":
                    src = bank[STK:P, 0:UQ // 2].bitcast(BF16).unsqueeze(1).to_broadcast([P - STK, 2, UQ])
                    nc.scalar.activation(qT[STK:P, 0:2, UQ * u:UQ * u + UQ], src, ACT.Copy).then_inc(wide_free, 1)
                elif kind == "k":
                    act.wait_ge(kparts_ready, 1)
                    act.wait_ge(cleared_ks, 1)
                    for c in range(NC):
                        if KPART[c] == 0:
                            stack_k(nc.scalar.copy, 0, c)
                elif kind == "q":
                    for c in (1, 2, 4):
                        act.wait_ge(qs_base, 3 * u + (1 if c < 4 else 2))
                        o = qs[:, UT * u:UT * u + UT].rearrange("p t r c m -> p (t r) c m")
                        nc.scalar.activation(o[:, :, c, :], o[:, :, 0 if c < 4 else 3, :], ACT.Copy).then_inc(qs_equal, 1)
                elif kind == "score":
                    w, quarter = fills[s][0]
                    if quarter == 3:
                        act.wait_ge(wide_full, w.turn)
                        done = exps[w]
                        if done >= NPT:
                            act.wait_ge(pv_full, (4 * (done - NPT) + 3) // 5 + 1)
                        nc.scalar.activation(pt[:, done % NPT].rearrange("p c q -> p (c q)"), pa[w.place][:],
                                             ACT.Exp, scale=SCALE).then_inc(wide_free, 1)
                elif kind == "route":
                    act.wait_ge(ld_ready, u + 1)
                    ts = slice(UT * u, UT * u + UT)
                    nc.scalar.activation(le[:, ts, :], ld[:, ts, :], ACT.Exp).then_inc(le_ready, 1)
                elif kind == "pv":
                    act.wait_ge(pv_full, pvs + 1)
                    if pvs >= 2:
                        act.wait_ge(ring_full, at_ring[("turn", (pvs - 2) // G, (pvs - 2) % G)] + 1)
                    nc.scalar.activation(oT[:, pvs % 2, :], pv[:, 0:UQ], ACT.Copy).then_inc(oT_ready, 1)
                    pvs += 1
                if s == ("q", 1, 0):
                    act.wait_ge(gates_in, 32)
                    nc.scalar.activation(tg[:], gates[:], ACT.Tanh).then_inc(gates_ready, 1)
            act.wait_ge(act_warm, 1)
            nc.scalar.activation(warm[:, 1:2], warm[:, 0:1], ACT.Gelu).then_inc(act_warm, 1)

            def copy_turned(i):
                act.wait_ge(xgT_ps, i + 1)
                if i >= 2:
                    act.wait_ge(h_ps, i - 1)
                nc.scalar.activation(xgT[:, i % 2], turned[i % 2][:, 0:P], ACT.Copy).then_inc(xgT_ready, 1)

            copy_turned(0)
            copy_turned(1)
            for i in range(NBLK):
                if i + 2 < NBLK:
                    copy_turned(i + 2)
                act.wait_ge(hb_ready, i + 1)
                if i >= 2:
                    act.wait_ge(y_ps, i - 1)
                nc.scalar.activation(hT[:, i % 2], hb[:, i % 2], ACT.Gelu).then_inc(hidden_ready, 1)

        @block.gpsimd
        def _(pool):
            nc.gpsimd.memset(zf[:], 0.0).then_inc(zeros, 1)
            nc.gpsimd.memset(zb[:], 0.0).then_inc(zeros, 1)
            pool.wait_ge(zeros, 2)
            for o, z in ((idf, zf), (idb, zb)):
                nc.gpsimd.affine_select(out=o[:], in_=z[:], compare_op=ALU.not_equal, fill=1.0, base=0,
                                        pattern=[[-1, P]], channel_multiplier=1).then_inc(ident, 1)
            nc.gpsimd.memset(cxL[:], 0.0).then_inc(cleared_cx, 1)
            nc.gpsimd.memset(mhalf[:], -0.5).then_inc(cleared_half, 1)
            nc.gpsimd.memset(lmask[:], 1.0).then_inc(mask_step, 1)
            pool.wait_ge(mask_step, 1)
            nc.gpsimd.affine_select(out=lmask[:], in_=lmask[:], compare_op=ALU.is_ge, fill=0.0, base=0,
                                    pattern=[[-32, J]], channel_multiplier=1).then_inc(mask_step, 1)
            pool.wait_ge(mask_step, 2)
            nc.gpsimd.affine_select(out=lmask[:], in_=lmask[:], compare_op=ALU.is_ge, fill=0.0, base=KL - 1,
                                    pattern=[[32, J]], channel_multiplier=-1).then_inc(mask_step, 1)
            nc.gpsimd.memset(ksL[:].rearrange("p n m -> p (n m)").bitcast(F32), 0.0).then_inc(cleared_ksL, 1)
            pool.wait_ge(cleared_ksL, 1)
            pool.wait_ge(mask_step, 3)
            for part in range(2):
                for j in range(J):
                    at = STK + H * part + j
                    o = ksL[:].rearrange("p (b g) m -> p b (g m)", b=NB)[:, :, at:at + (P + J) * (G - 1) + 1:P + J]
                    nc.gpsimd.tensor_copy(o, lmask[:, j:j + 1].unsqueeze(1).to_broadcast([P, NB, G])).then_inc(ones_ready, 1)

            def inverse_std(b):
                ts = slice(b * TB, (b + 1) * TB)
                pool.wait_ge(aggr, TB * (b + 1))
                nc.gpsimd.tensor_scalar(ve[:, ts], mv[:, ts, 1], EPS, None, ALU.add).then_inc(pl, 1)
                pool.wait_ge(pl, b + 1)
                pool.wait_ge(cleared_half, 1)
                nc.gpsimd.tensor_tensor(rstd[:, ts], ve[:, ts], mhalf[:, ts], ALU.pow).then_inc(rstd_ready, 1)

            inverse_std(0)
            nc.gpsimd.memset(qs[:, 0:UT, :, NC:, :], 0.0).then_inc(cleared_qs, 1)
            pool.wait_ge(kparts_ready, 3)
            for c in range(NC):
                nc.gpsimd.tensor_copy(ksL[:, :, 16 * c:16 * c + 16],
                                      kp[:, KPART[c], NB * C:].rearrange("p (n m) -> p n m", m=16)).then_inc(ksL_ready, 1)
            inverse_std(1)
            pool.wait_ge(cleared_ks, 1)
            for c in range(NC):
                stack_k(nc.gpsimd.tensor_copy, 1, c)
            for u in range(1, U):
                nc.gpsimd.memset(qs[:, UT * u:UT * u + UT, :, NC:, :], 0.0).then_inc(cleared_qs, 1)
            nc.gpsimd.memset(v[:].rearrange("p b h m -> p (b h m)"), 0.0).then_inc(cleared_v, 1)
            nc.gpsimd.memset(vL[:].rearrange("p b g j m -> p (b g j m)"), 0.0).then_inc(cleared_v, 1)
            nc.gpsimd.memset(ms[:].rearrange("p t m -> p (t m)").bitcast(F32), 0.0).then_inc(cleared_ms, 1)
            nc.gpsimd.memset(row[:, :, 2 * C:], 0.0).then_inc(cleared_row, 1)
            pool.wait_ge(gates_ready, 1)
            pool.wait_ge(bo_in, 16)
            nc.gpsimd.tensor_scalar(bias[:, 3, :], bias[:, 3, :], tg[:, 0:1], None, ALU.mult).then_inc(xb_ready, 1)
            pool.wait_ge(xb_ready, 1)
            for b in range(NB):
                pool.wait_ge(x_in[b], 16)
                nc.gpsimd.tensor_tensor(xb[:, b * TB:(b + 1) * TB, :], x[:, b * TB:(b + 1) * TB, :],
                                        bias[:, 3:4, :].to_broadcast([P, TB, C]), ALU.add).then_inc(xb_ready, 1)
            nc.gpsimd.iota(iota_i[:], [[1, P]], base=0, channel_multiplier=0).then_inc(iotas, 1)
            nc.gpsimd.iota(ip_i[:], [[0, 1]], base=0, channel_multiplier=1).then_inc(iotas, 1)
            nc.gpsimd.memset(ones[:], 1.0).then_inc(iotas, 1)
            nc.gpsimd.memset(one8[:], 1.0).then_inc(iotas, 1)
            pool.wait_ge(iotas, 4)
            nc.gpsimd.tensor_copy(io[:], iota_i[:]).then_inc(consts2, 1)
            nc.gpsimd.tensor_copy(ip[:], ip_i[:]).then_inc(consts2, 1)
            nc.gpsimd.affine_select(out=tri[:], in_=ones[:], compare_op=ALU.is_gt, fill=0.0, base=0,
                                    pattern=[[1, P]], channel_multiplier=-1).then_inc(consts2, 1)
            pool.wait_ge(consts2, 3)
            nc.gpsimd.tensor_scalar(rev[:], io[:, 0:E], -1.0, float(E), ALU.mult, ALU.add).then_inc(consts2, 1)
            nc.gpsimd.tensor_scalar(first[:], io[:, 0:E], 0.0, 0.5, ALU.is_equal, ALU.mult).then_inc(consts2, 1)
            nc.gpsimd.tensor_scalar(hi128[:], io[:, 0:NBLK + 1], float(P), None, ALU.mult).then_inc(consts2, 1)
            for u in range(U):
                ts = slice(UT * u, UT * u + UT)
                pool.wait_ge(aggr2, UT * (u + 1))
                nc.gpsimd.tensor_scalar(ve2[:, ts], mv2[:, ts, 1], EPS, None, ALU.add).then_inc(pl, 1)
                pool.wait_ge(pl, NB + u + 1)
                nc.gpsimd.tensor_tensor(rstd2[:, ts], ve2[:, ts], mhalf[:, ts], ALU.pow).then_inc(rstd2_ready, 1)
            ov = out.rearrange("b q c -> (b q) c")
            pool.wait_ge(rows_out, 16 * U)
            pool.wait_ge(index_ready, 2)
            for i in range(NBLK + AHEAD):
                if i < NBLK:
                    nc.gpsimd.indirect_dma_start(xg[:, i, :], None, rows[:],
                                                 bass.IndirectOffsetOnAxis(ap=gi[:, i:i + 1], axis=0)
                                                 ).then_inc(gathered[i], 16)
                if i >= AHEAD:
                    m = i - AHEAD
                    pool.wait_ge(yo_ready, m + 1)
                    nc.gpsimd.indirect_dma_start(ov, bass.IndirectOffsetOnAxis(ap=si[:, m:m + 1], axis=0),
                                                 yo[:, m % 4, :], None, bounds_check=T * P - 1,
                                                 oob_is_err=False).then_inc(scattered[m % 4], 16)
            for m in range(4):
                pool.wait_ge(scattered[m], 16 * len(range(m, NBLK, 4)))

        @block.vector
        def _(dve):
            chain = [0]

            def link(ins):
                chain[0] += 1
                ins.then_inc(dv, 1)
                dve.wait_ge(dv, chain[0])

            def statistics(b):
                dve.wait_ge(x_in[b], 16)
                for t in range(b * TB, (b + 1) * TB):
                    last = nc.vector.bn_stats(st[:, t, :], x[:, t, :])
                link(last)
                for t in range(b * TB, (b + 1) * TB):
                    nc.vector.bn_aggr(mv[:, t, :], st[:, t, :]).then_inc(aggr, 1)

            def normalise(b):
                dve.wait_ge(rstd_ready, b + 1)
                for t in range(b * TB, (b + 1) * TB):
                    nc.vector.tensor_scalar(xn[:, t, :], x[:, t, :], mv[:, t, 0:1], rstd[:, t:t + 1],
                                            ALU.subtract, ALU.mult).then_inc(xn_ready, 1)

            nc.vector.memset(ks[:].rearrange("p n a m -> p (n a m)").bitcast(F32), 0.0).then_inc(cleared_ks, 1)
            statistics(0)
            normalise(0)
            for s in steps:
                kind, u, n = s
                if kind == "shift":
                    uq = slice(UQ * u, UQ * u + UQ)
                    dve.wait_ge(wide_free, fills[s][0].turn)
                    nc.vector.tensor_copy(qT[STK:P, 2:, uq], qT[STK:P, 0:1, uq].to_broadcast([P - STK, PR - 2, UQ])
                                          ).then_inc(shift_spread, 1)
                if s not in at_ring:
                    continue
                r = at_ring[s]
                bank = ring[r % RB]
                if kind == "k":
                    dve.wait_ge(bk_in, 16)
                    dve.wait_ge(mask_step, 3)
                    dve.wait_ge(ring_full, r + 1)
                    kb = bias[:, 1:2, :].to_broadcast([P, NB, C])
                    nc.vector.tensor_tensor(k[:, 0:NB * C].rearrange("p (b c) -> p b c", b=NB),
                                            bank[:, 0:NB * C].rearrange("p (b c) -> p b c", b=NB), kb, ALU.add)
                    nc.vector.tensor_tensor(kl[:], bank[:, NB * C:].rearrange("p (b c) -> p b c", b=NB), kb,
                                            ALU.add).then_inc(ring_free, 1)
                    dve.wait_ge(ring_free, freed[r])
                    klj = kl[:].rearrange("p b (g j m) -> p (b g) j m", j=J, m=D)
                    link(nc.vector.tensor_tensor(klj, klj, lmask[:].unsqueeze(1).unsqueeze(3).to_broadcast([P, NB * G, J, D]),
                                                 ALU.mult))
                    link(nc.vector.tensor_tensor(k[:, NB * C:].rearrange("p (n m) -> p n m", m=2 * D),
                                                 klj[:, :, 0:2].rearrange("p n j m -> p n (j m)"),
                                                 klj[:, :, 2:4].rearrange("p n j m -> p n (j m)"), ALU.add))
                    nc.vector.tensor_copy(kp[:, 0], k[:]).then_inc(kparts_ready, 1)
                    dve.wait_ge(kparts_ready, 1)
                    link(nc.vector.tensor_tensor(kr[:], k[:], kp[:, 0], ALU.subtract))
                    nc.vector.tensor_copy(kp[:, 1], kr[:]).then_inc(kparts_ready, 1)
                    dve.wait_ge(kparts_ready, 2)
                    nc.vector.tensor_tensor(kp[:, 2], kr[:], kp[:, 1], ALU.subtract).then_inc(kparts_ready, 1)
                    dve.wait_ge(kparts_ready, 3)
                    dve.wait_ge(cleared_ks, 1)
                    for c in range(NC):
                        if KPART[c]:
                            stack_k(nc.vector.tensor_copy, 0, c)
                    for b in range(NB):
                        for part in range(2):
                            at = STK + H * part
                            o = ks[:, b * PR:(b + 1) * PR].rearrange("p r a m -> p (r a m)")[:, at:at + (P + 1) * (H - 1) + 1:P + 1]
                            nc.vector.memset(o, 1.0).then_inc(ks_ready[b], 1)
                elif kind == "q":
                    if u == 0:
                        dve.wait_ge(bq_in, 16)
                    dve.wait_ge(ring_full, r + 1)
                    qu, qru = q[:, u % 2], qr[:, u % 2]
                    nc.vector.tensor_tensor(qu, bank[:, 0:UT * C].rearrange("p (t c) -> p t c", c=C),
                                            bias[:, 0:1, :].to_broadcast([P, UT, C]), ALU.add).then_inc(ring_free, 1)
                    dve.wait_ge(ring_free, freed[r])
                    qf = qu.rearrange("p t (r m) -> p (t r) m", m=16)
                    qrf = qru.rearrange("p t (r m) -> p (t r) m", m=16)
                    o = qs[:, UT * u:UT * u + UT].rearrange("p t r c m -> p (t r) c m")
                    nc.vector.tensor_copy(o[:, :, 0, :], qf).then_inc(qs_base, 1)
                    dve.wait_ge(qs_base, 3 * u + 1)
                    link(nc.vector.tensor_tensor(qrf, qf, o[:, :, 0, :], ALU.subtract))
                    nc.vector.tensor_copy(o[:, :, 3, :], qrf).then_inc(qs_base, 1)
                    dve.wait_ge(qs_base, 3 * u + 2)
                    nc.vector.tensor_tensor(o[:, :, 5, :], qrf, o[:, :, 3, :], ALU.subtract).then_inc(qs_base, 1)
                    if u == 0:
                        statistics(1)
                        normalise(1)
                elif kind == "kLT":
                    dve.wait_ge(ring_full, r + 1)
                    nc.vector.tensor_copy(kLT[:].rearrange("p b g q -> p (b g q)"), bank[:].bitcast(BF16)).then_inc(ring_free, 1)
                elif kind == "v":
                    dve.wait_ge(ring_full, r + 1)
                    dve.wait_ge(bv_in, 16)
                    dve.wait_ge(cleared_v, 2)
                    for b in range(NB):
                        nc.vector.tensor_tensor(v[:, b, :, 0:D], bank[:, b * C:(b + 1) * C].rearrange("p (h d) -> p h d", d=D),
                                                bias[:, 2, :].rearrange("p (h d) -> p h d", d=D), ALU.add).then_inc(v_ready, 1)
                    nc.vector.memset(v[:, :, :, D:D + 1], 1.0).then_inc(v_ready, 1)
                    nc.vector.tensor_tensor(vLf[:], bank[:, 256:512].rearrange("p (b c) -> p b c", b=NB),
                                            bias[:, 2:3, :].to_broadcast([P, NB, C]), ALU.add).then_inc(ring_free, 1)
                    dve.wait_ge(ring_free, freed[r])
                    for j in range(J):
                        src = vLf[:].rearrange("p b (g m) -> p (b g) m", g=G)[:, :, 8 * j:8 * j + 8]
                        o = vL[:, :, :, j, :].rearrange("p b g m -> p (b g) m")
                        nc.vector.tensor_scalar(o[:, :, 0:D], src, lmask[:, j:j + 1], None, ALU.mult).then_inc(v_ready, 1)
                        nc.vector.tensor_copy(o[:, :, D], lmask[:, j:j + 1].to_broadcast([P, NB * G])).then_inc(v_ready, 1)
                elif kind == "max":
                    t, part = UT * u + n // 5, n % 5
                    dve.wait_ge(ring_full, r + 1)
                    if part < 4:
                        nc.vector.tensor_reduce(mm[:, t, 4 * part:4 * part + 4],
                                                bank[:].rearrange("p (h k) -> p h k", k=P), AX.X,
                                                ALU.max).then_inc(ring_free, 1)
                    else:
                        nc.vector.tensor_reduce(ml[:, t, :], bank[:].rearrange("p (h k) -> p h k", k=32)[:, :, 0:KL],
                                                AX.X, ALU.max).then_inc(ring_free, 1)
                    if n == 5 * UT - 1:
                        ts = slice(UT * u, UT * u + UT)
                        dve.wait_ge(ring_free, freed[r])
                        dve.wait_ge(cleared_ms, 1)
                        link(nc.vector.tensor_tensor(mx[:, ts, :], mm[:, ts, :], ml[:, ts, :], ALU.max))
                        link(nc.vector.tensor_scalar(ms[:, ts, STK:STK + H], mx[:, ts, :], -1.0, None, ALU.mult))
                        nc.vector.scalar_tensor_tensor(ms[:, ts, STK + H:P], mx[:, ts, :], -1.0,
                                                       ms[:, ts, STK:STK + H], ALU.mult, ALU.subtract).then_inc(shift_ready, 1)
                elif kind == "turn":
                    dve.wait_ge(ring_full, r + 1)
                    got = bank[:, 0:UT * P].rearrange("p (a m) -> p a m", m=32)
                    m = G * u + n
                    rcs = rc[:, m % 2].rearrange("p t j -> p (t j)")
                    link(nc.vector.reciprocal(rcs, got[:, :, D]))
                    for t in range(UT):
                        last = nc.vector.tensor_tensor(
                            ot[:, u % 2, t, 32 * n:32 * n + 32].rearrange("p (j d) -> p j d", d=D),
                            got[:, J * t:J * t + J, 0:D], rc[:, m % 2, t, :].unsqueeze(2).to_broadcast([P, J, D]), ALU.mult)
                    last.then_inc(ring_free, 1)
                elif kind == "back":
                    dve.wait_ge(ring_full, r + 1)
                    nc.vector.tensor_copy(onT[:, u % 2], bank[:, 0:UQ]).then_inc(ring_free, 1)
                elif kind == "out":
                    dve.wait_ge(ring_full, r + 1)
                    dve.wait_ge(xb_ready, 3)
                    ts = slice(UT * u, UT * u + UT)
                    nc.vector.scalar_tensor_tensor(x2[:, ts, :], bank[:, 0:UT * C].rearrange("p (t c) -> p t c", c=C),
                                                   tg[:, 0:1], xb[:, ts, :], ALU.mult, ALU.add).then_inc(x2_ready, 1)
                    dve.wait_ge(x2_ready, u + 1)
                    for t in range(UT * u, UT * u + UT):
                        last = nc.vector.bn_stats(st2[:, t, :], x2[:, t, :])
                    link(last)
                    for t in range(UT * u, UT * u + UT):
                        nc.vector.bn_aggr(mv2[:, t, :], st2[:, t, :]).then_inc(aggr2, 1)
                    dve.wait_ge(rstd2_ready, u + 1)
                    for t in range(UT * u, UT * u + UT):
                        nc.vector.tensor_scalar(xn2[:, t, :], x2[:, t, :], mv2[:, t, 0:1], rstd2[:, t:t + 1],
                                                ALU.subtract, ALU.mult).then_inc(xn2_ready, 1)
                elif kind == "normedT":
                    dve.wait_ge(ring_full, r + 1)
                    nc.vector.tensor_copy(xn2T[:, u % 2], bank[:, 0:UQ]).then_inc(ring_free, 1)
                elif kind == "route":
                    ts = slice(UT * u, UT * u + UT)
                    dve.wait_ge(consts2, 6)
                    dve.wait_ge(ring_full, r + 1)
                    nc.vector.tensor_copy(lg[:, ts, :], bank[:, 0:UT * E].rearrange("p (t e) -> p t e", e=E)).then_inc(ring_free, 1)
                    dve.wait_ge(ring_free, freed[r])
                    link(nc.vector.tensor_reduce(lmax[:, ts], lg[:, ts, :], AX.X, ALU.max))
                    nc.vector.tensor_tensor(ld[:, ts, :], lg[:, ts, :], lmax[:, ts].unsqueeze(2).to_broadcast([P, UT, E]),
                                            ALU.subtract).then_inc(ld_ready, 1)
                    dve.wait_ge(ld_ready, u + 1)
                    link(nc.vector.scalar_tensor_tensor(eq[:, ts, :], ld[:, ts, :], 0.0,
                                                        rev[:].unsqueeze(1).to_broadcast([P, UT, E]), ALU.is_equal, ALU.mult))
                    link(nc.vector.tensor_tensor(eq[:, ts, :], eq[:, ts, :], first[:].unsqueeze(1).to_broadcast([P, UT, E]),
                                                 ALU.add))
                    link(nc.vector.tensor_reduce(em[:, ts], eq[:, ts, :], AX.X, ALU.max))
                    nc.vector.tensor_tensor(oh[:, ts, :], eq[:, ts, :], em[:, ts].unsqueeze(2).to_broadcast([P, UT, E]),
                                            ALU.is_equal).then_inc(oh_ready, 1)
                    dve.wait_ge(le_ready, u + 1)
                    link(nc.vector.tensor_reduce(ls[:, ts], le[:, ts, :], AX.X, ALU.add))
                    link(nc.vector.reciprocal(lr[:, ts], ls[:, ts]))
                    dve.wait_ge(cleared_row, 1)
                    nc.vector.tensor_scalar(row[:, ts, 2 * C], lr[:, ts], tg[:, 1:2], None, ALU.mult).then_inc(weight_ready, 1)
            dve.wait_ge(rank_ps, 1)
            cnt = pv[:, T * E:T * E + E]
            dve.wait_ge(oh_ready, U)
            link(nc.vector.tensor_tensor(nbk[:], cnt.unsqueeze(2).to_broadcast([P, E, T]),
                                         hi128[:, 0:T].unsqueeze(1).to_broadcast([P, E, T]), ALU.is_gt))
            link(nc.vector.tensor_reduce(nb[:], nbk[:], AX.X, ALU.add))
            link(nc.vector.tensor_tensor_scan(end[:], one8[:], nb[:], 0.0, ALU.mult, ALU.add))
            link(nc.vector.tensor_tensor(base[:], end[:], nb[:], ALU.subtract))
            link(nc.vector.scalar_tensor_tensor(sl[:], base[:].unsqueeze(1).to_broadcast([P, T, E]), float(P),
                                                pv[:, 0:T * E].rearrange("p (t e) -> p t e", e=E), ALU.mult, ALU.add))
            link(nc.vector.tensor_tensor(sl[:], sl[:], oh[:], ALU.mult))
            link(nc.vector.tensor_reduce(slot[:], sl[:], AX.X, ALU.add))
            link(nc.vector.tensor_tensor(ge[:], slot[:].unsqueeze(2).to_broadcast([P, T, NBLK + 1]),
                                         hi128[:].unsqueeze(1).to_broadcast([P, T, NBLK + 1]), ALU.is_ge))
            link(nc.vector.tensor_reduce(hs[:], ge[:], AX.X, ALU.add))
            link(nc.vector.scalar_tensor_tensor(lo[:], hs[:], -float(P), slot[:], ALU.mult, ALU.add))
            link(nc.vector.tensor_scalar(lo[:], lo[:], float(P), None, ALU.add))
            for t in range(T):
                nc.vector.tensor_scalar(olo[:, t, :], io[:], lo[:, t:t + 1], None, ALU.is_equal).then_inc(olo_ready, 1)
            link(nc.vector.tensor_tensor(rhs[:, :, 0, :], ge[:, :, 0:NBLK], ge[:, :, 1:NBLK + 1], ALU.subtract))
            nc.vector.tensor_scalar(rhs[:, :, 1, :], rhs[:, :, 0, :], ip[:], None, ALU.mult).then_inc(olo_ready, 1)
            nc.vector.tensor_tensor(rhs[:, :, 2, :], rhs[:, :, 0, :], io[:, 0:T].unsqueeze(2).to_broadcast([P, T, NBLK]),
                                    ALU.mult).then_inc(olo_ready, 1)
            link(nc.vector.tensor_tensor(bge[:], io[:, 0:NBLK].unsqueeze(2).to_broadcast([P, NBLK, E]),
                                         end[:].unsqueeze(1).to_broadcast([P, NBLK, E]), ALU.is_ge))
            link(nc.vector.tensor_reduce(bef[:], bge[:], AX.X, ALU.add))
            nc.vector.tensor_scalar(be[:], bef[:], float(E - 1), None, ALU.min).then_inc(expert_ready, 1)
            dve.wait_ge(inv_ps, 1)
            link(nc.vector.tensor_copy(inv[:], ring[1][:, 0:3 * NBLK].rearrange("p (a i) -> p a i", a=3)))
            link(nc.vector.scalar_tensor_tensor(tokf[:], inv[:, 2], float(P), inv[:, 1], ALU.mult, ALU.add))
            nc.vector.tensor_copy(gi[:], tokf[:]).then_inc(index_ready, 1)
            link(nc.vector.scalar_tensor_tensor(sif[:], inv[:, 0], -float(2 * T * P), tokf[:], ALU.mult, ALU.add))
            nc.vector.tensor_scalar(si[:], sif[:], float(2 * T * P), None, ALU.add).then_inc(index_ready, 1)
            dve.wait_ge(b1_ps, 1)
            nc.vector.tensor_copy(b1[:], ring[0][:, 0:E * FC]).then_inc(b1_ready, 1)
            dve.wait_ge(b1_ready, 1)
            dve.wait_ge(w1_in, 32)
            dve.wait_ge(b2_in, 16)
            dve.wait_ge(expert_ready, 1)
            ex = {}

            def weights(i):
                ex[i] = nc.vector.value_load(be[0:1, i:i + 1], min_val=0, max_val=E - 1)
                if i >= 2:
                    dve.wait_ge(h_ps, i - 1)
                src = w1[:].rearrange("d e f -> d (e f)")[:, bass.ds(ex[i] * FF, FF)]
                nc.vector.tensor_copy(w1c[:, i % 2, :], src).then_inc(w1c_ready, 1)

            def finish(i):
                dve.wait_ge(y_ps, i + 1)
                bsl = b2[:].rearrange("p e c -> p (e c)")[:, bass.ds(ex[i] * C, C)]
                nc.vector.tensor_tensor(yb[:, i % 2, :], ring[i % 2][:, 0:C], bsl, ALU.add).then_inc(y_read, 1)
                dve.wait_ge(y_read, i + 1)
                if i >= 4:
                    dve.wait_ge(scattered[i % 4], 16 * (i // 4))
                g = xg[:, i, :]
                nc.vector.scalar_tensor_tensor(yo[:, i % 4, :], yb[:, i % 2, :], g[:, 2 * C:2 * C + 1], g[:, C:2 * C],
                                               ALU.mult, ALU.add).then_inc(yo_ready, 1)

            weights(0)
            weights(1)
            for i in range(NBLK):
                dve.wait_ge(h_ps, i + 1)
                if i >= 2:
                    dve.wait_ge(hidden_ready, i - 1)
                bb = b1[:, bass.ds(ex[i] * FC, FC)].unsqueeze(2).to_broadcast([P, FC, P])
                nc.vector.tensor_tensor(hb[:, i % 2].rearrange("p (c q) -> p c q", c=FC),
                                        pa[i % 2][:, 0:FF].rearrange("p (c q) -> p c q", c=FC), bb, ALU.add).then_inc(hb_ready, 1)
                if i + 2 < NBLK:
                    weights(i + 2)
                if i:
                    finish(i - 1)
            finish(NBLK - 1)

        @block.tensor
        def _(pe):
            pe.wait_ge(ident, 2)
            pvs = 0
            for s in steps:
                kind, u, n = s
                b = u * UT // TB
                uq = slice(UQ * u, UQ * u + UQ)
                if s in at_ring:
                    r = at_ring[s]
                    bank = ring[r % RB]
                    if r >= RB:
                        before = ringed[r - RB]
                        if before[0] == "out":
                            pe.wait_ge(x2_ready, before[1] + 1)
                        else:
                            pe.wait_ge(ring_free, freed[r - RB])
                if kind in WIDE:
                    w = fills[s][0]
                    wide = pa[w.place]
                    if w.before:
                        pe.wait_ge(wide_free, w.before)
                if kind == "ctxT":
                    pe.wait_ge(cx_in, 48)
                    for b in range(NB):
                        nc.tensor.transpose(wide[0:CK, b * P:(b + 1) * P], cx[:, b, :], idf[:])
                    nc.tensor.transpose(wide[0:CK, 256:256 + NB * KL], cx[0:NB * KL, 2, :],
                                        idf[0:NB * KL, 0:NB * KL]).then_inc(wide_full, 1)
                elif kind == "xT":
                    pe.wait_ge(xn_ready, TB * (u + 1))
                    for t in range(TB):
                        last = nc.tensor.transpose(wide[:, t * P:(t + 1) * P], xn[:, u * TB + t, :], idf[:])
                    last.then_inc(wide_full, 1)
                elif kind in ("k", "v"):
                    pe.wait_ge(wk_in if kind == "k" else wv_in, 16)
                    pe.wait_ge(wide_free, fills[("ctxT", 0, 0)][0].turn)
                    pe.wait_ge(cT_ready, 2)
                    w = wk if kind == "k" else wv
                    for b in range(NB):
                        nc.tensor.matmul(bank[:, b * P:(b + 1) * P], cxT[:, b * P:(b + 1) * P], w[:], start=True, stop=True)
                    for b in range(NB):
                        last = nc.tensor.matmul(bank[:, 256 + b * P:256 + (b + 1) * P],
                                                cxL[:, b].rearrange("c j k -> c (j k)"), w[:], start=True, stop=True)
                    last.then_inc(ring_full, 1)
                elif kind == "q":
                    pe.wait_ge(wq_in, 16)
                    pe.wait_ge(wide_free, fills[("xT", b, 0)][0].turn)
                    for t in range(UT):
                        last = nc.tensor.matmul(bank[:, t * P:(t + 1) * P],
                                                xnT[:, (UT * u + t) * P:(UT * u + t + 1) * P], wq[:], start=True, stop=True)
                    last.then_inc(ring_full, 1)
                elif kind == "kT":
                    pe.wait_ge(ks_ready[u], 2 * NC + 2)
                    for h in range(H):
                        last = nc.tensor.transpose(wide[:, 64 * h:64 * h + 64].bitcast(BF16), ks[:, u * PR + h // 2, h % 2, :],
                                                   idb[:])
                    last.then_inc(wide_full, 1)
                elif kind == "kLT":
                    pe.wait_ge(ksL_ready, NC)
                    pe.wait_ge(ones_ready, 2 * J)
                    for m in range(NB * G):
                        last = nc.tensor.transpose(bank[:, 64 * m:64 * m + 64].bitcast(BF16), ksL[:, m, :], idb[:])
                    last.then_inc(ring_full, 1)
                elif kind == "qT":
                    pe.wait_ge(qs_base, 3 * (u + 1))
                    pe.wait_ge(qs_equal, 3 * (u + 1))
                    pe.wait_ge(cleared_qs, u + 1)
                    for t in range(UT):
                        for r2 in range(PR):
                            at = 64 * (PR * t + r2)
                            last = nc.tensor.transpose(wide[:, at:at + 64].bitcast(BF16),
                                                       qs[:, UT * u + t, r2].rearrange("p c m -> p (c m)"), idb[:])
                    last.then_inc(wide_full, 1)
                elif kind == "max":
                    t, part = UT * u + n // 5, n % 5
                    if n == 0:
                        pe.wait_ge(wide_free, max(fills[("qT", u, 0)][0].turn, fills[("kT", b, 0)][0].turn if b or u else 0))
                        pe.wait_ge(ring_free, freed[at_ring[("kLT", 0, 0)]])
                    for r2 in ((2 * part, 2 * part + 1) if part < 4 else range(PR)):
                        w = qT[0:STK, r2, t * P:(t + 1) * P]
                        if part < 4:
                            o = bank[:, 256 * (r2 % 2):256 * (r2 % 2) + 256]
                            m = kT[0:STK, b, 2 * r2:2 * r2 + 2, :].rearrange("p h k -> p (h k)")
                        else:
                            o = bank[:, 64 * r2:64 * r2 + 64]
                            m = kLT[0:STK, b, r2 // 2, 64 * (r2 % 2):64 * (r2 % 2) + 64]
                        last = nc.tensor.matmul(o, w, m, start=True, stop=True)
                    last.then_inc(ring_full, 1)
                elif kind == "shift":
                    pe.wait_ge(shift_ready, u + 1)
                    for t in range(UT):
                        last = nc.tensor.transpose(wide[:, 64 * t:64 * t + 64].bitcast(BF16), ms[:, UT * u + t, :], idb[:])
                    last.then_inc(wide_full, 1)
                elif kind == "score":
                    if n == 0:
                        pe.wait_ge(wide_free, fills[("shift", u, 0)][0].turn)
                    if n == 5:
                        pe.wait_ge(shift_spread, u + 1)
                    w, quarter = fills[s][0]
                    g, c = n // 5, n % 5
                    if quarter == 0 and w.before:
                        pe.wait_ge(wide_free, w.before)
                    o = pa[w.place][:, UQ * quarter:UQ * quarter + UQ]
                    if c < J:
                        h = J * g + c
                        last = nc.tensor.matmul(o, kT[:, b, h, :], qT[:, h // 2, uq], start=True, stop=True)
                    else:
                        for half in range(2):
                            last = nc.tensor.matmul(o[64 * half:64 * half + 64, :],
                                                    kLT[:, b, g, 64 * half:64 * half + 64],
                                                    qT[:, 2 * g + half, uq], start=True, stop=True)
                    if quarter == 3:
                        last.then_inc(wide_full, 1)
                elif kind == "pv":
                    pe.wait_ge(wide_free, wide_of(u, n))
                    pe.wait_ge(v_ready, 3 + 2 * J)
                    if pvs:
                        pe.wait_ge(oT_ready, pvs)
                    c0 = 5 * (G * u + n)
                    pieces = [pt[:, ((c0 + c) // 4) % NPT, (c0 + c) % 4, :] for c in range(5)]
                    o = pv
                    nc.tensor.matmul(o[:, 0:UQ], vL[:, b, n].rearrange("p j m -> p (j m)"), pieces[4],
                                     start=True, stop=False, skip_group_check=True)
                    for j in range(J):
                        last = nc.tensor.matmul(o[32 * j:32 * j + 32, 0:UQ], v[:, b, J * n + j, :], pieces[j],
                                                start=False, stop=True, skip_group_check=True)
                    last.then_inc(pv_full, 1)
                    pvs += 1
                elif kind == "turn":
                    pe.wait_ge(oT_ready, G * u + n + 1)
                    for t in range(UT):
                        last = nc.tensor.transpose(bank[:, t * P:(t + 1) * P], oT[:, (G * u + n) % 2, t * P:(t + 1) * P], idf[:])
                    last.then_inc(ring_full, 1)
                elif kind == "back":
                    pe.wait_ge(ring_free, freed[at_ring[("turn", u, G - 1)]])
                    for t in range(UT):
                        last = nc.tensor.transpose(bank[:, t * P:(t + 1) * P], ot[:, u % 2, t, :], idf[:])
                    last.then_inc(ring_full, 1)
                elif kind == "out":
                    pe.wait_ge(ring_free, freed[at_ring[("back", u, 0)]])
                    pe.wait_ge(wo_in, 16)
                    for t in range(UT):
                        last = nc.tensor.matmul(bank[:, t * C:(t + 1) * C], onT[:, u % 2, t * P:(t + 1) * P], wo[:],
                                                start=True, stop=True)
                    last.then_inc(ring_full, 1)
                elif kind == "normedT":
                    pe.wait_ge(xn2_ready, UT * (u + 1))
                    for t in range(UT):
                        last = nc.tensor.transpose(bank[:, t * P:(t + 1) * P], xn2[:, UT * u + t, :], idf[:])
                    last.then_inc(ring_full, 1)
                elif kind == "route":
                    pe.wait_ge(ring_free, freed[at_ring[("normedT", u, 0)]])
                    pe.wait_ge(gw_in, 16)
                    for t in range(UT):
                        last = nc.tensor.matmul(bank[:, t * E:(t + 1) * E], xn2T[:, u % 2, t * P:(t + 1) * P], gw[:],
                                                start=True, stop=True)
                    last.then_inc(ring_full, 1)
            pe.wait_ge(oT_ready, U * G)
            pe.wait_ge(consts2, 6)
            pe.wait_ge(oh_ready, U)
            flat = oh[:].rearrange("p t e -> p (t e)")
            nc.tensor.matmul(pv[:, 0:T * E], tri[:], flat, start=True, stop=False, skip_group_check=True)
            for d in range(1, T):
                nc.tensor.matmul(pv[:, d * E:T * E], ones[:], flat[:, 0:(T - d) * E], start=False, stop=True,
                                 skip_group_check=True)
            for t in range(T):
                last = nc.tensor.matmul(pv[:, T * E:T * E + E], ones[:], flat[:, t * E:(t + 1) * E], start=False, stop=True,
                                        skip_group_check=True)
            last.then_inc(rank_ps, 1)
            pe.wait_ge(b1_in, 16)
            pe.wait_ge(ring_free, freed[-1])
            nc.tensor.transpose(ring[0][:, 0:E * FC], b1r[:], idf[0:E * FC, 0:E * FC]).then_inc(b1_ps, 1)
            pe.wait_ge(olo_ready, T + 2)
            for t in range(T):
                last = nc.tensor.matmul(ring[1][:, 0:3 * NBLK], olo[:, t, :], rhs[:, t].rearrange("p a i -> p (a i)"),
                                        start=(t == 0), stop=(t == T - 1))
            last.then_inc(inv_ps, 1)
            pe.wait_ge(index_ready, 1)
            pe.wait_ge(b1_ready, 1)
            pe.wait_ge(w2_in, 16 * E)
            pe.wait_ge(expert_ready, 1)

            def turn_rows(i):
                pe.wait_ge(gathered[i], 16)
                if i >= 2:
                    pe.wait_ge(xgT_ready, i - 1)
                nc.tensor.transpose(turned[i % 2][:, 0:P], xg[:, i, 0:C], idf[:]).then_inc(xgT_ps, 1)

            def first_half(i):
                pe.wait_ge(xgT_ready, i + 1)
                pe.wait_ge(w1c_ready, i + 1)
                if i >= 2:
                    pe.wait_ge(hb_ready, i - 1)
                for c in range(FC):
                    last = nc.tensor.matmul(pa[i % 2][:, c * P:(c + 1) * P], w1c[:, i % 2, c * P:(c + 1) * P], xgT[:, i % 2],
                                            start=True, stop=True)
                last.then_inc(h_ps, 1)

            w2f = w2[:].rearrange("p e c n -> p (e c n)")
            turn_rows(0)
            turn_rows(1)
            first_half(0)
            for i in range(NBLK):
                if i + 2 < NBLK:
                    turn_rows(i + 2)
                e = nc.tensor.value_load(be[0:1, i:i + 1], min_val=0, max_val=E - 1)
                if i + 1 < NBLK:
                    first_half(i + 1)
                pe.wait_ge(hidden_ready, i + 1)
                if i >= 2:
                    pe.wait_ge(y_read, i - 1)
                for c in range(FC):
                    last = nc.tensor.matmul(ring[i % 2][:, 0:C], hT[:, i % 2, c * P:(c + 1) * P],
                                            w2f[:, bass.ds(e * (FC * C) + c * C, C)], start=(c == 0), stop=(c == FC - 1))
                last.then_inc(y_ps, 1)


NAMES = ["x", "ctx_768", "g_xattn", "g_ffn", "L0_xattn_Wq", "L0_xattn_bq", "L0_xattn_Wk", "L0_xattn_bk",
         "L0_xattn_Wv", "L0_xattn_bv", "L0_xattn_Wo", "L0_xattn_bo", "L0_ffn_gate_w", "L0_ffn_w1",
         "L0_ffn_b1", "L0_ffn_w2", "L0_ffn_b2"]


def kernel(**inputs):
    import numpy as np
    import concourse.bacc as bacc
    from concourse.bass_utils import run_bass_kernel_spmd

    nc = bacc.Bacc("TRN2", target_bir_lowering=False, num_devices=1)
    arrays, a = {}, {}
    for name in NAMES:
        arr = np.ascontiguousarray(inputs[name])
        arrays[f"in_{name}"] = arr
        a[name] = nc.dram_tensor(f"in_{name}", arr.shape, mybir.dt.from_np(arr.dtype), kind="ExternalInput").ap()
    out = nc.dram_tensor("out_x", (NB, NQ, C), F32, kind="ExternalOutput").ap()
    program(nc, a, out)
    r = run_bass_kernel_spmd(nc, [arrays], core_ids=[0])
    return r.results[0]["out_x"]
```

```python
from contextlib import ExitStack

import concourse.bass as bass
from concourse import mybir

F32 = mybir.dt.float32
BF16 = mybir.dt.bfloat16
I32 = mybir.dt.int32
ALU = mybir.AluOpType
ACT = mybir.ActivationFunctionType
AX = mybir.AxisListType

P = 128
NB, NQ, C = 2, 512, 128
NK, CK = 154, 96
H, D = 16, 8
T = NB * NQ // P
TB = NQ // P
KL = NK - P
G, J = 4, 4
PR = H // 2
RB = 3
NBLK = T + 7
ROW = 2 * C + 4
STK = 96
NC = 6
QPART = (0, 0, 0, 1, 1, 2)
KPART = (0, 1, 2, 0, 1, 0)
KW = NB * C + NB * C // 2
U, UT = 4, 2
UQ = UT * P
WARM = (13, 14)
AHEAD = 8
CH = 5 * G
E, FF = 8, 512
FC = FF // P
SCALE = float(D) ** -0.5
CLAMP = 1e4
LIMIT = 0.95 * CLAMP / SCALE
GD, GA, GP = 14, 4, 4
EPS = 1e-5


def plan():
    steps = [("ctxT", 0, 0), ("xT", 0, 0), ("k", 0, 0), ("q", 0, 0), ("kT", 0, 0), ("qT", 0, 0), ("kLT", 0, 0)]
    first = [("max", 0, k) for k in range(5 * UT)]
    steps += first[:4] + [("xT", 1, 0)] + first[4:] + [("q", 1, 0), ("shift", 0, 0), ("v", 0, 0), ("qT", 1, 0)]
    at = {}

    def put(when, *step):
        at.setdefault(when, []).append(step)

    for u in range(U):
        t0 = CH * u
        if u + 1 < U:
            for k in range(5 * UT):
                put(t0 + PLAN["max0"] + k * PLAN["maxn"] // 8, "max", u + 1, k)
            put(t0 + PLAN["shift"], "shift", u + 1, 0)
        if u + 2 < U:
            put(t0 + PLAN["q"], "q", u + 2, 0)
            put(t0 + PLAN["qT"], "qT", u + 2, 0)
        if u == 0:
            put(t0 + PLAN["kT"], "kT", 1, 0)
        for g in range(G):
            full = 4 * ((5 * g + 4) // 4) + 3
            when = t0 + full + PLAN["pv"]
            put(when, "pv", u, g)
            put(when + PLAN["turn"], "turn", u, g)
        when += PLAN["turn"]
        for kind in ("back", "out", "normedT", "route"):
            when += PLAN[kind]
            put(when, kind, u, 0)
            if kind == "out" and u == U - 1:
                put(when, "check", u, 0)
    for n in range(max(at) + 1):
        if n < U * CH:
            steps.append(("score", n // CH, n % CH))
        steps += at.get(n, [])
    return steps


PLAN = {"max0": 1, "maxn": 12, "shift": 16, "q": 3, "qT": 8, "kT": 4, "pv": 4, "turn": 4, "back": 5, "out": 3,
        "normedT": 5, "route": 3}
WIDE = ("ctxT", "xT", "kT", "qT", "shift")
RING = ("k", "q", "kLT", "v", "max", "turn", "back", "check", "out", "normedT", "route")


class Wide:

    def __init__(self, place, before):
        self.place, self.before, self.turn = place, before, None


def fillings(steps):
    last, count, open_, of = [0, 0], 0, None, {}
    held = [0, 0]

    def new():
        place = min((n for n in range(2) if open_ is None or n != open_[0].place), key=lambda n: held[n])
        return Wide(place, last[place])

    for s in steps:
        if s[0] in WIDE:
            w = new()
            count += 1
            w.turn = count
            last[w.place] = held[w.place] = count
            of[s] = [w]
        elif s[0] == "score":
            if open_ is None:
                open_ = [new(), 0]
                held[open_[0].place] = 10 ** 6
            of[s] = [(open_[0], open_[1])]
            open_[1] += 1
            if open_[1] == 4:
                count += 1
                open_[0].turn = count
                last[open_[0].place] = held[open_[0].place] = count
                open_ = None
    assert open_ is None
    return of


def program(nc, a, out):
    ctx = ExitStack()
    with ctx:
        def sb(name, shape, dt=F32):
            return ctx.enter_context(nc.sbuf_tensor(name, shape, dt))

        def sem(name):
            return ctx.enter_context(nc.semaphore(name))

        x = sb("x_sb", [P, T, C])
        xb = sb("x_plus_bias", [P, T, C])
        xn = sb("x_normed", [P, T, C])
        xnT = sb("x_normed_T", [P, T * P])
        cx = sb("context", [P, 3, CK])
        cxT = sb("context_T", [CK, NB * P])
        cxL = sb("context_left_T", [CK, NB, J, 32])
        wq = sb("wq", [C, C]); wk = sb("wk", [CK, C]); wv = sb("wv", [CK, C])
        wo = sb("wo", [C, C])
        bias = sb("bias_rows", [P, 4, C])
        gates = sb("gates", [P, 2]); tg = sb("tanh_gates", [P, 2])
        zf = sb("zeros_f", [P, P]); zb = sb("zeros_b", [P, P], BF16)
        idf = sb("ident_f", [P, P]); idb = sb("ident_b", [P, P], BF16)
        lmask = sb("left_mask", [P, J])
        st = sb("bn_stats", [P, T, 6]); mv = sb("mean_var", [P, T, 2])
        ve = sb("var_eps", [P, T]); rstd = sb("rstd", [P, T]); mhalf = sb("minus_half", [P, T])
        warm = sb("warm", [P, 2])
        q = sb("q_f", [P, 2, UT, C]); qr = sb("q_rest", [P, 2, UT, C])
        qs = sb("q_stack", [P, T, PR, 8, 16], BF16)
        qT = sb("q_stack_T", [P, PR, T * P], BF16)
        k = sb("k_f", [P, KW]); kr = sb("k_rest", [P, KW]); kp = sb("k_parts", [P, 3, KW], BF16)
        kl = sb("k_left_f", [P, NB, C])
        ks = sb("k_stack", [P, NB * PR, 2, P], BF16)
        ksL = sb("k_left_stack", [P, NB * G, P], BF16)
        kT = sb("k_stack_T", [P, NB, H, P], BF16)
        kLT = sb("k_left_stack_T", [P, NB, G, P], BF16)
        v = sb("v_main", [P, NB, H, 32]); vL = sb("v_left", [P, NB, G, J, 32])
        vLf = sb("v_left_f", [P, NB, C])
        mm = sb("max_main", [P, T, H]); ml = sb("max_left", [P, T, H]); mx = sb("max", [P, T, H])
        ms = sb("shift_parts", [P, T, P], BF16)
        NPT = 6
        pt = sb("probs_T", [P, NPT, 4, UQ])
        oT = sb("o_T", [P, 2, UQ])
        ot = sb("o_tokens", [P, 2, UT, C])
        rcs = sb("sum_reciprocals", [P, U * G * UT * J])
        fine = sb("fine", [P, T * H]); fine2 = sb("fine2", [P, T * H]); finec = sb("fine_count", [P, 1], BF16)
        odd = sb("odd", [P, 1], I32)
        onT = sb("o_normed_T", [P, 2, UQ])
        row = sb("row", [P, T, ROW])
        xn2, x2 = row[:, :, 0:C], row[:, :, C:2 * C]
        rows = nc.dram_tensor("rows", (T * P, ROW), F32, kind="Internal").ap()
        st2 = sb("bn_stats2", [P, T, 6]); mv2 = sb("mean_var2", [P, T, 2])
        ve2 = sb("var_eps2", [P, T]); rstd2 = sb("rstd2", [P, T])
        xn2T = sb("x2_normed_T", [P, 2, UQ])
        gw = sb("gate_w", [C, E]);
        lmax = sb("logit_max", [P, T]); ld = sb("logit_diff", [P, T, E]); le = sb("logit_exp", [P, T, E])
        ls = sb("exp_sum", [P, T]); lr = sb("exp_sum_recip", [P, T])
        eq = sb("is_max", [P, T, E]); em = sb("best", [P, T])
        oh = sb("one_hot", [P, T, E], BF16)
        iota_i = sb("iota_i", [P, P], I32); io = sb("iota", [P, P]); iob = sb("iota_b", [P, P], BF16); ip = sb("iota_p", [P, 1]); ip_i = sb("iota_p_i", [P, 1], I32)
        rev = sb("rev", [P, E]); first = sb("first", [P, E])
        hi128 = sb("multiples_of_128", [P, NBLK + 1]); one8 = sb("ones8", [P, E])
        io_t = sb("iota_t", [P, T]); tri = sb("before", [P, P], BF16); ones = sb("ones", [P, P], BF16)
        nbk = sb("blocks_gt", [P, E, T]); nb = sb("blocks", [P, E]); end = sb("block_end", [P, E])
        base = sb("slot_base", [P, E]); sl = sb("slot_of_expert", [P, T, E]); slot = sb("slot", [P, T])
        ge = sb("block_ge", [P, T, NBLK + 1]); hs = sb("block_number", [P, T]); lo = sb("slot_in_block", [P, T])
        olo = sb("slot_one_hot", [P, T, P], BF16); rhs = sb("block_one_hot", [P, T, 3, NBLK], BF16)
        gi = sb("gather_index", [P, NBLK], I32)
        tokf = sb("slot_token", [P, NBLK]); sif = sb("scatter_f", [P, NBLK]); si = sb("scatter_index", [P, NBLK], I32)
        bge = sb("block_past", [P, NBLK, E]); bef = sb("block_expert_f", [P, NBLK]); be = sb("block_expert", [P, NBLK], I32)
        w1 = sb("w1", [C, E, FF]); w2 = sb("w2", [P, E, FC, C]); b1r = sb("b1_rows", [E * FC, P])
        b1 = sb("b1_T", [P, E * FC]); b2 = sb("b2", [P, E, C])
        xg = qT[:].rearrange("p r q -> p (r q)").bitcast(F32)[:, 0:NBLK * ROW].rearrange("p (i c) -> p i c", i=NBLK)
        xgT = sb("gathered_T", [P, 2, P]); 
        old = qs[:].rearrange("p t r c m -> p (t r c m)").bitcast(F32)
        w1c, hb, hT = (old[:, 2 * FF * n:2 * FF * (n + 1)].rearrange("p (s f) -> p s f", s=2) for n in range(3))
        yo = old[:, 6 * FF:7 * FF].rearrange("p (s f) -> p s f", s=4)
        yb = old[:, 7 * FF:7 * FF + 2 * C].rearrange("p (s f) -> p s f", s=2)

        gs, gok, gpT = pt[:, 0, :, 0:NK], pt[:, 1, :, 0:NK], pt[:, 2].rearrange("p c q -> p (c q)")
        gone = pt[:, 3].rearrange("p c q -> p (c q)")[:, 0:NQ]
        gmean = pt[:, 4].rearrange("p c q -> p (c q)")[:, 0:P]
        gqk = pt[0:D, 5].rearrange("p c q -> p (c q)")[:, 0:NQ + NK]
        gw_ = sb("head_weights", [P, 2, D]); gb = sb("head_biases", [1, 2, D])
        gm = sb("general_max", [P, TB]); gr = sb("general_sum", [P, TB])
        gn = sb("numbers", [P, NB * H]); gnc = sb("numbers_count", [P, 1]); gi_ = sb("others", [P, 1], I32)
        ring = [ctx.enter_context(nc.psum_tensor(f"ring{i}", [P, 512], F32)) for i in range(RB)]
        pa = [ctx.enter_context(nc.psum_tensor(f"wide{i}", [P, 1024], F32)) for i in range(2)]
        pv = ctx.enter_context(nc.psum_tensor("pv", [P, 512], F32))
        turned = [pv, ring[2]]

        tally_ready = sem("tally_ready");
        gp_dve = sem("general_dve"); gp_pe = sem("general_pe"); gp_act = sem("general_act")
        gp_link = sem("general_link"); gp_mean = sem("general_mean"); gp_out = sem("general_out")
        wk_in = sem("wk_in"); wv_in = sem("wv_in"); bk_in = sem("bk_in"); bq_in = sem("bq_in"); bv_in = sem("bv_in")
        bo_in = sem("bo_in"); act_warm = sem("act_warm"); wide_full = sem("wide_full"); wide_free = sem("wide_free")
        cleared_cx = sem("cleared_cx"); cleared_half = sem("cleared_half"); cleared_ksL = sem("cleared_ksL")
        cleared_ks = sem("cleared_ks"); cleared_qs = sem("cleared_qs"); 
        cleared_v = sem("cleared_v"); shift_spread = sem("shift_spread"); cleared_ms = sem("cleared_ms"); cleared_row = sem("cleared_row")
        qs_base = sem("qs_base"); qs_equal = sem("qs_equal"); kparts_ready = sem("kparts_ready")
        ksL_ready = sem("ksL_ready"); ones_ready = sem("ones_ready")
        x_in = [sem(f"x_in{i}") for i in range(2)]
        cx_in = sem("cx_in"); wq_in = sem("wq_in"); wkv_in = sem("wkv_in")
        wo_in = sem("wo_in"); bias_in = sem("bias_in"); gates_in = sem("gates_in")
        zeros = sem("zeros"); ident = sem("ident"); cleared = sem("cleared")
        sel_ready = sem("sel_ready"); mask_step = sem("mask_step")
        gates_ready = sem("gates_ready")
        dv = sem("dve_chain"); pl = sem("pool_chain")
        aggr = sem("aggr"); rstd_ready = sem("rstd_ready"); xn_ready = sem("xn_ready")
        xT_ps = sem("xT_ps"); xT_ready = sem("xT_ready"); q_ps = sem("q_ps"); q_read = sem("q_read")
        qbase = sem("q_base"); qs_ready = sem("qs_ready"); qsT_ps = sem("qsT_ps"); qT_ready = sem("qT_ready")
        cT_ps = sem("cT_ps"); cT_ready = sem("cT_ready"); kv_ps = sem("kv_ps"); kv_read = sem("kv_read")
        v_ready = sem("v_ready"); ks_ready = [sem(f"ks_ready{b}") for b in range(NB)]; ksT_ps = sem("ksT_ps"); kT_ready = sem("kT_ready")
        ring_full = sem("ring_full"); ring_free = sem("ring_free")
        score_full = sem("score_full"); probs_ready = sem("probs_ready")
        shift_ready = sem("shift_ready"); mT_ready = sem("mT_ready")
        pv_full = sem("pv_full"); oT_ready = sem("oT_ready"); sum_done = sem("sum_done")
        xb_ready = sem("xb_ready"); on_ready = sem("on_ready"); x2_ready = sem("x2_ready")
        out_done = sem("out_done"); onT_ready = sem("onT_ready"); gw_in = sem("gw_in"); b1_in = sem("b1_in")
        b2_in = sem("b2_in"); w1_in = sem("w1_in"); w2_in = sem("w2_in"); rows_out = sem("rows_out")
        weight_ready = sem("weight_ready"); aggr2 = sem("aggr2"); rstd2_ready = sem("rstd2_ready")
        xn2_ready = sem("xn2_ready"); le_ready = sem("le_ready")
        oh_ready = sem("oh_ready"); rank_ps = sem("rank_ps"); iotas = sem("iotas"); consts2 = sem("consts2")
        olo_ready = sem("olo_ready"); inv_ps = sem("inv_ps"); index_ready = sem("index_ready")
        expert_ready = sem("expert_ready"); b1_ps = sem("b1_ps"); b1_ready = sem("b1_ready")
        gathered = [sem(f"gathered{i}") for i in range(NBLK)]
        xgT_ps = sem("xgT_ps"); xgT_ready = sem("xgT_ready"); w1c_ready = sem("w1c_ready")
        h_ps = sem("h_ps"); hb_ready = sem("hb_ready"); hidden_ready = sem("hidden_ready")
        scattered = [sem(f"scattered{i}") for i in range(4)]; y_ps = sem("y_ps"); y_read = sem("y_read"); yo_ready = sem("yo_ready")

        steps = plan()
        again = [(kind, u, 1) for u in range(U) for kind in ("back", "out", "normedT", "route")]
        ringed = [s for s in steps + again if s[0] in RING]
        fills = fillings(steps)
        exps = {}
        for s in steps:
            if s[0] == "score" and fills[s][0][1] == 3:
                exps[fills[s][0][0]] = len(exps)
        turn_of = {n: w.turn for w, n in exps.items()}
        at_ring = {s: n for n, s in enumerate(ringed)}
        freed = [sum(x[0] != "out" for x in ringed[:n + 1]) for n in range(len(ringed))]
        units = [(u, g) for u in range(U) for g in range(G)]

        odd_known = freed[at_ring[("check", U - 1, 0)]]
        last_free = freed[at_ring[steps[-1]]]

        def wide_of(u, g):
            return turn_of[(5 * (G * u + g) + 4) // 4]

        block = ctx.enter_context(nc.Block())

        def stack_k(copy, b, c):
            for par in range(2):
                src = kp[:, KPART[c], b * C:(b + 1) * C].rearrange("p (n m) -> p n m", m=2 * D)
                own = slice(D * par, D * par + D)
                o = ks[:, b * PR:(b + 1) * PR, par, 16 * c:16 * c + 16]
                copy(o[:, :, own], src[:, :, own]).then_inc(ks_ready[b], 1)

        @block.sync
        def _(sp):
            xv = a["x"].rearrange("b (t p) c -> p (b t) c", p=P)
            sp.dma_start(x[:, 0:TB, :], xv[:, 0:TB, :]).then_inc(x_in[0], 16)
            sp.dma_start(wk[:], a["L0_xattn_Wk"]).then_inc(wk_in, 16)
            sp.dma_start(wq[:], a["L0_xattn_Wq"]).then_inc(wq_in, 16)
            sp.dma_start(bias[:, 1, :], a["L0_xattn_bk"].partition_broadcast(P)).then_inc(bk_in, 16)
            sp.dma_start(bias[:, 0, :], a["L0_xattn_bq"].partition_broadcast(P)).then_inc(bq_in, 16)
            sp.dma_start(x[:, TB:T, :], xv[:, TB:T, :]).then_inc(x_in[1], 16)
            sp.dma_start(wv[:], a["L0_xattn_Wv"]).then_inc(wv_in, 16)
            sp.dma_start(bias[:, 2, :], a["L0_xattn_bv"].partition_broadcast(P)).then_inc(bv_in, 16)
            sp.dma_start(gates[:, 0:1], a["g_xattn"].partition_broadcast(P)).then_inc(gates_in, 16)
            sp.dma_start(gates[:, 1:2], a["g_ffn"].partition_broadcast(P)).then_inc(gates_in, 16)
            sp.dma_start(bias[:, 3, :], a["L0_xattn_bo"].partition_broadcast(P)).then_inc(bo_in, 16)
            sp.dma_start(wo[:], a["L0_xattn_Wo"]).then_inc(wo_in, 16)
            sp.dma_start(gw[:], a["L0_ffn_gate_w"]).then_inc(gw_in, 16)
            sp.dma_start(b1r[:], a["L0_ffn_b1"].rearrange("e (c p) -> (e c) p", p=P)).then_inc(b1_in, 16)
            sp.dma_start(b2[:], a["L0_ffn_b2"].partition_broadcast(P)).then_inc(b2_in, 16)
            w1v = a["L0_ffn_w1"].rearrange("e d f -> d e f")
            w2v = a["L0_ffn_w2"].rearrange("e (c p) n -> p e c n", p=P)
            for h in range(2):
                es = slice(h * E // 2, (h + 1) * E // 2)
                sp.dma_start(w1[:, es, :], w1v[:, es, :]).then_inc(w1_in, 16)
                for e in range(h * E // 2, (h + 1) * E // 2):
                    sp.dma_start(w2[:, e], w2v[:, e]).then_inc(w2_in, 16)
            rv = rows.rearrange("(t p) c -> p t c", p=P)

            def rows_of(n):
                for u in range(U):
                    sp.wait_ge(weight_ready, U * n + u + 1)
                    sp.dma_start(rv[:, UT * u:UT * u + UT, :], row[:, UT * u:UT * u + UT, :]).then_inc(rows_out, 16)

            rows_of(0)
            sp.wait_ge(ring_free, odd_known)
            with sp.If(sp.value_load(odd[0:1, 0:1], min_val=0, max_val=P * P) > 0):
                sp.wait_ge(rows_out, 16 * U)
                rows_of(1)

        @block.scalar
        def _(act):
            cv = a["ctx_768"]
            act.dma_start(cx[:, 0:2, :], cv[:, 0:P, :].rearrange("b p c -> p b c")).then_inc(cx_in, 16)
            for b in range(NB):
                act.dma_start(cx[KL * b:KL * b + KL, 2, :], cv[b, P:NK, :]).then_inc(cx_in, 16)
            act.wait_ge(zeros, 1)
            nc.scalar.activation(warm[:, 0:1], zf[:, 0:1], ACT.Exp).then_inc(act_warm, 1)
            pvs = 0

            def exponentials(s):
                u = s[1]
                act.wait_ge(ring_free, freed[at_ring[s]])
                ts = slice(UT * u, UT * u + UT)
                nc.scalar.activation(le[:, ts, :], ld[:, ts, :], ACT.Exp).then_inc(le_ready, 1)

            for s in steps:
                kind, u, n = s
                if kind in WIDE:
                    w = fills[s][0]
                    bank = pa[w.place]
                    act.wait_ge(wide_full, w.turn)
                if kind == "ctxT":
                    nc.scalar.activation(cxT[:], bank[0:CK, 0:NB * P], ACT.Copy).then_inc(cT_ready, 1)
                    act.wait_ge(cleared_cx, 1)
                    src = bank[0:CK, 256:256 + NB * KL].rearrange("c (b k) -> c b k", b=NB)
                    for b in range(NB):
                        last = nc.scalar.activation(cxL[:, b, :, 0:KL], src[:, b].unsqueeze(1).to_broadcast([CK, J, KL]),
                                                    ACT.Copy)
                        if b == 0:
                            last.then_inc(cT_ready, 1)
                    last.then_inc(wide_free, 1)
                elif kind == "xT":
                    nc.scalar.activation(xnT[:, u * 512:(u + 1) * 512], bank[:, 0:512], ACT.Copy).then_inc(wide_free, 1)
                elif kind == "kT":
                    nc.scalar.activation(kT[:, u].rearrange("p h q -> p (h q)"), bank[:].bitcast(BF16),
                                         ACT.Copy).then_inc(wide_free, 1)
                elif kind == "qT":
                    src = bank[0:STK].bitcast(BF16).rearrange("p (t r q) -> p r t q", t=UT, r=PR)
                    o = qT[0:STK, :, UQ * u:UQ * u + UQ].rearrange("p r (t q) -> p r t q", t=UT)
                    for t in range(UT):
                        last = nc.scalar.activation(o[:, :, t, :], src[:, :, t, :], ACT.Copy)
                    last.then_inc(wide_free, 1)
                elif kind == "shift":
                    src = bank[STK:P, 0:UQ // 2].bitcast(BF16).unsqueeze(1).to_broadcast([P - STK, 2, UQ])
                    nc.scalar.activation(qT[STK:P, 0:2, UQ * u:UQ * u + UQ], src, ACT.Copy).then_inc(wide_free, 1)
                elif kind == "k":
                    act.wait_ge(kparts_ready, 1)
                    act.wait_ge(cleared_ks, 1)
                    for c in range(NC):
                        if KPART[c] == 0:
                            stack_k(nc.scalar.copy, 0, c)
                elif kind == "q":
                    for c in (1, 2, 4):
                        act.wait_ge(qs_base, 3 * u + (1 if c < 4 else 2))
                        o = qs[:, UT * u:UT * u + UT].rearrange("p t r c m -> p (t r) c m")
                        nc.scalar.activation(o[:, :, c, :], o[:, :, 0 if c < 4 else 3, :], ACT.Copy).then_inc(qs_equal, 1)
                elif kind == "score":
                    w, quarter = fills[s][0]
                    if quarter == 3:
                        act.wait_ge(wide_full, w.turn)
                        done = exps[w]
                        if done >= NPT:
                            act.wait_ge(pv_full, (4 * (done - NPT) + 3) // 5 + 1)
                        nc.scalar.activation(pt[:, done % NPT].rearrange("p c q -> p (c q)"), pa[w.place][:],
                                             ACT.Exp, scale=SCALE).then_inc(wide_free, 1)
                elif kind == "route":
                    exponentials(s)
                elif kind == "pv":
                    act.wait_ge(pv_full, pvs + 1)
                    if pvs >= 2:
                        act.wait_ge(ring_full, at_ring[("turn", (pvs - 2) // G, (pvs - 2) % G)] + 1)
                    nc.scalar.activation(oT[:, pvs % 2, :], pv[:, 0:UQ], ACT.Copy).then_inc(oT_ready, 1)
                    pvs += 1
                if s == ("q", 1, 0):
                    act.wait_ge(gates_in, 32)
                    nc.scalar.activation(tg[:], gates[:], ACT.Tanh).then_inc(gates_ready, 1)
            act.wait_ge(ring_free, odd_known)
            with act.If(act.value_load(odd[0:1, 0:1], min_val=0, max_val=P * P) > 0):
                for b in range(NB):
                    with act.Fori(0, H) as h:
                        it = h * GA + b * H * GA
                        act.wait_ge(gp_pe, h * GP + (b * H * GP + 1))
                        nc.scalar.activation(gqk, pa[1][0:D, 0:NQ + NK], ACT.Copy).then_inc(gp_act, 1)
                        act.wait_ge(gp_dve, h * GD + (b * H * GD + 10))
                        nc.scalar.activation(gs, gs, ACT.Exp).then_inc(gp_act, 1)
                        act.wait_ge(gp_pe, h * GP + (b * H * GP + 3))
                        nc.scalar.activation(gpT[:, 0:NQ], pa[1][:, 0:NQ], ACT.Copy).then_inc(gp_act, 1)
                        nc.scalar.activation(gpT[0:KL, NQ:], pa[1][0:KL, NQ:], ACT.Copy).then_inc(gp_act, 1)
                for s in again:
                    if s[0] == "route":
                        exponentials(s)
            act.wait_ge(act_warm, 1)
            nc.scalar.activation(warm[:, 1:2], warm[:, 0:1], ACT.Gelu).then_inc(act_warm, 1)

            def copy_turned(i):
                act.wait_ge(xgT_ps, i + 1)
                if i >= 2:
                    act.wait_ge(h_ps, i - 1)
                nc.scalar.activation(xgT[:, i % 2], turned[i % 2][:, 0:P], ACT.Copy).then_inc(xgT_ready, 1)

            copy_turned(0)
            copy_turned(1)
            for i in range(NBLK):
                if i + 2 < NBLK:
                    copy_turned(i + 2)
                act.wait_ge(hb_ready, i + 1)
                if i >= 2:
                    act.wait_ge(y_ps, i - 1)
                nc.scalar.activation(hT[:, i % 2], hb[:, i % 2], ACT.Gelu).then_inc(hidden_ready, 1)

        @block.gpsimd
        def _(pool):
            nc.gpsimd.memset(zf[:], 0.0).then_inc(zeros, 1)
            nc.gpsimd.memset(zb[:], 0.0).then_inc(zeros, 1)
            pool.wait_ge(zeros, 2)
            for o, z in ((idf, zf), (idb, zb)):
                nc.gpsimd.affine_select(out=o[:], in_=z[:], compare_op=ALU.not_equal, fill=1.0, base=0,
                                        pattern=[[-1, P]], channel_multiplier=1).then_inc(ident, 1)
            nc.gpsimd.memset(cxL[:], 0.0).then_inc(cleared_cx, 1)
            nc.gpsimd.memset(mhalf[:], -0.5).then_inc(cleared_half, 1)
            nc.gpsimd.memset(lmask[:], 1.0).then_inc(mask_step, 1)
            pool.wait_ge(mask_step, 1)
            nc.gpsimd.affine_select(out=lmask[:], in_=lmask[:], compare_op=ALU.is_ge, fill=0.0, base=0,
                                    pattern=[[-32, J]], channel_multiplier=1).then_inc(mask_step, 1)
            pool.wait_ge(mask_step, 2)
            nc.gpsimd.affine_select(out=lmask[:], in_=lmask[:], compare_op=ALU.is_ge, fill=0.0, base=KL - 1,
                                    pattern=[[32, J]], channel_multiplier=-1).then_inc(mask_step, 1)
            nc.gpsimd.memset(ksL[:].rearrange("p n m -> p (n m)").bitcast(F32), 0.0).then_inc(cleared_ksL, 1)
            pool.wait_ge(cleared_ksL, 1)
            pool.wait_ge(mask_step, 3)
            for part in range(2):
                for j in range(J):
                    at = STK + H * part + j
                    o = ksL[:].rearrange("p (b g) m -> p b (g m)", b=NB)[:, :, at:at + (P + J) * (G - 1) + 1:P + J]
                    nc.gpsimd.tensor_copy(o, lmask[:, j:j + 1].unsqueeze(1).to_broadcast([P, NB, G])).then_inc(ones_ready, 1)

            def inverse_std(b):
                ts = slice(b * TB, (b + 1) * TB)
                pool.wait_ge(aggr, TB * (b + 1))
                nc.gpsimd.tensor_scalar(ve[:, ts], mv[:, ts, 1], EPS, None, ALU.add).then_inc(pl, 1)
                pool.wait_ge(pl, b + 1)
                pool.wait_ge(cleared_half, 1)
                nc.gpsimd.tensor_tensor(rstd[:, ts], ve[:, ts], mhalf[:, ts], ALU.pow).then_inc(rstd_ready, 1)

            inverse_std(0)
            nc.gpsimd.memset(qs[:, 0:UT, :, NC:, :], 0.0).then_inc(cleared_qs, 1)
            pool.wait_ge(kparts_ready, 3)
            for c in range(NC):
                nc.gpsimd.tensor_copy(ksL[:, :, 16 * c:16 * c + 16],
                                      kp[:, KPART[c], NB * C:].rearrange("p (n m) -> p n m", m=16)).then_inc(ksL_ready, 1)
            inverse_std(1)
            pool.wait_ge(cleared_ks, 1)
            for c in range(NC):
                stack_k(nc.gpsimd.tensor_copy, 1, c)
            for u in range(1, U):
                nc.gpsimd.memset(qs[:, UT * u:UT * u + UT, :, NC:, :], 0.0).then_inc(cleared_qs, 1)
            nc.gpsimd.memset(v[:].rearrange("p b h m -> p (b h m)"), 0.0).then_inc(cleared_v, 1)
            nc.gpsimd.memset(vL[:].rearrange("p b g j m -> p (b g j m)"), 0.0).then_inc(cleared_v, 1)
            nc.gpsimd.memset(ms[:].rearrange("p t m -> p (t m)").bitcast(F32), 0.0).then_inc(cleared_ms, 1)
            nc.gpsimd.memset(row[:, :, 2 * C:], 0.0).then_inc(cleared_row, 1)
            pool.wait_ge(gates_ready, 1)
            pool.wait_ge(bo_in, 16)
            nc.gpsimd.tensor_scalar(bias[:, 3, :], bias[:, 3, :], tg[:, 0:1], None, ALU.mult).then_inc(xb_ready, 1)
            pool.wait_ge(xb_ready, 1)
            for b in range(NB):
                pool.wait_ge(x_in[b], 16)
                nc.gpsimd.tensor_tensor(xb[:, b * TB:(b + 1) * TB, :], x[:, b * TB:(b + 1) * TB, :],
                                        bias[:, 3:4, :].to_broadcast([P, TB, C]), ALU.add).then_inc(xb_ready, 1)
            nc.gpsimd.iota(iota_i[:], [[1, P]], base=0, channel_multiplier=0).then_inc(iotas, 1)
            nc.gpsimd.iota(ip_i[:], [[0, 1]], base=0, channel_multiplier=1).then_inc(iotas, 1)
            nc.gpsimd.memset(ones[:], 1.0).then_inc(iotas, 1)
            nc.gpsimd.memset(one8[:], 1.0).then_inc(iotas, 1)
            pool.wait_ge(iotas, 4)
            nc.gpsimd.tensor_copy(io[:], iota_i[:]).then_inc(consts2, 1)
            nc.gpsimd.tensor_copy(iob[:], iota_i[:]).then_inc(consts2, 1)
            nc.gpsimd.memset(base[:, 0:1], 0.0).then_inc(consts2, 1)
            nc.gpsimd.tensor_copy(ip[:], ip_i[:]).then_inc(consts2, 1)
            nc.gpsimd.affine_select(out=tri[:], in_=ones[:], compare_op=ALU.is_gt, fill=0.0, base=0,
                                    pattern=[[1, P]], channel_multiplier=-1).then_inc(consts2, 1)
            pool.wait_ge(consts2, 5)
            nc.gpsimd.tensor_scalar(rev[:], io[:, 0:E], -1.0, float(E), ALU.mult, ALU.add).then_inc(consts2, 1)
            nc.gpsimd.tensor_scalar(first[:], io[:, 0:E], 0.0, 0.5, ALU.is_equal, ALU.mult).then_inc(consts2, 1)
            nc.gpsimd.tensor_scalar(hi128[:], io[:, 0:NBLK + 1], float(P), None, ALU.mult).then_inc(consts2, 1)
            def inverse_std2(u, n):
                ts = slice(UT * u, UT * u + UT)
                pool.wait_ge(aggr2, UT * (U * n + u + 1))
                nc.gpsimd.tensor_scalar(ve2[:, ts], mv2[:, ts, 1], EPS, None, ALU.add).then_inc(pl, 1)
                pool.wait_ge(pl, NB + U * n + u + 1)
                nc.gpsimd.tensor_tensor(rstd2[:, ts], ve2[:, ts], mhalf[:, ts], ALU.pow).then_inc(rstd2_ready, 1)

            for u in range(U):
                inverse_std2(u, 0)
            pool.wait_ge(ring_free, odd_known)
            with pool.If(pool.value_load(odd[0:1, 0:1], min_val=0, max_val=P * P) > 0):
                for u in range(U):
                    inverse_std2(u, 1)
                pool.wait_ge(oh_ready, 2 * U)
                pool.wait_ge(rows_out, 2 * 16 * U)
            ov = out.rearrange("b q c -> (b q) c")
            pool.wait_ge(rows_out, 16 * U)
            pool.wait_ge(index_ready, 1)
            for i in range(NBLK + AHEAD):
                if i < NBLK:
                    nc.gpsimd.indirect_dma_start(xg[:, i, :], None, rows[:],
                                                 bass.IndirectOffsetOnAxis(ap=gi[:, i:i + 1], axis=0)
                                                 ).then_inc(gathered[i], 16)
                if i >= AHEAD:
                    m = i - AHEAD
                    pool.wait_ge(index_ready, 2)
                    pool.wait_ge(yo_ready, m + 1)
                    nc.gpsimd.indirect_dma_start(ov, bass.IndirectOffsetOnAxis(ap=si[:, m:m + 1], axis=0),
                                                 yo[:, m % 4, :], None, bounds_check=T * P - 1,
                                                 oob_is_err=False).then_inc(scattered[m % 4], 16)
            for m in range(4):
                pool.wait_ge(scattered[m], 16 * len(range(m, NBLK, 4)))

        @block.vector
        def _(dve):
            chain = {"sem": dv, "count": 0}

            def link(ins):
                chain["count"] += 1
                ins.then_inc(chain["sem"], 1)
                dve.wait_ge(chain["sem"], chain["count"])

            def statistics(b):
                dve.wait_ge(x_in[b], 16)
                for t in range(b * TB, (b + 1) * TB):
                    last = nc.vector.bn_stats(st[:, t, :], x[:, t, :])
                link(last)
                for t in range(b * TB, (b + 1) * TB):
                    nc.vector.bn_aggr(mv[:, t, :], st[:, t, :]).then_inc(aggr, 1)

            def normalise(b):
                dve.wait_ge(rstd_ready, b + 1)
                for t in range(b * TB, (b + 1) * TB):
                    nc.vector.tensor_scalar(xn[:, t, :], x[:, t, :], mv[:, t, 0:1], rstd[:, t:t + 1],
                                            ALU.subtract, ALU.mult).then_inc(xn_ready, 1)

            nc.vector.memset(ks[:].rearrange("p n a m -> p (n a m)").bitcast(F32), 0.0).then_inc(cleared_ks, 1)
            statistics(0)
            normalise(0)

            def step(s):
                kind, u, n = s
                if kind == "shift":
                    uq = slice(UQ * u, UQ * u + UQ)
                    dve.wait_ge(wide_free, fills[s][0].turn)
                    nc.vector.tensor_copy(qT[STK:P, 2:, uq], qT[STK:P, 0:1, uq].to_broadcast([P - STK, PR - 2, UQ])
                                          ).then_inc(shift_spread, 1)
                if s not in at_ring:
                    return
                r = at_ring[s]
                bank = ring[r % RB]
                if kind == "k":
                    dve.wait_ge(bk_in, 16)
                    dve.wait_ge(mask_step, 3)
                    dve.wait_ge(ring_full, r + 1)
                    kb = bias[:, 1:2, :].to_broadcast([P, NB, C])
                    nc.vector.tensor_tensor(k[:, 0:NB * C].rearrange("p (b c) -> p b c", b=NB),
                                            bank[:, 0:NB * C].rearrange("p (b c) -> p b c", b=NB), kb, ALU.add)
                    nc.vector.tensor_tensor(kl[:], bank[:, NB * C:].rearrange("p (b c) -> p b c", b=NB), kb,
                                            ALU.add).then_inc(ring_free, 1)
                    dve.wait_ge(ring_free, freed[r])
                    klj = kl[:].rearrange("p b (g j m) -> p (b g) j m", j=J, m=D)
                    link(nc.vector.tensor_tensor(klj, klj, lmask[:].unsqueeze(1).unsqueeze(3).to_broadcast([P, NB * G, J, D]),
                                                 ALU.mult))
                    link(nc.vector.tensor_tensor(k[:, NB * C:].rearrange("p (n m) -> p n m", m=2 * D),
                                                 klj[:, :, 0:2].rearrange("p n j m -> p n (j m)"),
                                                 klj[:, :, 2:4].rearrange("p n j m -> p n (j m)"), ALU.add))
                    nc.vector.tensor_copy(kp[:, 0], k[:]).then_inc(kparts_ready, 1)
                    dve.wait_ge(kparts_ready, 1)
                    link(nc.vector.tensor_tensor(kr[:], k[:], kp[:, 0], ALU.subtract))
                    nc.vector.tensor_copy(kp[:, 1], kr[:]).then_inc(kparts_ready, 1)
                    dve.wait_ge(kparts_ready, 2)
                    nc.vector.tensor_tensor(kp[:, 2], kr[:], kp[:, 1], ALU.subtract).then_inc(kparts_ready, 1)
                    dve.wait_ge(kparts_ready, 3)
                    dve.wait_ge(cleared_ks, 1)
                    for c in range(NC):
                        if KPART[c]:
                            stack_k(nc.vector.tensor_copy, 0, c)
                    for b in range(NB):
                        for part in range(2):
                            at = STK + H * part
                            o = ks[:, b * PR:(b + 1) * PR].rearrange("p r a m -> p (r a m)")[:, at:at + (P + 1) * (H - 1) + 1:P + 1]
                            nc.vector.memset(o, 1.0).then_inc(ks_ready[b], 1)
                elif kind == "q":
                    if u == 0:
                        dve.wait_ge(bq_in, 16)
                    dve.wait_ge(ring_full, r + 1)
                    qu, qru = q[:, u % 2], qr[:, u % 2]
                    nc.vector.tensor_tensor(qu, bank[:, 0:UT * C].rearrange("p (t c) -> p t c", c=C),
                                            bias[:, 0:1, :].to_broadcast([P, UT, C]), ALU.add).then_inc(ring_free, 1)
                    dve.wait_ge(ring_free, freed[r])
                    qf = qu.rearrange("p t (r m) -> p (t r) m", m=16)
                    qrf = qru.rearrange("p t (r m) -> p (t r) m", m=16)
                    o = qs[:, UT * u:UT * u + UT].rearrange("p t r c m -> p (t r) c m")
                    nc.vector.tensor_copy(o[:, :, 0, :], qf).then_inc(qs_base, 1)
                    dve.wait_ge(qs_base, 3 * u + 1)
                    link(nc.vector.tensor_tensor(qrf, qf, o[:, :, 0, :], ALU.subtract))
                    nc.vector.tensor_copy(o[:, :, 3, :], qrf).then_inc(qs_base, 1)
                    dve.wait_ge(qs_base, 3 * u + 2)
                    nc.vector.tensor_tensor(o[:, :, 5, :], qrf, o[:, :, 3, :], ALU.subtract).then_inc(qs_base, 1)
                    if u == 0:
                        statistics(1)
                        normalise(1)
                elif kind == "kLT":
                    dve.wait_ge(ring_full, r + 1)
                    nc.vector.tensor_copy(kLT[:].rearrange("p b g q -> p (b g q)"), bank[:].bitcast(BF16)).then_inc(ring_free, 1)
                elif kind == "v":
                    dve.wait_ge(ring_full, r + 1)
                    dve.wait_ge(bv_in, 16)
                    dve.wait_ge(cleared_v, 2)
                    for b in range(NB):
                        nc.vector.tensor_tensor(v[:, b, :, 0:D], bank[:, b * C:(b + 1) * C].rearrange("p (h d) -> p h d", d=D),
                                                bias[:, 2, :].rearrange("p (h d) -> p h d", d=D), ALU.add).then_inc(v_ready, 1)
                    nc.vector.memset(v[:, :, :, D:D + 1], 1.0).then_inc(v_ready, 1)
                    nc.vector.tensor_tensor(vLf[:], bank[:, 256:512].rearrange("p (b c) -> p b c", b=NB),
                                            bias[:, 2:3, :].to_broadcast([P, NB, C]), ALU.add).then_inc(ring_free, 1)
                    dve.wait_ge(ring_free, freed[r])
                    for j in range(J):
                        src = vLf[:].rearrange("p b (g m) -> p (b g) m", g=G)[:, :, 8 * j:8 * j + 8]
                        o = vL[:, :, :, j, :].rearrange("p b g m -> p (b g) m")
                        nc.vector.tensor_scalar(o[:, :, 0:D], src, lmask[:, j:j + 1], None, ALU.mult).then_inc(v_ready, 1)
                        nc.vector.tensor_copy(o[:, :, D], lmask[:, j:j + 1].to_broadcast([P, NB * G])).then_inc(v_ready, 1)
                elif kind == "max":
                    t, part = UT * u + n // 5, n % 5
                    dve.wait_ge(ring_full, r + 1)
                    if part < 4:
                        nc.vector.tensor_reduce(mm[:, t, 4 * part:4 * part + 4],
                                                bank[:].rearrange("p (h k) -> p h k", k=P), AX.X,
                                                ALU.max).then_inc(ring_free, 1)
                    else:
                        nc.vector.tensor_reduce(ml[:, t, :], bank[:].rearrange("p (h k) -> p h k", k=32)[:, :, 0:KL],
                                                AX.X, ALU.max).then_inc(ring_free, 1)
                    if n == 5 * UT - 1:
                        ts = slice(UT * u, UT * u + UT)
                        dve.wait_ge(ring_free, freed[r])
                        dve.wait_ge(cleared_ms, 1)
                        link(nc.vector.tensor_tensor(mx[:, ts, :], mm[:, ts, :], ml[:, ts, :], ALU.max))
                        link(nc.vector.tensor_scalar(ms[:, ts, STK:STK + H], mx[:, ts, :], -1.0, None, ALU.mult))
                        nc.vector.scalar_tensor_tensor(ms[:, ts, STK + H:P], mx[:, ts, :], -1.0,
                                                       ms[:, ts, STK:STK + H], ALU.mult, ALU.subtract).then_inc(shift_ready, 1)
                elif kind == "turn":
                    dve.wait_ge(ring_full, r + 1)
                    got = bank[:, 0:UT * P].rearrange("p (a m) -> p a m", m=32)
                    m = G * u + n
                    rc = rcs[:, UT * J * m:UT * J * m + UT * J].rearrange("p (t j) -> p t j", j=J)
                    link(nc.vector.reciprocal(rcs[:, UT * J * m:UT * J * m + UT * J], got[:, :, D]))
                    for t in range(UT):
                        last = nc.vector.tensor_tensor(
                            ot[:, u % 2, t, 32 * n:32 * n + 32].rearrange("p (j d) -> p j d", d=D),
                            got[:, J * t:J * t + J, 0:D], rc[:, t].unsqueeze(2).to_broadcast([P, J, D]), ALU.mult)
                    last.then_inc(ring_free, 1)
                elif kind == "check":
                    mxf = mx[:].rearrange("p t h -> p (t h)")
                    link(nc.vector.tensor_scalar(fine[:], mxf, -LIMIT, None, ALU.is_ge))
                    link(nc.vector.scalar_tensor_tensor(fine[:], mxf, LIMIT, fine[:], ALU.is_le, ALU.mult))
                    link(nc.vector.tensor_tensor(fine2[:], rcs[:], rcs[:], ALU.is_equal))
                    link(nc.vector.tensor_tensor(fine[:], fine[:], fine2[:], ALU.mult))
                    with nc.allow_low_precision("whole numbers up to 128"):
                        nc.vector.tensor_reduce(finec[:], fine[:], AX.X, ALU.add).then_inc(tally_ready, 1)
                    dve.wait_ge(ring_full, r + 1)
                    nc.vector.tensor_scalar(odd[:], bank[:, 0:1], -1.0, float(P * P), ALU.mult, ALU.add).then_inc(ring_free, 1)
                elif kind == "back":
                    dve.wait_ge(ring_full, r + 1)
                    nc.vector.tensor_copy(onT[:, u % 2], bank[:, 0:UQ]).then_inc(ring_free, 1)
                elif kind == "out":
                    dve.wait_ge(ring_full, r + 1)
                    dve.wait_ge(xb_ready, 3)
                    ts = slice(UT * u, UT * u + UT)
                    nc.vector.scalar_tensor_tensor(x2[:, ts, :], bank[:, 0:UT * C].rearrange("p (t c) -> p t c", c=C),
                                                   tg[:, 0:1], xb[:, ts, :], ALU.mult, ALU.add).then_inc(x2_ready, 1)
                    dve.wait_ge(x2_ready, U * n + u + 1)
                    for t in range(UT * u, UT * u + UT):
                        last = nc.vector.bn_stats(st2[:, t, :], x2[:, t, :])
                    link(last)
                    for t in range(UT * u, UT * u + UT):
                        nc.vector.bn_aggr(mv2[:, t, :], st2[:, t, :]).then_inc(aggr2, 1)
                    dve.wait_ge(rstd2_ready, U * n + u + 1)
                    for t in range(UT * u, UT * u + UT):
                        nc.vector.tensor_scalar(xn2[:, t, :], x2[:, t, :], mv2[:, t, 0:1], rstd2[:, t:t + 1],
                                                ALU.subtract, ALU.mult).then_inc(xn2_ready, 1)
                elif kind == "normedT":
                    dve.wait_ge(ring_full, r + 1)
                    nc.vector.tensor_copy(xn2T[:, u % 2], bank[:, 0:UQ]).then_inc(ring_free, 1)
                elif kind == "route":
                    ts = slice(UT * u, UT * u + UT)
                    dve.wait_ge(consts2, 8)
                    dve.wait_ge(ring_full, r + 1)
                    logits = bank[:, 0:UT * E].rearrange("p (t e) -> p t e", e=E)
                    link(nc.vector.tensor_reduce(lmax[:, ts], logits, AX.X, ALU.max))
                    nc.vector.tensor_tensor(ld[:, ts, :], logits, lmax[:, ts].unsqueeze(2).to_broadcast([P, UT, E]),
                                            ALU.subtract).then_inc(ring_free, 1)
                    dve.wait_ge(ring_free, freed[r])
                    link(nc.vector.scalar_tensor_tensor(eq[:, ts, :], ld[:, ts, :], 0.0,
                                                        rev[:].unsqueeze(1).to_broadcast([P, UT, E]), ALU.is_equal, ALU.mult))
                    link(nc.vector.tensor_tensor(eq[:, ts, :], eq[:, ts, :], first[:].unsqueeze(1).to_broadcast([P, UT, E]),
                                                 ALU.add))
                    link(nc.vector.tensor_reduce(em[:, ts], eq[:, ts, :], AX.X, ALU.max))
                    nc.vector.tensor_tensor(oh[:, ts, :], eq[:, ts, :], em[:, ts].unsqueeze(2).to_broadcast([P, UT, E]),
                                            ALU.is_equal).then_inc(oh_ready, 1)
                    dve.wait_ge(le_ready, U * n + u + 1)
                    link(nc.vector.tensor_reduce(ls[:, ts], le[:, ts, :], AX.X, ALU.add))
                    link(nc.vector.reciprocal(lr[:, ts], ls[:, ts]))
                    dve.wait_ge(cleared_row, 1)
                    nc.vector.tensor_scalar(row[:, ts, 2 * C], lr[:, ts], tg[:, 1:2], None, ALU.mult).then_inc(weight_ready, 1)

            for s in steps:
                step(s)
            dve.wait_ge(ring_free, odd_known)
            with dve.If(dve.value_load(odd[0:1, 0:1], min_val=0, max_val=P * P) > 0):
                chain["sem"], chain["count"], before = gp_link, 0, chain["count"]
                link(nc.vector.memset(gone, 1.0))
                nc.vector.memset(gmean, 1.0 / NK).then_inc(gp_mean, 1)
                for b in range(NB):
                    with dve.Fori(0, H) as h:
                        done = [0]

                        def then(ins):
                            done[0] += 1
                            ins.then_inc(gp_dve, 1)
                            dve.wait_ge(gp_dve, h * GD + (b * H * GD + done[0]))

                        cols = bass.ds(h * D, D)
                        for n, w in ((0, wq), (1, wk)):
                            rows_ = slice(0, C if n == 0 else CK)
                            then(nc.vector.tensor_copy(gw_[rows_, n, :], w[rows_, cols]))
                            then(nc.vector.tensor_copy(gb[:, n, :], bias[0:1, n, cols]))
                        dve.wait_ge(gp_pe, h * GP + (b * H * GP + 2))
                        got = pa[0][:].rearrange("p (t k) -> p t k", t=TB)[:, :, 0:NK]
                        then(nc.vector.tensor_scalar(gs, got, SCALE, None, ALU.mult))
                        then(nc.vector.tensor_tensor(gok, gs, gs, ALU.is_equal))
                        then(nc.vector.tensor_reduce(gn[:, bass.ds(h + b * H, 1)], gok, AX.XY, ALU.add))
                        then(nc.vector.tensor_scalar(gs, gs, CLAMP, -CLAMP, ALU.min, ALU.max))
                        then(nc.vector.tensor_reduce(gm[:], gs, AX.X, ALU.max))
                        then(nc.vector.tensor_tensor(gs, gs, gm[:].unsqueeze(2).to_broadcast([P, TB, NK]), ALU.subtract))
                        dve.wait_ge(gp_act, h * GA + (b * H * GA + 2))
                        then(nc.vector.tensor_reduce(gm[:], gs, AX.X, ALU.add))
                        then(nc.vector.reciprocal(gr[:], gm[:]))
                        then(nc.vector.tensor_tensor(gs, gs, gr[:].unsqueeze(2).to_broadcast([P, TB, NK]), ALU.mult))
                        dve.wait_ge(gp_pe, h * GP + (b * H * GP + 4))
                        then(nc.vector.tensor_copy(xn[:, b * TB:(b + 1) * TB, cols],
                                                   pv[:, 0:TB * D].rearrange("p (t d) -> p t d", d=D)))
                        assert done[0] == GD
                link(nc.vector.tensor_reduce(gnc[:], gn[:], AX.X, ALU.add))
                dve.wait_ge(gp_mean, 2)
                link(nc.vector.tensor_scalar(gi_[:], pv[:, 0:1], -1.0, float(P * NB * H * TB * NK), ALU.mult, ALU.add))
                with dve.If(dve.value_load(gi_[0:1, 0:1], min_val=0, max_val=P * NB * H * TB * NK) > 0):
                    for t in range(T):
                        nc.vector.tensor_copy(xn[:, t, :], ring[0][:, (t // TB) * C:(t // TB) * C + C]).then_inc(gp_out, 1)
                    dve.wait_ge(gp_out, T)
                nc.vector.tensor_copy(gm[:, 0:1], gnc[:]).then_inc(gp_link, 1)
                chain["count"] += 1
                dve.wait_ge(rows_out, 16 * U)
                for s in again:
                    step(s)
                chain["sem"], chain["count"] = dv, before
            dve.wait_ge(rank_ps, 1)
            cnt = pv[:, T * E:T * E + E]
            dve.wait_ge(oh_ready, U)
            link(nc.vector.tensor_tensor(nbk[:], cnt.unsqueeze(2).to_broadcast([P, E, T]),
                                         hi128[:, 0:T].unsqueeze(1).to_broadcast([P, E, T]), ALU.is_gt))
            link(nc.vector.tensor_reduce(nb[:], nbk[:], AX.X, ALU.add))
            link(nc.vector.tensor_tensor_scan(base[:, 1:E], one8[:, 1:E], nb[:, 0:E - 1], 0.0, ALU.mult, ALU.add))
            link(nc.vector.scalar_tensor_tensor(sl[:], base[:].unsqueeze(1).to_broadcast([P, T, E]), float(P),
                                                pv[:, 0:T * E].rearrange("p (t e) -> p t e", e=E), ALU.mult, ALU.add))
            link(nc.vector.tensor_tensor(sl[:], sl[:], oh[:], ALU.mult))
            link(nc.vector.tensor_reduce(slot[:], sl[:], AX.X, ALU.add))
            link(nc.vector.tensor_tensor(ge[:], slot[:].unsqueeze(2).to_broadcast([P, T, NBLK + 1]),
                                    hi128[:].unsqueeze(1).to_broadcast([P, T, NBLK + 1]), ALU.is_ge))
            link(nc.vector.tensor_reduce(hs[:], ge[:, :, 1:], AX.X, ALU.add))
            link(nc.vector.scalar_tensor_tensor(lo[:], hs[:], -float(P), slot[:], ALU.mult, ALU.add))
            for t in range(T):
                nc.vector.tensor_scalar(olo[:, t, :], iob[:], lo[:, t:t + 1], None, ALU.is_equal).then_inc(olo_ready, 1)
            link(nc.vector.tensor_tensor(rhs[:, :, 0, :], ge[:, :, 0:NBLK], ge[:, :, 1:NBLK + 1], ALU.subtract))
            nc.vector.tensor_scalar(rhs[:, :, 1, :], rhs[:, :, 0, :], ip[:], None, ALU.mult).then_inc(olo_ready, 1)
            nc.vector.tensor_tensor(rhs[:, :, 2, :], rhs[:, :, 0, :], hi128[:, 0:T].unsqueeze(2).to_broadcast([P, T, NBLK]),
                                    ALU.mult).then_inc(olo_ready, 1)
            link(nc.vector.tensor_tensor(end[:], base[:], nb[:], ALU.add))
            link(nc.vector.tensor_tensor(bge[:], io[:, 0:NBLK].unsqueeze(2).to_broadcast([P, NBLK, E]),
                                         end[:].unsqueeze(1).to_broadcast([P, NBLK, E]), ALU.is_ge))
            link(nc.vector.tensor_reduce(bef[:], bge[:], AX.X, ALU.add))
            nc.vector.tensor_scalar(be[:], bef[:], float(E - 1), None, ALU.min).then_inc(expert_ready, 1)
            dve.wait_ge(inv_ps, 1)
            inv = ring[1][:, 0:3 * NBLK].rearrange("p (a i) -> p a i", a=3)
            link(nc.vector.tensor_reduce(tokf[:], inv[:, 1:3].rearrange("p a i -> p i a"), AX.X, ALU.add))
            nc.vector.tensor_copy(gi[:], tokf[:]).then_inc(index_ready, 1)
            link(nc.vector.scalar_tensor_tensor(sif[:], inv[:, 0], -float(2 * T * P), tokf[:], ALU.mult, ALU.add))
            nc.vector.tensor_scalar(si[:], sif[:], float(2 * T * P), None, ALU.add).then_inc(index_ready, 1)
            dve.wait_ge(b1_ps, 1)
            nc.vector.tensor_copy(b1[:], ring[0][:, 0:E * FC]).then_inc(b1_ready, 1)
            dve.wait_ge(b1_ready, 1)
            dve.wait_ge(w1_in, 32)
            dve.wait_ge(b2_in, 16)
            dve.wait_ge(expert_ready, 1)
            ex = {}

            def weights(i):
                ex[i] = nc.vector.value_load(be[0:1, i:i + 1], min_val=0, max_val=E - 1)
                if i >= 2:
                    dve.wait_ge(h_ps, i - 1)
                src = w1[:].rearrange("d e f -> d (e f)")[:, bass.ds(ex[i] * FF, FF)]
                nc.vector.tensor_copy(w1c[:, i % 2, :], src).then_inc(w1c_ready, 1)

            def finish(i):
                dve.wait_ge(y_ps, i + 1)
                bsl = b2[:].rearrange("p e c -> p (e c)")[:, bass.ds(ex[i] * C, C)]
                nc.vector.tensor_tensor(yb[:, i % 2, :], ring[i % 2][:, 0:C], bsl, ALU.add).then_inc(y_read, 1)
                dve.wait_ge(y_read, i + 1)
                if i >= 4:
                    dve.wait_ge(scattered[i % 4], 16 * (i // 4))
                g = xg[:, i, :]
                nc.vector.scalar_tensor_tensor(yo[:, i % 4, :], yb[:, i % 2, :], g[:, 2 * C:2 * C + 1], g[:, C:2 * C],
                                               ALU.mult, ALU.add).then_inc(yo_ready, 1)

            weights(0)
            weights(1)
            for i in range(NBLK):
                dve.wait_ge(h_ps, i + 1)
                if i >= 2:
                    dve.wait_ge(hidden_ready, i - 1)
                bb = b1[:, bass.ds(ex[i] * FC, FC)].unsqueeze(2).to_broadcast([P, FC, P])
                nc.vector.tensor_tensor(hb[:, i % 2].rearrange("p (c q) -> p c q", c=FC),
                                        pa[i % 2][:, 0:FF].rearrange("p (c q) -> p c q", c=FC), bb, ALU.add).then_inc(hb_ready, 1)
                if i + 2 < NBLK:
                    weights(i + 2)
                if i:
                    finish(i - 1)
            finish(NBLK - 1)

        @block.tensor
        def _(pe):
            pe.wait_ge(ident, 2)
            pvs = [0]

            def step(s):
                kind, u, n = s
                b = u * UT // TB
                uq = slice(UQ * u, UQ * u + UQ)
                if s in at_ring:
                    r = at_ring[s]
                    bank = ring[r % RB]
                    if r >= RB:
                        before = ringed[r - RB]
                        if before[0] == "out":
                            pe.wait_ge(x2_ready, U * before[2] + before[1] + 1)
                        else:
                            pe.wait_ge(ring_free, freed[r - RB])
                if kind in WIDE:
                    w = fills[s][0]
                    wide = pa[w.place]
                    if w.before:
                        pe.wait_ge(wide_free, w.before)
                if kind == "ctxT":
                    pe.wait_ge(cx_in, 48)
                    for b in range(NB):
                        nc.tensor.transpose(wide[0:CK, b * P:(b + 1) * P], cx[:, b, :], idf[:])
                    nc.tensor.transpose(wide[0:CK, 256:256 + NB * KL], cx[0:NB * KL, 2, :],
                                        idf[0:NB * KL, 0:NB * KL]).then_inc(wide_full, 1)
                elif kind == "xT":
                    pe.wait_ge(xn_ready, TB * (u + 1))
                    for t in range(TB):
                        last = nc.tensor.transpose(wide[:, t * P:(t + 1) * P], xn[:, u * TB + t, :], idf[:])
                    last.then_inc(wide_full, 1)
                elif kind in ("k", "v"):
                    pe.wait_ge(wk_in if kind == "k" else wv_in, 16)
                    pe.wait_ge(wide_free, fills[("ctxT", 0, 0)][0].turn)
                    pe.wait_ge(cT_ready, 2)
                    w = wk if kind == "k" else wv
                    for b in range(NB):
                        nc.tensor.matmul(bank[:, b * P:(b + 1) * P], cxT[:, b * P:(b + 1) * P], w[:], start=True, stop=True)
                    for b in range(NB):
                        last = nc.tensor.matmul(bank[:, 256 + b * P:256 + (b + 1) * P],
                                                cxL[:, b].rearrange("c j k -> c (j k)"), w[:], start=True, stop=True)
                    last.then_inc(ring_full, 1)
                elif kind == "q":
                    pe.wait_ge(wq_in, 16)
                    pe.wait_ge(wide_free, fills[("xT", b, 0)][0].turn)
                    for t in range(UT):
                        last = nc.tensor.matmul(bank[:, t * P:(t + 1) * P],
                                                xnT[:, (UT * u + t) * P:(UT * u + t + 1) * P], wq[:], start=True, stop=True)
                    last.then_inc(ring_full, 1)
                elif kind == "kT":
                    pe.wait_ge(ks_ready[u], 2 * NC + 2)
                    for h in range(H):
                        last = nc.tensor.transpose(wide[:, 64 * h:64 * h + 64].bitcast(BF16), ks[:, u * PR + h // 2, h % 2, :],
                                                   idb[:])
                    last.then_inc(wide_full, 1)
                elif kind == "kLT":
                    pe.wait_ge(ksL_ready, NC)
                    pe.wait_ge(ones_ready, 2 * J)
                    for m in range(NB * G):
                        last = nc.tensor.transpose(bank[:, 64 * m:64 * m + 64].bitcast(BF16), ksL[:, m, :], idb[:])
                    last.then_inc(ring_full, 1)
                elif kind == "qT":
                    pe.wait_ge(qs_base, 3 * (u + 1))
                    pe.wait_ge(qs_equal, 3 * (u + 1))
                    pe.wait_ge(cleared_qs, u + 1)
                    for t in range(UT):
                        for r2 in range(PR):
                            at = 64 * (PR * t + r2)
                            last = nc.tensor.transpose(wide[:, at:at + 64].bitcast(BF16),
                                                       qs[:, UT * u + t, r2].rearrange("p c m -> p (c m)"), idb[:])
                    last.then_inc(wide_full, 1)
                elif kind == "max":
                    t, part = UT * u + n // 5, n % 5
                    if n == 0:
                        pe.wait_ge(wide_free, max(fills[("qT", u, 0)][0].turn, fills[("kT", b, 0)][0].turn if b or u else 0))
                        pe.wait_ge(ring_free, freed[at_ring[("kLT", 0, 0)]])
                    for r2 in ((2 * part, 2 * part + 1) if part < 4 else range(PR)):
                        w = qT[0:STK, r2, t * P:(t + 1) * P]
                        if part < 4:
                            o = bank[:, 256 * (r2 % 2):256 * (r2 % 2) + 256]
                            m = kT[0:STK, b, 2 * r2:2 * r2 + 2, :].rearrange("p h k -> p (h k)")
                        else:
                            o = bank[:, 64 * r2:64 * r2 + 64]
                            m = kLT[0:STK, b, r2 // 2, 64 * (r2 % 2):64 * (r2 % 2) + 64]
                        last = nc.tensor.matmul(o, w, m, start=True, stop=True)
                    last.then_inc(ring_full, 1)
                elif kind == "shift":
                    pe.wait_ge(shift_ready, u + 1)
                    for t in range(UT):
                        last = nc.tensor.transpose(wide[:, 64 * t:64 * t + 64].bitcast(BF16), ms[:, UT * u + t, :], idb[:])
                    last.then_inc(wide_full, 1)
                elif kind == "score":
                    if n == 0:
                        pe.wait_ge(wide_free, fills[("shift", u, 0)][0].turn)
                    if n == 5:
                        pe.wait_ge(shift_spread, u + 1)
                    w, quarter = fills[s][0]
                    g, c = n // 5, n % 5
                    if quarter == 0 and w.before:
                        pe.wait_ge(wide_free, w.before)
                    o = pa[w.place][:, UQ * quarter:UQ * quarter + UQ]
                    if c < J:
                        h = J * g + c
                        last = nc.tensor.matmul(o, kT[:, b, h, :], qT[:, h // 2, uq], start=True, stop=True)
                    else:
                        for half in range(2):
                            last = nc.tensor.matmul(o[64 * half:64 * half + 64, :],
                                                    kLT[:, b, g, 64 * half:64 * half + 64],
                                                    qT[:, 2 * g + half, uq], start=True, stop=True)
                    if quarter == 3:
                        last.then_inc(wide_full, 1)
                elif kind == "pv":
                    pe.wait_ge(wide_free, wide_of(u, n))
                    pe.wait_ge(v_ready, 3 + 2 * J)
                    if pvs[0]:
                        pe.wait_ge(oT_ready, pvs[0])
                    c0 = 5 * (G * u + n)
                    pieces = [pt[:, ((c0 + c) // 4) % NPT, (c0 + c) % 4, :] for c in range(5)]
                    o = pv
                    nc.tensor.matmul(o[:, 0:UQ], vL[:, b, n].rearrange("p j m -> p (j m)"), pieces[4],
                                     start=True, stop=False, skip_group_check=True)
                    for j in range(J):
                        last = nc.tensor.matmul(o[32 * j:32 * j + 32, 0:UQ], v[:, b, J * n + j, :], pieces[j],
                                                start=False, stop=True, skip_group_check=True)
                    last.then_inc(pv_full, 1)
                    pvs[0] += 1
                elif kind == "turn":
                    pe.wait_ge(oT_ready, G * u + n + 1)
                    for t in range(UT):
                        last = nc.tensor.transpose(bank[:, t * P:(t + 1) * P], oT[:, (G * u + n) % 2, t * P:(t + 1) * P], idf[:])
                    last.then_inc(ring_full, 1)
                elif kind == "back":
                    if n == 0:
                        pe.wait_ge(ring_free, freed[at_ring[("turn", u, G - 1)]])
                    for t in range(UT):
                        src = xn[:, UT * u + t, :] if n else ot[:, u % 2, t, :]
                        last = nc.tensor.transpose(bank[:, t * P:(t + 1) * P], src, idf[:])
                    last.then_inc(ring_full, 1)
                elif kind == "check":
                    pe.wait_ge(tally_ready, 1)
                    nc.tensor.matmul(bank[:, 0:1], ones[:], finec[:], start=True, stop=True).then_inc(ring_full, 1)
                elif kind == "out":
                    pe.wait_ge(ring_free, freed[at_ring[("back", u, n)]])
                    pe.wait_ge(wo_in, 16)
                    for t in range(UT):
                        last = nc.tensor.matmul(bank[:, t * C:(t + 1) * C], onT[:, u % 2, t * P:(t + 1) * P], wo[:],
                                                start=True, stop=True)
                    last.then_inc(ring_full, 1)
                elif kind == "normedT":
                    pe.wait_ge(xn2_ready, UT * (U * n + u + 1))
                    for t in range(UT):
                        last = nc.tensor.transpose(bank[:, t * P:(t + 1) * P], xn2[:, UT * u + t, :], idf[:])
                    last.then_inc(ring_full, 1)
                elif kind == "route":
                    pe.wait_ge(ring_free, freed[at_ring[("normedT", u, n)]])
                    pe.wait_ge(gw_in, 16)
                    for t in range(UT):
                        last = nc.tensor.matmul(bank[:, t * E:(t + 1) * E], xn2T[:, u % 2, t * P:(t + 1) * P], gw[:],
                                                start=True, stop=True)
                    last.then_inc(ring_full, 1)

            for s in steps:
                step(s)
            pe.wait_ge(ring_free, odd_known)
            with pe.If(pe.value_load(odd[0:1, 0:1], min_val=0, max_val=P * P) > 0):
                pe.wait_ge(oT_ready, U * G)
                pe.wait_ge(ring_free, last_free)
                pe.wait_ge(gp_mean, 1)
                for b in range(NB):
                    with pe.Fori(0, H) as h:
                        pe.wait_ge(gp_dve, h * GD + (b * H * GD + 4))
                        for n, at, src in ((0, 0, xnT[:, b * NQ:(b + 1) * NQ]), (1, NQ, cxT[:, b * P:(b + 1) * P]),
                                           (1, NQ + P, cxL[:, b, 0, 0:KL])):
                            width = src.shape[-1]
                            rows_ = slice(0, C if n == 0 else CK)
                            nc.tensor.matmul(pa[1][0:D, at:at + width], gw_[rows_, n, :], src, start=True, stop=False)
                            last = nc.tensor.matmul(pa[1][0:D, at:at + width], gb[:, n, :], gone[0:1, 0:width],
                                                    start=False, stop=True)
                        last.then_inc(gp_pe, 1)
                        pe.wait_ge(gp_act, h * GA + (b * H * GA + 1))
                        for t in range(TB):
                            last = nc.tensor.matmul(pa[0][:, 256 * t:256 * t + NK], gqk[:, t * P:(t + 1) * P], gqk[:, NQ:],
                                                    start=True, stop=True)
                        last.then_inc(gp_pe, 1)
                        pe.wait_ge(gp_dve, h * GD + (b * H * GD + 13))
                        for t in range(TB):
                            nc.tensor.transpose(pa[1][:, t * P:(t + 1) * P], gs[:, t, 0:P], idf[:])
                            last = nc.tensor.transpose(pa[1][0:KL, NQ + t * P:NQ + (t + 1) * P], gs[:, t, P:], idf[:])
                        last.then_inc(gp_pe, 1)
                        pe.wait_ge(gp_act, h * GA + (b * H * GA + 4))
                        vf = v[:].rearrange("p b h m -> p (b h m)")
                        vlf = vLf[:].rearrange("p b c -> p (b c)")
                        for t in range(TB):
                            nc.tensor.matmul(pv[:, t * D:(t + 1) * D], gpT[:, t * P:(t + 1) * P],
                                             vf[:, bass.ds(h * 32 + b * H * 32, D)], start=True, stop=False)
                            last = nc.tensor.matmul(pv[:, t * D:(t + 1) * D], gpT[0:KL, NQ + t * P:NQ + (t + 1) * P],
                                                    vlf[0:KL, bass.ds(h * D + b * C, D)], start=False, stop=True)
                        last.then_inc(gp_pe, 1)
                pe.wait_ge(gp_dve, NB * H * GD)
                pe.wait_ge(gp_link, 2)
                nc.tensor.matmul(pv[:, 0:1], gone[:, 0:P], gnc[:], start=True, stop=True)
                for b in range(NB):
                    nc.tensor.matmul(ring[0][:, b * C:(b + 1) * C], gmean, v[:, b, :, 0:D], start=True, stop=False)
                    last = nc.tensor.matmul(ring[0][:, b * C:(b + 1) * C], gmean[0:KL, :], vLf[0:KL, b, :],
                                            start=False, stop=True)
                last.then_inc(gp_mean, 1)
                pe.wait_ge(gp_link, 4)
                for s in again:
                    step(s)
                pe.wait_ge(oh_ready, 2 * U)
            pe.wait_ge(oT_ready, U * G)
            pe.wait_ge(consts2, 8)
            pe.wait_ge(oh_ready, U)
            flat = oh[:].rearrange("p t e -> p (t e)")
            nc.tensor.matmul(pv[:, 0:T * E], tri[:], flat, start=True, stop=False, skip_group_check=True)
            for d in range(1, T):
                nc.tensor.matmul(pv[:, d * E:T * E], ones[:], flat[:, 0:(T - d) * E], start=False, stop=True,
                                 skip_group_check=True)
            for t in range(T):
                last = nc.tensor.matmul(pv[:, T * E:T * E + E], ones[:], flat[:, t * E:(t + 1) * E], start=False, stop=True,
                                        skip_group_check=True)
            last.then_inc(rank_ps, 1)
            def stay_warm(n):
                for _ in range(n):
                    nc.tensor.matmul(pa[0][:, 0:512], idb[:], kT[:, 0, 0:4].rearrange("p h k -> p (h k)"), start=True, stop=True)

            pe.wait_ge(b1_in, 16)
            pe.wait_ge(ring_free, last_free)
            nc.tensor.transpose(ring[0][:, 0:E * FC], b1r[:], idf[0:E * FC, 0:E * FC]).then_inc(b1_ps, 1)
            stay_warm(WARM[0])
            pe.wait_ge(olo_ready, T + 2)
            for t in range(T):
                last = nc.tensor.matmul(ring[1][:, 0:3 * NBLK], olo[:, t, :], rhs[:, t].rearrange("p a i -> p (a i)"),
                                        start=(t == 0), stop=(t == T - 1))
            last.then_inc(inv_ps, 1)
            stay_warm(WARM[1])
            pe.wait_ge(index_ready, 1)
            pe.wait_ge(b1_ready, 1)
            pe.wait_ge(w2_in, 16 * E)
            pe.wait_ge(expert_ready, 1)

            def turn_rows(i):
                pe.wait_ge(gathered[i], 16)
                if i >= 2:
                    pe.wait_ge(xgT_ready, i - 1)
                nc.tensor.transpose(turned[i % 2][:, 0:P], xg[:, i, 0:C], idf[:]).then_inc(xgT_ps, 1)

            def first_half(i):
                pe.wait_ge(xgT_ready, i + 1)
                pe.wait_ge(w1c_ready, i + 1)
                if i >= 2:
                    pe.wait_ge(hb_ready, i - 1)
                for c in range(FC):
                    last = nc.tensor.matmul(pa[i % 2][:, c * P:(c + 1) * P], w1c[:, i % 2, c * P:(c + 1) * P], xgT[:, i % 2],
                                            start=True, stop=True)
                last.then_inc(h_ps, 1)

            w2f = w2[:].rearrange("p e c n -> p (e c n)")
            turn_rows(0)
            turn_rows(1)
            first_half(0)
            for i in range(NBLK):
                if i + 2 < NBLK:
                    turn_rows(i + 2)
                e = nc.tensor.value_load(be[0:1, i:i + 1], min_val=0, max_val=E - 1)
                if i + 1 < NBLK:
                    first_half(i + 1)
                pe.wait_ge(hidden_ready, i + 1)
                if i >= 2:
                    pe.wait_ge(y_read, i - 1)
                for c in range(FC):
                    last = nc.tensor.matmul(ring[i % 2][:, 0:C], hT[:, i % 2, c * P:(c + 1) * P],
                                            w2f[:, bass.ds(e * (FC * C) + c * C, C)], start=(c == 0), stop=(c == FC - 1))
                last.then_inc(y_ps, 1)


NAMES = ["x", "ctx_768", "g_xattn", "g_ffn", "L0_xattn_Wq", "L0_xattn_bq", "L0_xattn_Wk", "L0_xattn_bk",
         "L0_xattn_Wv", "L0_xattn_bv", "L0_xattn_Wo", "L0_xattn_bo", "L0_ffn_gate_w", "L0_ffn_w1",
         "L0_ffn_b1", "L0_ffn_w2", "L0_ffn_b2"]


def kernel(**inputs):
    import numpy as np
    import concourse.bacc as bacc
    from concourse.bass_utils import run_bass_kernel_spmd

    nc = bacc.Bacc("TRN2", target_bir_lowering=False, num_devices=1)
    arrays, a = {}, {}
    for name in NAMES:
        arr = np.ascontiguousarray(inputs[name])
        arrays[f"in_{name}"] = arr
        a[name] = nc.dram_tensor(f"in_{name}", arr.shape, mybir.dt.from_np(arr.dtype), kind="ExternalInput").ap()
    out = nc.dram_tensor("out_x", (NB, NQ, C), F32, kind="ExternalOutput").ap()
    program(nc, a, out)
    r = run_bass_kernel_spmd(nc, [arrays], core_ids=[0])
    return r.results[0]["out_x"]
```

```python
from contextlib import ExitStack

import concourse.bass as bass
from concourse import mybir

F32 = mybir.dt.float32
BF16 = mybir.dt.bfloat16
I32 = mybir.dt.int32
ALU = mybir.AluOpType
ACT = mybir.ActivationFunctionType
AX = mybir.AxisListType

P = 128
NB, NQ, C = 2, 512, 128
NK, CK = 154, 96
H, D = 16, 8
T = NB * NQ // P
TB = NQ // P
KL = NK - P
G, J = 4, 4
PR = H // 2
RB = 3
E, FF = 8, 512
FC = FF // P
NBLK = T + E - 1
ROW = 2 * C + 4
NPT = 6
STK = 96
NC = 6
KPART = (0, 1, 2, 0, 1, 0)
KW = NB * C + NB * C // 2
U, UT = 4, 2
UQ = UT * P
WARM = (13, 14)
AHEAD = 8
CH = (J + 1) * G
SCALE = float(D) ** -0.5
CLAMP = 1e4
LIMIT = 0.95 * CLAMP / SCALE
GD, GA, GP = 14, 4, 4
EPS = 1e-5


def plan():
    steps = [("warm", 0, PLAN["warm0"]), ("ctxT", 0, 0), ("xT", 0, 0), ("k", 0, 0), ("q", 0, 0), ("warm", 1, PLAN["warm1"]),
             ("kT", 0, 0), ("qT", 0, 0), ("kLT", 0, 0)]
    first = [("max", 0, k) for k in range(5 * UT)]
    first.insert(PLAN["xT1"], ("xT", 1, 0))
    first.append(("shift", 0, 0))
    first.insert(PLAN["q1"], ("q", 1, 0))
    first.insert(PLAN["warmat"], ("warm", 3, PLAN["warm3"]))
    steps += first
    at = {}

    def put(when, *step):
        at.setdefault(when, []).append(step)

    put(PLAN["qT1"], "qT", 1, 0)
    put(PLAN["v"], "v", 0, 0)
    for u in range(U):
        t0 = CH * u
        if u + 1 < U:
            put(t0 + CH + PLAN["spread"], "spread", u + 1, 0)
            for k in range(5 * UT):
                put(t0 + PLAN["max0"] + k * PLAN["maxn"] // 8, "max", u + 1, k)
            put(t0 + PLAN["shift"], "shift", u + 1, 0)
        if u + 2 < U:
            put(t0 + PLAN["q"], "q", u + 2, 0)
            put(t0 + PLAN["qT"], "qT", u + 2, 0)
        if u == 0:
            put(t0 + PLAN["kT"], "kT", 1, 0)
            put(t0 + PLAN["spread"], "spread", 0, 0)
        for g in range(G):
            full = 4 * ((5 * g + 4) // 4) + 3
            when = t0 + full + PLAN["pv"]
            put(when, "pv", u, g)
            put(when + PLAN["turn"], "turn", u, g)
        when += PLAN["turn"]
        for kind in ("back", "out", "norm", "normedT", "route"):
            if kind == "normedT" and u == U - 1:
                put(when, "check", u, 0)
            when += PLAN[kind]
            put(when, kind, u, 0)
            if kind == "out" and u == U - 1:
                put(when, "warm", 2, PLAN["warm2"])
    for n in range(max(at) + 1):
        if n < U * CH:
            steps.append(("score", n // CH, n % CH))
        steps += at.get(n, [])
    return steps


PLAN = {
    "max0": 1, "maxn": 12, "shift": 16, "spread": 3, "q": 3, "qT": 7, "kT": 4, "qT1": 1, "v": 0,
    "pv": 4, "turn": 4, "back": 5, "out": 4, "norm": 8, "normedT": 4, "route": 7,
    "xT1": 5, "norm1": 1, "q1": 12, "warmat": 11, "warm0": 11, "warm1": 10, "warm2": 2, "warm3": 3}
WIDE = ("ctxT", "xT", "kT", "qT", "shift")
RING = ("k", "q", "kLT", "v", "max", "turn", "back", "check", "out", "normedT", "route")


class Wide:

    def __init__(self, place, before):
        self.place, self.before, self.turn = place, before, None


def fillings(steps):
    last, count, open_, of = [0, 0], 0, None, {}
    held = [0, 0]

    def new():
        place = min((n for n in range(2) if open_ is None or n != open_[0].place), key=lambda n: held[n])
        return Wide(place, last[place])

    for s in steps:
        if s[0] in WIDE:
            w = new()
            count += 1
            w.turn = count
            last[w.place] = held[w.place] = count
            of[s] = [w]
        elif s[0] == "score":
            if open_ is None:
                open_ = [new(), 0]
                held[open_[0].place] = 10 ** 6
            of[s] = [(open_[0], open_[1])]
            open_[1] += 1
            if open_[1] == 4:
                count += 1
                open_[0].turn = count
                last[open_[0].place] = held[open_[0].place] = count
                open_ = None
    assert open_ is None
    return of


def program(nc, a, out):
    ctx = ExitStack()
    with ctx:
        def sb(name, shape, dt=F32):
            return ctx.enter_context(nc.sbuf_tensor(name, shape, dt))

        def sem(name):
            return ctx.enter_context(nc.semaphore(name))

        x = sb("x_sb", [P, T, C])
        cx = sb("context", [P, 3, CK])
        wq = sb("wq", [C, C]); wk = sb("wk", [CK, C]); wv = sb("wv", [CK, C]); wo = sb("wo", [C, C])
        bias = sb("bias_rows", [P, 4, C])
        gates = sb("gates", [P, 2]); gw = sb("gate_w", [C, E])
        w1 = sb("w1", [C, E, FF]); w2 = sb("w2", [P, E, FC, C])
        b1r = sb("b1_rows", [E * FC, P]); b2 = sb("b2", [P, E, C])

        zf = sb("zeros_f", [P, P]); zb = sb("zeros_b", [P, P], BF16)
        idf = sb("ident_f", [P, P]); idb = sb("ident_b", [P, P], BF16)
        lmask = sb("left_mask", [P, J])
        mhalf = sb("minus_half", [P, T]); warm = sb("warm", [P, 2])
        iota_i = sb("iota_i", [P, P], I32); io = sb("iota", [P, P]); iob = sb("iota_b", [P, P], BF16)
        ip_i = sb("iota_p_i", [P, 1], I32); ip = sb("iota_p", [P, 1])
        rev = sb("rev", [P, E]); first = sb("first", [P, E]); one8 = sb("ones8", [P, E])
        hi128 = sb("multiples_of_128", [P, NBLK + 1])
        tri = sb("before", [P, P], BF16); ones = sb("ones", [P, P], BF16)

        st = sb("bn_stats", [P, T, 6]); mv = sb("mean_var", [P, T, 2])
        ve = sb("var_eps", [P, T]); rstd = sb("rstd", [P, T])
        xn = sb("x_normed", [P, T, C]); xnT = sb("x_normed_T", [P, T * P])
        cxT = sb("context_T", [CK, NB * P])
        cxL = sb("context_left_T", [CK, NB, J, 32])
        q = sb("q_f", [P, 2, UT, C]); qr = sb("q_rest", [P, 2, UT, C])
        qs = sb("q_stack", [P, T, PR, 8, 16], BF16)
        qT = sb("q_stack_T", [P, PR, T * P], BF16)
        k = sb("k_f", [P, KW]); kr = sb("k_rest", [P, KW]); kp = sb("k_parts", [P, 3, KW], BF16)
        kl = sb("k_left_f", [P, NB, C])
        ks = sb("k_stack", [P, NB * PR, 2, P], BF16); ksL = sb("k_left_stack", [P, NB * G, P], BF16)
        kT = sb("k_stack_T", [P, NB, H, P], BF16); kLT = sb("k_left_stack_T", [P, NB, G, P], BF16)
        v = sb("v_main", [P, NB, H, 32]); vL = sb("v_left", [P, NB, G, J, 32]); vLf = sb("v_left_f", [P, NB, C])

        mm = sb("max_main", [P, T, H]); ml = sb("max_left", [P, T, H]); mx = sb("max", [P, T, H])
        ms = sb("shift_parts", [P, T, P], BF16)
        pt = sb("probs_T", [P, NPT, 4, UQ])
        oT = sb("o_T", [P, 2, UQ]); ot = sb("o_tokens", [P, 2, UT, C]); onT = sb("o_normed_T", [P, 2, UQ])
        rcs = sb("sum_reciprocals", [P, U * G * UT * J])
        fine = sb("fine", [P, T * H]); finec = sb("fine_count", [P, 1], BF16)
        odd = sb("odd", [P, 1], I32)
        tg = sb("tanh_gates", [P, 2]); xb = sb("x_plus_bias", [P, T, C])

        row = sb("row", [P, T, ROW])
        xn2, x2 = row[:, :, 0:C], row[:, :, C:2 * C]
        rows = nc.dram_tensor("rows", (T * P, ROW), F32, kind="Internal").ap()
        st2 = sb("bn_stats2", [P, T, 6]); mv2 = sb("mean_var2", [P, T, 2])
        ve2 = sb("var_eps2", [P, T]); rstd2 = sb("rstd2", [P, T])
        xn2T = sb("x2_normed_T", [P, 2, UQ])
        lmax = sb("logit_max", [P, T]); ld = sb("logit_diff", [P, T, E]); le = sb("logit_exp", [P, T, E])
        ls = sb("exp_sum", [P, T]); lr = sb("exp_sum_recip", [P, T])
        eq = sb("is_max", [P, T, E]); em = sb("best", [P, T]); oh = sb("one_hot", [P, T, E], BF16)

        nbk = sb("blocks_gt", [P, E, T]); nb = sb("blocks", [P, E])
        base = sb("first_block", [P, E]); end = sb("block_end", [P, E])
        sl = sb("slot_of_expert", [P, T, E]); slot = sb("slot", [P, T])
        ge = sb("block_ge", [P, T, NBLK + 1]); hs = sb("block_number", [P, T]); lo = sb("slot_in_block", [P, T])
        olo = sb("slot_one_hot", [P, T, P], BF16); rhs = sb("block_one_hot", [P, T, 3, NBLK], BF16)
        tokf = sb("slot_token", [P, NBLK]); gi = sb("gather_index", [P, NBLK], I32)
        sif = sb("scatter_f", [P, NBLK]); si = sb("scatter_index", [P, NBLK], I32)
        bge = sb("block_past", [P, NBLK, E]); bef = sb("block_expert_f", [P, NBLK])
        be = sb("block_expert", [P, NBLK], I32); ub = sb("blocks_used", [P, 1], I32)

        b1 = sb("b1_T", [P, E * FC]); xgT = sb("gathered_T", [P, 2, P])
        xg = qT[:].rearrange("p r q -> p (r q)").bitcast(F32)[:, 0:NBLK * ROW].rearrange("p (i c) -> p i c", i=NBLK)
        old = qs[:].rearrange("p t r c m -> p (t r c m)").bitcast(F32)
        w1c, hb, hT = (old[:, 2 * FF * n:2 * FF * (n + 1)].rearrange("p (s f) -> p s f", s=2) for n in range(3))
        yo = old[:, 6 * FF:7 * FF].rearrange("p (s f) -> p s f", s=4)
        yb = old[:, 7 * FF:7 * FF + 2 * C].rearrange("p (s f) -> p s f", s=2)

        flat = pt[:].rearrange("p n c q -> p n (c q)")
        gs, gok = pt[:, 0, :, 0:NK], pt[:, 1, :, 0:NK]
        gpT = flat[:, 2]
        gone, gmean = flat[:, 3, 0:NQ], flat[:, 4, 0:P]
        gqk = flat[0:D, 5, 0:NQ + NK]
        gw_ = sb("head_weights", [P, 2, D]); gb = sb("head_biases", [1, 2, D])
        gm = sb("general_max", [P, TB]); gr = sb("general_sum", [P, TB])
        gn = sb("numbers", [P, NB * H]); gnc = sb("numbers_count", [P, 1]); others = sb("others", [P, 1], I32)

        ring = [ctx.enter_context(nc.psum_tensor(f"ring{i}", [P, 512], F32)) for i in range(RB)]
        pa = [ctx.enter_context(nc.psum_tensor(f"wide{i}", [P, 1024], F32)) for i in range(2)]
        pv = ctx.enter_context(nc.psum_tensor("pv", [P, 512], F32))
        turned = [pv, ring[2]]

        x_in = [sem(f"x_in{i}") for i in range(NB)]; cx_in = sem("cx_in"); gates_in = sem("gates_in")
        wq_in = sem("wq_in"); wk_in = sem("wk_in"); wv_in = sem("wv_in"); wo_in = sem("wo_in")
        bq_in = sem("bq_in"); bk_in = sem("bk_in"); bv_in = sem("bv_in"); bo_in = sem("bo_in")
        gw_in = sem("gw_in"); w1_in = sem("w1_in"); w2_in = sem("w2_in"); b1_in = sem("b1_in"); b2_in = sem("b2_in")
        zeros = sem("zeros"); ident = sem("ident"); mask_step = sem("mask_step"); act_warm = sem("act_warm")
        ones_ready = sem("ones_ready"); iotas = sem("iotas"); consts2 = sem("consts2"); gates_ready = sem("gates_ready")
        cleared_cx = sem("cleared_cx"); cleared_half = sem("cleared_half"); cleared_ksL = sem("cleared_ksL")
        cleared_ks = sem("cleared_ks"); cleared_qs = sem("cleared_qs"); cleared_v = sem("cleared_v")
        cleared_ms = sem("cleared_ms"); cleared_row = sem("cleared_row")
        dv = sem("dve_chain"); pl = sem("pool_chain")
        aggr = sem("aggr"); rstd_ready = sem("rstd_ready"); xn_ready = sem("xn_ready"); cT_ready = sem("cT_ready")
        qs_base = sem("qs_base"); qs_equal = sem("qs_equal"); qT_begun = sem("qT_begun"); kparts_ready = sem("kparts_ready")
        ks_ready = [sem(f"ks_ready{b}") for b in range(NB)]; ksL_ready = sem("ksL_ready"); v_ready = sem("v_ready")
        ring_full = sem("ring_full"); ring_free = sem("ring_free")
        wide_full = sem("wide_full"); wide_free = sem("wide_free"); pv_full = sem("pv_full"); oT_ready = sem("oT_ready")
        shift_ready = sem("shift_ready"); shift_spread = sem("shift_spread"); tally_ready = sem("tally_ready")
        xb_ready = sem("xb_ready"); x2_ready = sem("x2_ready")
        aggr2 = sem("aggr2"); rstd2_ready = sem("rstd2_ready"); xn2_ready = sem("xn2_ready")
        le_ready = sem("le_ready"); weight_ready = sem("weight_ready"); rows_out = sem("rows_out")
        oh_ready = sem("oh_ready"); rank_ps = sem("rank_ps"); olo_ready = sem("olo_ready"); inv_ps = sem("inv_ps")
        index_ready = sem("index_ready"); expert_ready = sem("expert_ready")
        gp_dve = sem("general_dve"); gp_pe = sem("general_pe"); gp_act = sem("general_act")
        gp_link = sem("general_link"); gp_mean = sem("general_mean"); gp_out = sem("general_out")
        b1_ps = sem("b1_ps"); b1_ready = sem("b1_ready"); gathered = [sem(f"gathered{i}") for i in range(NBLK)]
        xgT_ps = sem("xgT_ps"); xgT_ready = sem("xgT_ready"); w1c_ready = sem("w1c_ready")
        h_ps = sem("h_ps"); hb_ready = sem("hb_ready"); hidden_ready = sem("hidden_ready")
        y_ps = sem("y_ps"); y_read = sem("y_read"); yo_ready = sem("yo_ready")
        scattered = [sem(f"scattered{i}") for i in range(4)]

        steps = plan()
        again = [(kind, u, 1) for u in range(U) for kind in ("back", "out", "norm", "normedT", "route")]
        ringed = [s for s in steps + again if s[0] in RING]
        fills = fillings(steps)
        exps = {}
        for s in steps:
            if s[0] == "score" and fills[s][0][1] == 3:
                exps[fills[s][0][0]] = len(exps)
        turn_of = {n: w.turn for w, n in exps.items()}
        at_ring = {s: n for n, s in enumerate(ringed)}
        freed = [sum(x[0] != "out" for x in ringed[:n + 1]) for n in range(len(ringed))]

        odd_known = freed[at_ring[("check", U - 1, 0)]]
        last_free = freed[at_ring[steps[-1]]]

        def wide_of(u, g):
            return turn_of[((J + 1) * (G * u + g) + J) // 4]

        def blocks_used(eng):
            eng.wait_ge(expert_ready, 2)
            return eng.value_load(ub[0:1, 0:1], min_val=T, max_val=NBLK)

        def for_block(eng, used, i, work):
            if i < T:
                work(i)
            elif i < NBLK:
                with eng.If(used > i):
                    work(i)

        block = ctx.enter_context(nc.Block())

        def stack_k(copy, b, c):
            for par in range(2):
                src = kp[:, KPART[c], b * C:(b + 1) * C].rearrange("p (n m) -> p n m", m=2 * D)
                own = slice(D * par, D * par + D)
                o = ks[:, b * PR:(b + 1) * PR, par, 16 * c:16 * c + 16]
                copy(o[:, :, own], src[:, :, own]).then_inc(ks_ready[b], 1)

        @block.sync
        def _(sp):
            xv = a["x"].rearrange("b (t p) c -> p (b t) c", p=P)
            sp.dma_start(x[:, 0:TB, :], xv[:, 0:TB, :]).then_inc(x_in[0], 16)
            sp.dma_start(wk[:], a["L0_xattn_Wk"]).then_inc(wk_in, 16)
            sp.dma_start(wq[:], a["L0_xattn_Wq"]).then_inc(wq_in, 16)
            sp.dma_start(bias[:, 1, :], a["L0_xattn_bk"].partition_broadcast(P)).then_inc(bk_in, 16)
            sp.dma_start(bias[:, 0, :], a["L0_xattn_bq"].partition_broadcast(P)).then_inc(bq_in, 16)
            sp.dma_start(x[:, TB:T, :], xv[:, TB:T, :]).then_inc(x_in[1], 16)
            sp.dma_start(wv[:], a["L0_xattn_Wv"]).then_inc(wv_in, 16)
            sp.dma_start(bias[:, 2, :], a["L0_xattn_bv"].partition_broadcast(P)).then_inc(bv_in, 16)
            sp.dma_start(gates[:, 0:1], a["g_xattn"].partition_broadcast(P)).then_inc(gates_in, 16)
            sp.dma_start(gates[:, 1:2], a["g_ffn"].partition_broadcast(P)).then_inc(gates_in, 16)
            sp.dma_start(bias[:, 3, :], a["L0_xattn_bo"].partition_broadcast(P)).then_inc(bo_in, 16)
            sp.dma_start(wo[:], a["L0_xattn_Wo"]).then_inc(wo_in, 16)
            sp.dma_start(gw[:], a["L0_ffn_gate_w"]).then_inc(gw_in, 16)
            sp.dma_start(b1r[:], a["L0_ffn_b1"].rearrange("e (c p) -> (e c) p", p=P)).then_inc(b1_in, 16)
            sp.dma_start(b2[:], a["L0_ffn_b2"].partition_broadcast(P)).then_inc(b2_in, 16)
            w1v = a["L0_ffn_w1"].rearrange("e d f -> d e f")
            w2v = a["L0_ffn_w2"].rearrange("e (c p) n -> p e c n", p=P)
            for h in range(2):
                es = slice(h * E // 2, (h + 1) * E // 2)
                sp.dma_start(w1[:, es, :], w1v[:, es, :]).then_inc(w1_in, 16)
                for e in range(h * E // 2, (h + 1) * E // 2):
                    sp.dma_start(w2[:, e], w2v[:, e]).then_inc(w2_in, 16)
            rv = rows.rearrange("(t p) c -> p t c", p=P)

            def rows_of(n):
                for u in range(U):
                    sp.wait_ge(weight_ready, U * n + u + 1)
                    sp.dma_start(rv[:, UT * u:UT * u + UT, :], row[:, UT * u:UT * u + UT, :]).then_inc(rows_out, 16)

            rows_of(0)
            sp.wait_ge(ring_free, odd_known)
            with sp.If(sp.value_load(odd[0:1, 0:1], min_val=0, max_val=P * P) > 0):
                sp.wait_ge(rows_out, 16 * U)
                rows_of(1)

        @block.scalar
        def _(act):
            cv = a["ctx_768"]
            act.dma_start(cx[:, 0:2, :], cv[:, 0:P, :].rearrange("b p c -> p b c")).then_inc(cx_in, 16)
            for b in range(NB):
                act.dma_start(cx[KL * b:KL * b + KL, 2, :], cv[b, P:NK, :]).then_inc(cx_in, 16)
            act.wait_ge(zeros, 1)
            nc.scalar.activation(warm[:, 0:1], zf[:, 0:1], ACT.Exp).then_inc(act_warm, 1)
            pvs = 0

            def exponentials(s):
                u = s[1]
                act.wait_ge(ring_free, freed[at_ring[s]])
                ts = slice(UT * u, UT * u + UT)
                nc.scalar.activation(le[:, ts, :], ld[:, ts, :], ACT.Exp).then_inc(le_ready, 1)

            for s in steps:
                kind, u, n = s
                if kind in WIDE:
                    w = fills[s][0]
                    bank = pa[w.place]
                    act.wait_ge(wide_full, w.turn)
                if kind == "ctxT":
                    nc.scalar.activation(cxT[:], bank[0:CK, 0:NB * P], ACT.Copy).then_inc(cT_ready, 1)
                    act.wait_ge(cleared_cx, 1)
                    src = bank[0:CK, 256:256 + NB * KL].rearrange("c (b k) -> c b k", b=NB)
                    for b in range(NB):
                        last = nc.scalar.activation(cxL[:, b, :, 0:KL], src[:, b].unsqueeze(1).to_broadcast([CK, J, KL]),
                                                    ACT.Copy)
                        if b == 0:
                            last.then_inc(cT_ready, 1)
                    last.then_inc(wide_free, 1)
                elif kind == "xT":
                    nc.scalar.activation(xnT[:, u * 512:(u + 1) * 512], bank[:, 0:512], ACT.Copy).then_inc(wide_free, 1)
                elif kind == "kT":
                    nc.scalar.activation(kT[:, u].rearrange("p h q -> p (h q)"), bank[:].bitcast(BF16),
                                         ACT.Copy).then_inc(wide_free, 1)
                elif kind == "qT":
                    src = bank[0:STK].bitcast(BF16).rearrange("p (t r q) -> p r t q", t=UT, r=PR)
                    o = qT[0:STK, :, UQ * u:UQ * u + UQ].rearrange("p r (t q) -> p r t q", t=UT)
                    for t in range(UT):
                        nc.scalar.activation(o[:, :, t, :], src[:, :, t, :], ACT.Copy
                                             ).then_inc(wide_free if t == UT - 1 else qT_begun, 1)
                elif kind == "shift":
                    src = bank[STK:P, 0:UQ // 2].bitcast(BF16).unsqueeze(1).to_broadcast([P - STK, 2, UQ])
                    nc.scalar.activation(qT[STK:P, 0:2, UQ * u:UQ * u + UQ], src, ACT.Copy).then_inc(wide_free, 1)
                elif kind == "k":
                    act.wait_ge(kparts_ready, 1)
                    act.wait_ge(cleared_ks, 1)
                    for c in range(NC):
                        if KPART[c] == 0:
                            stack_k(nc.scalar.copy, 0, c)
                elif kind == "q":
                    for c in (1, 2, 4):
                        act.wait_ge(qs_base, 3 * u + (1 if c < 4 else 2))
                        o = qs[:, UT * u:UT * u + UT].rearrange("p t r c m -> p (t r) c m")
                        nc.scalar.activation(o[:, :, c, :], o[:, :, 0 if c < 4 else 3, :], ACT.Copy).then_inc(qs_equal, 1)
                elif kind == "score":
                    w, quarter = fills[s][0]
                    if quarter == 3:
                        act.wait_ge(wide_full, w.turn)
                        done = exps[w]
                        if done >= NPT:
                            act.wait_ge(pv_full, (4 * (done - NPT) + 3) // 5 + 1)
                        nc.scalar.activation(pt[:, done % NPT].rearrange("p c q -> p (c q)"), pa[w.place][:],
                                             ACT.Exp, scale=SCALE).then_inc(wide_free, 1)
                elif kind == "route":
                    exponentials(s)
                elif kind == "pv":
                    act.wait_ge(pv_full, pvs + 1)
                    if pvs >= 2:
                        act.wait_ge(ring_full, at_ring[("turn", (pvs - 2) // G, (pvs - 2) % G)] + 1)
                    nc.scalar.activation(oT[:, pvs % 2, :], pv[:, 0:UQ], ACT.Copy).then_inc(oT_ready, 1)
                    pvs += 1
                if s == ("q", 1, 0):
                    act.wait_ge(gates_in, 32)
                    nc.scalar.activation(tg[:], gates[:], ACT.Tanh).then_inc(gates_ready, 1)
            act.wait_ge(ring_free, odd_known)
            with act.If(act.value_load(odd[0:1, 0:1], min_val=0, max_val=P * P) > 0):
                for b in range(NB):
                    with act.Fori(0, H) as h:
                        act.wait_ge(gp_pe, h * GP + (b * H * GP + 1))
                        nc.scalar.activation(gqk, pa[1][0:D, 0:NQ + NK], ACT.Copy).then_inc(gp_act, 1)
                        act.wait_ge(gp_dve, h * GD + (b * H * GD + 10))
                        nc.scalar.activation(gs, gs, ACT.Exp).then_inc(gp_act, 1)
                        act.wait_ge(gp_pe, h * GP + (b * H * GP + 3))
                        nc.scalar.activation(gpT[:, 0:NQ], pa[1][:, 0:NQ], ACT.Copy).then_inc(gp_act, 1)
                        nc.scalar.activation(gpT[0:KL, NQ:], pa[1][0:KL, NQ:], ACT.Copy).then_inc(gp_act, 1)
                for s in again:
                    if s[0] == "route":
                        exponentials(s)
            act.wait_ge(act_warm, 1)
            nc.scalar.activation(warm[:, 1:2], warm[:, 0:1], ACT.Gelu).then_inc(act_warm, 1)

            def copy_turned(i):
                act.wait_ge(xgT_ps, i + 1)
                if i >= 2:
                    act.wait_ge(h_ps, i - 1)
                nc.scalar.activation(xgT[:, i % 2], turned[i % 2][:, 0:P], ACT.Copy).then_inc(xgT_ready, 1)

            def gelu(i):
                act.wait_ge(hb_ready, i + 1)
                if i >= 2:
                    act.wait_ge(y_ps, i - 1)
                nc.scalar.activation(hT[:, i % 2], hb[:, i % 2], ACT.Gelu).then_inc(hidden_ready, 1)

            used = blocks_used(act)
            copy_turned(0)
            copy_turned(1)
            for i in range(NBLK):
                for_block(act, used, i + 2, copy_turned)
                for_block(act, used, i, gelu)

        @block.gpsimd
        def _(pool):
            nc.gpsimd.memset(zf[:], 0.0).then_inc(zeros, 1)
            nc.gpsimd.memset(zb[:], 0.0).then_inc(zeros, 1)
            pool.wait_ge(zeros, 2)
            for o, z in ((idf, zf), (idb, zb)):
                nc.gpsimd.affine_select(out=o[:], in_=z[:], compare_op=ALU.not_equal, fill=1.0, base=0,
                                        pattern=[[-1, P]], channel_multiplier=1).then_inc(ident, 1)
            nc.gpsimd.memset(cxL[:], 0.0).then_inc(cleared_cx, 1)
            nc.gpsimd.memset(mhalf[:], -0.5).then_inc(cleared_half, 1)
            nc.gpsimd.memset(lmask[:], 1.0).then_inc(mask_step, 1)
            pool.wait_ge(mask_step, 1)
            nc.gpsimd.affine_select(out=lmask[:], in_=lmask[:], compare_op=ALU.is_ge, fill=0.0, base=0,
                                    pattern=[[-32, J]], channel_multiplier=1).then_inc(mask_step, 1)
            pool.wait_ge(mask_step, 2)
            nc.gpsimd.affine_select(out=lmask[:], in_=lmask[:], compare_op=ALU.is_ge, fill=0.0, base=KL - 1,
                                    pattern=[[32, J]], channel_multiplier=-1).then_inc(mask_step, 1)
            nc.gpsimd.memset(ksL[:].rearrange("p n m -> p (n m)").bitcast(F32), 0.0).then_inc(cleared_ksL, 1)
            pool.wait_ge(cleared_ksL, 1)
            pool.wait_ge(mask_step, 3)
            for part in range(2):
                for j in range(J):
                    at = STK + H * part + j
                    o = ksL[:].rearrange("p (b g) m -> p b (g m)", b=NB)[:, :, at:at + (P + J) * (G - 1) + 1:P + J]
                    nc.gpsimd.tensor_copy(o, lmask[:, j:j + 1].unsqueeze(1).to_broadcast([P, NB, G])).then_inc(ones_ready, 1)

            def inverse_std(b):
                ts = slice(b * TB, (b + 1) * TB)
                pool.wait_ge(aggr, TB * (b + 1))
                nc.gpsimd.tensor_scalar(ve[:, ts], mv[:, ts, 1], EPS, None, ALU.add).then_inc(pl, 1)
                pool.wait_ge(pl, b + 1)
                pool.wait_ge(cleared_half, 1)
                nc.gpsimd.tensor_tensor(rstd[:, ts], ve[:, ts], mhalf[:, ts], ALU.pow).then_inc(rstd_ready, 1)

            inverse_std(0)
            nc.gpsimd.memset(qs[:, 0:UT, :, NC:, :], 0.0).then_inc(cleared_qs, 1)
            pool.wait_ge(kparts_ready, 3)
            for c in range(NC):
                nc.gpsimd.tensor_copy(ksL[:, :, 16 * c:16 * c + 16],
                                      kp[:, KPART[c], NB * C:].rearrange("p (n m) -> p n m", m=16)).then_inc(ksL_ready, 1)
            inverse_std(1)
            for u in range(1, U):
                nc.gpsimd.memset(qs[:, UT * u:UT * u + UT, :, NC:, :], 0.0).then_inc(cleared_qs, 1)
            nc.gpsimd.memset(ms[:].rearrange("p t m -> p (t m)").bitcast(F32), 0.0).then_inc(cleared_ms, 1)
            pool.wait_ge(cleared_ks, 1)
            for c in range(NC):
                stack_k(nc.gpsimd.tensor_copy, 1, c)
            nc.gpsimd.memset(v[:].rearrange("p b h m -> p (b h m)"), 0.0).then_inc(cleared_v, 1)
            nc.gpsimd.memset(vL[:].rearrange("p b g j m -> p (b g j m)"), 0.0).then_inc(cleared_v, 1)
            nc.gpsimd.memset(row[:, :, 2 * C:], 0.0).then_inc(cleared_row, 1)
            pool.wait_ge(gates_ready, 1)
            pool.wait_ge(bo_in, 16)
            nc.gpsimd.tensor_scalar(bias[:, 3, :], bias[:, 3, :], tg[:, 0:1], None, ALU.mult).then_inc(xb_ready, 1)
            pool.wait_ge(xb_ready, 1)
            for b in range(NB):
                pool.wait_ge(x_in[b], 16)
                nc.gpsimd.tensor_tensor(xb[:, b * TB:(b + 1) * TB, :], x[:, b * TB:(b + 1) * TB, :],
                                        bias[:, 3:4, :].to_broadcast([P, TB, C]), ALU.add).then_inc(xb_ready, 1)
            nc.gpsimd.iota(iota_i[:], [[1, P]], base=0, channel_multiplier=0).then_inc(iotas, 1)
            nc.gpsimd.iota(ip_i[:], [[0, 1]], base=0, channel_multiplier=1).then_inc(iotas, 1)
            nc.gpsimd.memset(ones[:], 1.0).then_inc(iotas, 1)
            nc.gpsimd.memset(one8[:], 1.0).then_inc(iotas, 1)
            pool.wait_ge(iotas, 4)
            nc.gpsimd.tensor_copy(io[:], iota_i[:]).then_inc(consts2, 1)
            nc.gpsimd.tensor_copy(iob[:], iota_i[:]).then_inc(consts2, 1)
            nc.gpsimd.memset(base[:, 0:1], 0.0).then_inc(consts2, 1)
            nc.gpsimd.tensor_copy(ip[:], ip_i[:]).then_inc(consts2, 1)
            nc.gpsimd.affine_select(out=tri[:], in_=ones[:], compare_op=ALU.is_gt, fill=0.0, base=0,
                                    pattern=[[1, P]], channel_multiplier=-1).then_inc(consts2, 1)
            pool.wait_ge(consts2, 5)
            nc.gpsimd.tensor_scalar(rev[:], io[:, 0:E], -1.0, float(E), ALU.mult, ALU.add).then_inc(consts2, 1)
            nc.gpsimd.tensor_scalar(first[:], io[:, 0:E], 0.0, 0.5, ALU.is_equal, ALU.mult).then_inc(consts2, 1)
            nc.gpsimd.tensor_scalar(hi128[:], io[:, 0:NBLK + 1], float(P), None, ALU.mult).then_inc(consts2, 1)
            def inverse_std2(u, n):
                ts = slice(UT * u, UT * u + UT)
                pool.wait_ge(aggr2, UT * (U * n + u + 1))
                nc.gpsimd.tensor_scalar(ve2[:, ts], mv2[:, ts, 1], EPS, None, ALU.add).then_inc(pl, 1)
                pool.wait_ge(pl, NB + U * n + u + 1)
                nc.gpsimd.tensor_tensor(rstd2[:, ts], ve2[:, ts], mhalf[:, ts], ALU.pow).then_inc(rstd2_ready, 1)

            for u in range(U):
                inverse_std2(u, 0)
            pool.wait_ge(ring_free, odd_known)
            with pool.If(pool.value_load(odd[0:1, 0:1], min_val=0, max_val=P * P) > 0):
                for u in range(U):
                    inverse_std2(u, 1)
                pool.wait_ge(oh_ready, 2 * U)
                pool.wait_ge(rows_out, 2 * 16 * U)
            ov = out.rearrange("b q c -> (b q) c")
            pool.wait_ge(rows_out, 16 * U)
            pool.wait_ge(index_ready, 1)
            def gather(i):
                nc.gpsimd.indirect_dma_start(xg[:, i, :], None, rows[:],
                                             bass.IndirectOffsetOnAxis(ap=gi[:, i:i + 1], axis=0)).then_inc(gathered[i], 16)

            def scatter(i):
                pool.wait_ge(yo_ready, i + 1)
                nc.gpsimd.indirect_dma_start(ov, bass.IndirectOffsetOnAxis(ap=si[:, i:i + 1], axis=0),
                                             yo[:, i % 4, :], None, bounds_check=T * P - 1,
                                             oob_is_err=False).then_inc(scattered[i % 4], 16)

            for i in range(AHEAD):
                gather(i)
            used = blocks_used(pool)
            pool.wait_ge(index_ready, 2)
            for i in range(NBLK):
                for_block(pool, used, i, scatter)
                for_block(pool, used, i + AHEAD, gather)
            for i in range(NBLK):
                for_block(pool, used, i, lambda i: pool.wait_ge(scattered[i % 4], 16 * (i // 4 + 1)))

        @block.vector
        def _(dve):
            chain, is_odd = {"sem": dv, "count": 0}, []

            def link(ins):
                chain["count"] += 1
                ins.then_inc(chain["sem"], 1)
                dve.wait_ge(chain["sem"], chain["count"])

            def statistics(b):
                dve.wait_ge(x_in[b], 16)
                for t in range(b * TB, (b + 1) * TB):
                    last = nc.vector.bn_stats(st[:, t, :], x[:, t, :])
                link(last)
                for t in range(b * TB, (b + 1) * TB):
                    nc.vector.bn_aggr(mv[:, t, :], st[:, t, :]).then_inc(aggr, 1)

            def normalise(b):
                dve.wait_ge(rstd_ready, b + 1)
                for t in range(b * TB, (b + 1) * TB):
                    nc.vector.tensor_scalar(xn[:, t, :], x[:, t, :], mv[:, t, 0:1], rstd[:, t:t + 1],
                                            ALU.subtract, ALU.mult).then_inc(xn_ready, 1)

            nc.vector.memset(ks[:].rearrange("p n a m -> p (n a m)").bitcast(F32), 0.0).then_inc(cleared_ks, 1)
            statistics(0)
            normalise(0)

            def step(s):
                kind, u, n = s
                if kind == "spread":
                    uq = slice(UQ * u, UQ * u + UQ)
                    dve.wait_ge(wide_free, fills[("shift", u, 0)][0].turn)
                    nc.vector.tensor_copy(qT[STK:P, 2:, uq], qT[STK:P, 0:1, uq].to_broadcast([P - STK, PR - 2, UQ])
                                          ).then_inc(shift_spread, 1)
                if s in at_ring:
                    r = at_ring[s]
                    bank = ring[r % RB]
                if kind == "k":
                    dve.wait_ge(bk_in, 16)
                    dve.wait_ge(mask_step, 3)
                    dve.wait_ge(ring_full, r + 1)
                    kb = bias[:, 1:2, :].to_broadcast([P, NB, C])
                    nc.vector.tensor_tensor(k[:, 0:NB * C].rearrange("p (b c) -> p b c", b=NB),
                                            bank[:, 0:NB * C].rearrange("p (b c) -> p b c", b=NB), kb, ALU.add)
                    nc.vector.tensor_tensor(kl[:], bank[:, NB * C:].rearrange("p (b c) -> p b c", b=NB), kb,
                                            ALU.add).then_inc(ring_free, 1)
                    dve.wait_ge(ring_free, freed[r])
                    klj = kl[:].rearrange("p b (g j m) -> p (b g) j m", j=J, m=D)
                    link(nc.vector.tensor_tensor(klj, klj, lmask[:].unsqueeze(1).unsqueeze(3).to_broadcast([P, NB * G, J, D]),
                                                 ALU.mult))
                    link(nc.vector.tensor_tensor(k[:, NB * C:].rearrange("p (n m) -> p n m", m=2 * D),
                                                 klj[:, :, 0:2].rearrange("p n j m -> p n (j m)"),
                                                 klj[:, :, 2:4].rearrange("p n j m -> p n (j m)"), ALU.add))
                    nc.vector.tensor_copy(kp[:, 0], k[:]).then_inc(kparts_ready, 1)
                    dve.wait_ge(kparts_ready, 1)
                    link(nc.vector.tensor_tensor(kr[:], k[:], kp[:, 0], ALU.subtract))
                    nc.vector.tensor_copy(kp[:, 1], kr[:]).then_inc(kparts_ready, 1)
                    dve.wait_ge(kparts_ready, 2)
                    nc.vector.tensor_tensor(kp[:, 2], kr[:], kp[:, 1], ALU.subtract).then_inc(kparts_ready, 1)
                    dve.wait_ge(kparts_ready, 3)
                    dve.wait_ge(cleared_ks, 1)
                    for c in range(NC):
                        if KPART[c]:
                            stack_k(nc.vector.tensor_copy, 0, c)
                    for b in range(NB):
                        for part in range(2):
                            at = STK + H * part
                            o = ks[:, b * PR:(b + 1) * PR].rearrange("p r a m -> p (r a m)")[:, at:at + (P + 1) * (H - 1) + 1:P + 1]
                            nc.vector.memset(o, 1.0).then_inc(ks_ready[b], 1)
                elif kind == "q":
                    if u == 0:
                        dve.wait_ge(bq_in, 16)
                    dve.wait_ge(ring_full, r + 1)
                    qu, qru = q[:, u % 2], qr[:, u % 2]
                    nc.vector.tensor_tensor(qu, bank[:, 0:UT * C].rearrange("p (t c) -> p t c", c=C),
                                            bias[:, 0:1, :].to_broadcast([P, UT, C]), ALU.add).then_inc(ring_free, 1)
                    dve.wait_ge(ring_free, freed[r])
                    qf = qu.rearrange("p t (r m) -> p (t r) m", m=16)
                    qrf = qru.rearrange("p t (r m) -> p (t r) m", m=16)
                    o = qs[:, UT * u:UT * u + UT].rearrange("p t r c m -> p (t r) c m")
                    nc.vector.tensor_copy(o[:, :, 0, :], qf).then_inc(qs_base, 1)
                    dve.wait_ge(qs_base, 3 * u + 1)
                    link(nc.vector.tensor_tensor(qrf, qf, o[:, :, 0, :], ALU.subtract))
                    nc.vector.tensor_copy(o[:, :, 3, :], qrf).then_inc(qs_base, 1)
                    dve.wait_ge(qs_base, 3 * u + 2)
                    nc.vector.tensor_tensor(o[:, :, 5, :], qrf, o[:, :, 3, :], ALU.subtract).then_inc(qs_base, 1)
                    if u == 0:
                        statistics(1)
                elif kind == "kLT":
                    dve.wait_ge(ring_full, r + 1)
                    nc.vector.tensor_copy(kLT[:].rearrange("p b g q -> p (b g q)"), bank[:].bitcast(BF16)).then_inc(ring_free, 1)
                elif kind == "v":
                    dve.wait_ge(ring_full, r + 1)
                    dve.wait_ge(bv_in, 16)
                    dve.wait_ge(cleared_v, 2)
                    for b in range(NB):
                        nc.vector.tensor_tensor(v[:, b, :, 0:D], bank[:, b * C:(b + 1) * C].rearrange("p (h d) -> p h d", d=D),
                                                bias[:, 2, :].rearrange("p (h d) -> p h d", d=D), ALU.add).then_inc(v_ready, 1)
                    nc.vector.memset(v[:, :, :, D:D + 1], 1.0).then_inc(v_ready, 1)
                    nc.vector.tensor_tensor(vLf[:], bank[:, 256:512].rearrange("p (b c) -> p b c", b=NB),
                                            bias[:, 2:3, :].to_broadcast([P, NB, C]), ALU.add).then_inc(ring_free, 1)
                    dve.wait_ge(ring_free, freed[r])
                    for j in range(J):
                        src = vLf[:].rearrange("p b (g m) -> p (b g) m", g=G)[:, :, 8 * j:8 * j + 8]
                        o = vL[:, :, :, j, :].rearrange("p b g m -> p (b g) m")
                        nc.vector.tensor_scalar(o[:, :, 0:D], src, lmask[:, j:j + 1], None, ALU.mult).then_inc(v_ready, 1)
                        nc.vector.tensor_copy(o[:, :, D], lmask[:, j:j + 1].to_broadcast([P, NB * G])).then_inc(v_ready, 1)
                elif kind == "max":
                    t, part = UT * u + n // 5, n % 5
                    dve.wait_ge(ring_full, r + 1)
                    if part < 4:
                        nc.vector.tensor_reduce(mm[:, t, 4 * part:4 * part + 4],
                                                bank[:].rearrange("p (h k) -> p h k", k=P), AX.X,
                                                ALU.max).then_inc(ring_free, 1)
                    else:
                        nc.vector.tensor_reduce(ml[:, t, :], bank[:].rearrange("p (h k) -> p h k", k=32)[:, :, 0:KL],
                                                AX.X, ALU.max).then_inc(ring_free, 1)
                    if s == ("max", 0, PLAN["norm1"]):
                        normalise(1)
                    if n == 5 * UT - 1:
                        ts = slice(UT * u, UT * u + UT)
                        dve.wait_ge(ring_free, freed[r])
                        dve.wait_ge(cleared_ms, 1)
                        link(nc.vector.tensor_tensor(mx[:, ts, :], mm[:, ts, :], ml[:, ts, :], ALU.max))
                        link(nc.vector.tensor_scalar(ms[:, ts, STK:STK + H], mx[:, ts, :], -1.0, None, ALU.mult))
                        nc.vector.scalar_tensor_tensor(ms[:, ts, STK + H:P], mx[:, ts, :], -1.0,
                                                       ms[:, ts, STK:STK + H], ALU.mult, ALU.subtract).then_inc(shift_ready, 1)
                        if u == U - 1:
                            mxf = mx[:].rearrange("p t h -> p (t h)")
                            link(nc.vector.tensor_scalar(fine[:], mxf, -LIMIT, None, ALU.is_ge))
                            link(nc.vector.scalar_tensor_tensor(fine[:], mxf, LIMIT, fine[:], ALU.is_le, ALU.mult))
                elif kind == "turn":
                    dve.wait_ge(ring_full, r + 1)
                    got = bank[:, 0:UT * P].rearrange("p (a m) -> p a m", m=32)
                    m = G * u + n
                    rc = rcs[:, UT * J * m:UT * J * m + UT * J].rearrange("p (t j) -> p t j", j=J)
                    link(nc.vector.reciprocal(rcs[:, UT * J * m:UT * J * m + UT * J], got[:, :, D]))
                    for t in range(UT):
                        last = nc.vector.tensor_tensor(
                            ot[:, u % 2, t, 32 * n:32 * n + 32].rearrange("p (j d) -> p j d", d=D),
                            got[:, J * t:J * t + J, 0:D], rc[:, t].unsqueeze(2).to_broadcast([P, J, D]), ALU.mult)
                    last.then_inc(ring_free, 1)
                elif kind == "check":
                    link(nc.vector.scalar_tensor_tensor(fine[:], rcs[:], 2.0, fine[:], ALU.is_le, ALU.mult))
                    with nc.allow_low_precision("whole numbers up to 128"):
                        nc.vector.tensor_reduce(finec[:], fine[:], AX.X, ALU.add).then_inc(tally_ready, 1)
                    dve.wait_ge(ring_full, r + 1)
                    nc.vector.tensor_scalar(odd[:], bank[:, 0:1], -1.0, float(P * P), ALU.mult, ALU.add).then_inc(ring_free, 1)
                elif kind == "back":
                    dve.wait_ge(ring_full, r + 1)
                    nc.vector.tensor_copy(onT[:, u % 2], bank[:, 0:UQ]).then_inc(ring_free, 1)
                elif kind == "out":
                    dve.wait_ge(ring_full, r + 1)
                    dve.wait_ge(xb_ready, 3)
                    ts = slice(UT * u, UT * u + UT)
                    nc.vector.scalar_tensor_tensor(x2[:, ts, :], bank[:, 0:UT * C].rearrange("p (t c) -> p t c", c=C),
                                                   tg[:, 0:1], xb[:, ts, :], ALU.mult, ALU.add).then_inc(x2_ready, 1)
                    dve.wait_ge(x2_ready, U * n + u + 1)
                    for t in range(UT * u, UT * u + UT):
                        last = nc.vector.bn_stats(st2[:, t, :], x2[:, t, :])
                    link(last)
                    for t in range(UT * u, UT * u + UT):
                        nc.vector.bn_aggr(mv2[:, t, :], st2[:, t, :]).then_inc(aggr2, 1)
                elif kind == "norm":
                    dve.wait_ge(rstd2_ready, U * n + u + 1)
                    for t in range(UT * u, UT * u + UT):
                        nc.vector.tensor_scalar(xn2[:, t, :], x2[:, t, :], mv2[:, t, 0:1], rstd2[:, t:t + 1],
                                                ALU.subtract, ALU.mult).then_inc(xn2_ready, 1)
                elif kind == "normedT":
                    dve.wait_ge(ring_full, r + 1)
                    nc.vector.tensor_copy(xn2T[:, u % 2], bank[:, 0:UQ]).then_inc(ring_free, 1)
                    if u == U - 1 and n == 0:
                        dve.wait_ge(ring_free, odd_known)
                        is_odd.append(dve.value_load(odd[0:1, 0:1], min_val=0, max_val=P * P))
                elif kind == "route":
                    ts = slice(UT * u, UT * u + UT)
                    dve.wait_ge(consts2, 8)
                    dve.wait_ge(ring_full, r + 1)
                    logits = bank[:, 0:UT * E].rearrange("p (t e) -> p t e", e=E)
                    link(nc.vector.tensor_reduce(lmax[:, ts], logits, AX.X, ALU.max))
                    nc.vector.tensor_tensor(ld[:, ts, :], logits, lmax[:, ts].unsqueeze(2).to_broadcast([P, UT, E]),
                                            ALU.subtract).then_inc(ring_free, 1)
                    dve.wait_ge(ring_free, freed[r])
                    link(nc.vector.scalar_tensor_tensor(eq[:, ts, :], ld[:, ts, :], 0.0,
                                                        rev[:].unsqueeze(1).to_broadcast([P, UT, E]), ALU.is_equal, ALU.mult))
                    link(nc.vector.tensor_tensor(eq[:, ts, :], eq[:, ts, :], first[:].unsqueeze(1).to_broadcast([P, UT, E]),
                                                 ALU.add))
                    link(nc.vector.tensor_reduce(em[:, ts], eq[:, ts, :], AX.X, ALU.max))
                    nc.vector.tensor_tensor(oh[:, ts, :], eq[:, ts, :], em[:, ts].unsqueeze(2).to_broadcast([P, UT, E]),
                                            ALU.is_equal).then_inc(oh_ready, 1)
                    dve.wait_ge(le_ready, U * n + u + 1)
                    link(nc.vector.tensor_reduce(ls[:, ts], le[:, ts, :], AX.X, ALU.add))
                    link(nc.vector.reciprocal(lr[:, ts], ls[:, ts]))
                    dve.wait_ge(cleared_row, 1)
                    nc.vector.tensor_scalar(row[:, ts, 2 * C], lr[:, ts], tg[:, 1:2], None, ALU.mult).then_inc(weight_ready, 1)

            for s in steps:
                step(s)
            with dve.If(is_odd[0] > 0):
                chain["sem"], chain["count"], before = gp_link, 0, chain["count"]
                link(nc.vector.memset(gone, 1.0))
                nc.vector.memset(gmean, 1.0 / NK).then_inc(gp_mean, 1)
                for b in range(NB):
                    with dve.Fori(0, H) as h:
                        done = [0]

                        def then(ins):
                            done[0] += 1
                            ins.then_inc(gp_dve, 1)
                            dve.wait_ge(gp_dve, h * GD + (b * H * GD + done[0]))

                        cols = bass.ds(h * D, D)
                        for n, w in ((0, wq), (1, wk)):
                            rows_ = slice(0, C if n == 0 else CK)
                            then(nc.vector.tensor_copy(gw_[rows_, n, :], w[rows_, cols]))
                            then(nc.vector.tensor_copy(gb[:, n, :], bias[0:1, n, cols]))
                        dve.wait_ge(gp_pe, h * GP + (b * H * GP + 2))
                        got = pa[0][:].rearrange("p (t k) -> p t k", t=TB)[:, :, 0:NK]
                        then(nc.vector.tensor_scalar(gs, got, SCALE, None, ALU.mult))
                        then(nc.vector.tensor_tensor(gok, gs, gs, ALU.is_equal))
                        then(nc.vector.tensor_reduce(gn[:, bass.ds(h + b * H, 1)], gok, AX.XY, ALU.add))
                        then(nc.vector.tensor_scalar(gs, gs, CLAMP, -CLAMP, ALU.min, ALU.max))
                        then(nc.vector.tensor_reduce(gm[:], gs, AX.X, ALU.max))
                        then(nc.vector.tensor_tensor(gs, gs, gm[:].unsqueeze(2).to_broadcast([P, TB, NK]), ALU.subtract))
                        dve.wait_ge(gp_act, h * GA + (b * H * GA + 2))
                        then(nc.vector.tensor_reduce(gm[:], gs, AX.X, ALU.add))
                        then(nc.vector.reciprocal(gr[:], gm[:]))
                        then(nc.vector.tensor_tensor(gs, gs, gr[:].unsqueeze(2).to_broadcast([P, TB, NK]), ALU.mult))
                        dve.wait_ge(gp_pe, h * GP + (b * H * GP + 4))
                        then(nc.vector.tensor_copy(xn[:, b * TB:(b + 1) * TB, cols],
                                                   pv[:, 0:TB * D].rearrange("p (t d) -> p t d", d=D)))
                        assert done[0] == GD
                link(nc.vector.tensor_reduce(gnc[:], gn[:], AX.X, ALU.add))
                dve.wait_ge(gp_mean, 2)
                link(nc.vector.tensor_scalar(others[:], pv[:, 0:1], -1.0, float(P * NB * H * TB * NK), ALU.mult, ALU.add))
                with dve.If(dve.value_load(others[0:1, 0:1], min_val=0, max_val=P * NB * H * TB * NK) > 0):
                    for t in range(T):
                        nc.vector.tensor_copy(xn[:, t, :], ring[0][:, (t // TB) * C:(t // TB) * C + C]).then_inc(gp_out, 1)
                    dve.wait_ge(gp_out, T)
                nc.vector.tensor_copy(gm[:, 0:1], gnc[:]).then_inc(gp_link, 1)
                chain["count"] += 1
                dve.wait_ge(rows_out, 16 * U)
                for s in again:
                    step(s)
                chain["sem"], chain["count"] = dv, before
            dve.wait_ge(rank_ps, 1)
            cnt = pv[:, T * E:T * E + E]
            dve.wait_ge(oh_ready, U)
            link(nc.vector.tensor_tensor(nbk[:], cnt.unsqueeze(2).to_broadcast([P, E, T]),
                                         hi128[:, 0:T].unsqueeze(1).to_broadcast([P, E, T]), ALU.is_gt))
            link(nc.vector.tensor_reduce(nb[:], nbk[:], AX.X, ALU.add))
            link(nc.vector.tensor_tensor_scan(base[:, 1:E], one8[:, 1:E], nb[:, 0:E - 1], 0.0, ALU.mult, ALU.add))
            link(nc.vector.scalar_tensor_tensor(sl[:], base[:].unsqueeze(1).to_broadcast([P, T, E]), float(P),
                                                pv[:, 0:T * E].rearrange("p (t e) -> p t e", e=E), ALU.mult, ALU.add))
            link(nc.vector.tensor_tensor(sl[:], sl[:], oh[:], ALU.mult))
            link(nc.vector.tensor_reduce(slot[:], sl[:], AX.X, ALU.add))
            link(nc.vector.tensor_tensor(ge[:], slot[:].unsqueeze(2).to_broadcast([P, T, NBLK + 1]),
                                    hi128[:].unsqueeze(1).to_broadcast([P, T, NBLK + 1]), ALU.is_ge))
            link(nc.vector.tensor_reduce(hs[:], ge[:, :, 1:], AX.X, ALU.add))
            link(nc.vector.scalar_tensor_tensor(lo[:], hs[:], -float(P), slot[:], ALU.mult, ALU.add))
            for t in range(T):
                nc.vector.tensor_scalar(olo[:, t, :], iob[:], lo[:, t:t + 1], None, ALU.is_equal).then_inc(olo_ready, 1)
            link(nc.vector.tensor_tensor(rhs[:, :, 0, :], ge[:, :, 0:NBLK], ge[:, :, 1:NBLK + 1], ALU.subtract))
            nc.vector.tensor_scalar(rhs[:, :, 1, :], rhs[:, :, 0, :], ip[:], None, ALU.mult).then_inc(olo_ready, 1)
            nc.vector.tensor_tensor(rhs[:, :, 2, :], rhs[:, :, 0, :], hi128[:, 0:T].unsqueeze(2).to_broadcast([P, T, NBLK]),
                                    ALU.mult).then_inc(olo_ready, 1)
            link(nc.vector.tensor_tensor(end[:], base[:], nb[:], ALU.add))
            link(nc.vector.tensor_tensor(bge[:], io[:, 0:NBLK].unsqueeze(2).to_broadcast([P, NBLK, E]),
                                         end[:].unsqueeze(1).to_broadcast([P, NBLK, E]), ALU.is_ge))
            link(nc.vector.tensor_reduce(bef[:], bge[:], AX.X, ALU.add))
            nc.vector.tensor_scalar(be[:], bef[:], float(E - 1), None, ALU.min).then_inc(expert_ready, 1)
            nc.vector.tensor_copy(ub[:], end[:, E - 1:E]).then_inc(expert_ready, 1)
            dve.wait_ge(inv_ps, 1)
            inv = ring[1][:, 0:3 * NBLK].rearrange("p (a i) -> p a i", a=3)
            link(nc.vector.tensor_reduce(tokf[:], inv[:, 1:3].rearrange("p a i -> p i a"), AX.X, ALU.add))
            nc.vector.tensor_copy(gi[:], tokf[:]).then_inc(index_ready, 1)
            link(nc.vector.scalar_tensor_tensor(sif[:], inv[:, 0], -float(2 * T * P), tokf[:], ALU.mult, ALU.add))
            nc.vector.tensor_scalar(si[:], sif[:], float(2 * T * P), None, ALU.add).then_inc(index_ready, 1)
            dve.wait_ge(b1_ps, 1)
            nc.vector.tensor_copy(b1[:], ring[0][:, 0:E * FC]).then_inc(b1_ready, 1)
            dve.wait_ge(b1_ready, 1)
            dve.wait_ge(w1_in, 32)
            dve.wait_ge(b2_in, 16)
            dve.wait_ge(expert_ready, 2)
            ex = {}

            def load_expert(i):
                if i < NBLK:
                    ex[i] = nc.vector.value_load(be[0:1, i:i + 1], min_val=0, max_val=E - 1)

            def weights(i):
                if i >= 2:
                    dve.wait_ge(h_ps, i - 1)
                src = w1[:].rearrange("d e f -> d (e f)")[:, bass.ds(ex[i] * FF, FF)]
                nc.vector.tensor_copy(w1c[:, i % 2, :], src).then_inc(w1c_ready, 1)

            def finish(i):
                dve.wait_ge(y_ps, i + 1)
                bsl = b2[:].rearrange("p e c -> p (e c)")[:, bass.ds(ex[i] * C, C)]
                nc.vector.tensor_tensor(yb[:, i % 2, :], ring[i % 2][:, 0:C], bsl, ALU.add).then_inc(y_read, 1)
                dve.wait_ge(y_read, i + 1)
                if i >= 4:
                    dve.wait_ge(scattered[i % 4], 16 * (i // 4))
                g = xg[:, i, :]
                nc.vector.scalar_tensor_tensor(yo[:, i % 4, :], yb[:, i % 2, :], g[:, 2 * C:2 * C + 1], g[:, C:2 * C],
                                               ALU.mult, ALU.add).then_inc(yo_ready, 1)

            def biased(i):
                dve.wait_ge(h_ps, i + 1)
                if i >= 2:
                    dve.wait_ge(hidden_ready, i - 1)
                bb = b1[:, bass.ds(ex[i] * FC, FC)].unsqueeze(2).to_broadcast([P, FC, P])
                nc.vector.tensor_tensor(hb[:, i % 2].rearrange("p (c q) -> p c q", c=FC),
                                        pa[i % 2][:, 0:FF].rearrange("p (c q) -> p c q", c=FC), bb, ALU.add).then_inc(hb_ready, 1)

            used = blocks_used(dve)
            load_expert(0)
            weights(0)
            load_expert(1)
            weights(1)
            for i in range(NBLK + 2):
                for_block(dve, used, i, biased)
                load_expert(i + 2)
                for_block(dve, used, i + 2, weights)
                if i >= 2:
                    for_block(dve, used, i - 2, finish)

        @block.tensor
        def _(pe):
            def stay_warm(where, n):
                for _ in range(n):
                    nc.tensor.matmul(where[:, 0:512], zb[:], zb[:].unsqueeze(1).to_broadcast([P, 4, P]), start=True, stop=True)

            pvs, is_odd = [0], []

            def step(s):
                kind, u, n = s
                b = u * UT // TB
                uq = slice(UQ * u, UQ * u + UQ)
                if s in at_ring:
                    r = at_ring[s]
                    bank = ring[r % RB]
                    if r >= RB:
                        before = ringed[r - RB]
                        if before[0] == "out":
                            pe.wait_ge(x2_ready, U * before[2] + before[1] + 1)
                        else:
                            pe.wait_ge(ring_free, freed[r - RB])
                if kind == "warm":
                    if u == 0:
                        pe.wait_ge(zeros, 2)
                    if u == 2:
                        pe.wait_ge(oT_ready, U * G)
                    stay_warm(pv, n)
                if kind in WIDE:
                    w = fills[s][0]
                    wide = pa[w.place]
                    if w.before:
                        pe.wait_ge(wide_free, w.before)
                if kind == "ctxT":
                    pe.wait_ge(ident, 2)
                    pe.wait_ge(cx_in, 48)
                    for b in range(NB):
                        nc.tensor.transpose(wide[0:CK, b * P:(b + 1) * P], cx[:, b, :], idf[:])
                    nc.tensor.transpose(wide[0:CK, 256:256 + NB * KL], cx[0:NB * KL, 2, :],
                                        idf[0:NB * KL, 0:NB * KL]).then_inc(wide_full, 1)
                elif kind == "xT":
                    pe.wait_ge(xn_ready, TB * (u + 1))
                    for t in range(TB):
                        last = nc.tensor.transpose(wide[:, t * P:(t + 1) * P], xn[:, u * TB + t, :], idf[:])
                    last.then_inc(wide_full, 1)
                elif kind in ("k", "v"):
                    pe.wait_ge(wk_in if kind == "k" else wv_in, 16)
                    pe.wait_ge(wide_free, fills[("ctxT", 0, 0)][0].turn)
                    pe.wait_ge(cT_ready, 2)
                    w = wk if kind == "k" else wv
                    for b in range(NB):
                        nc.tensor.matmul(bank[:, b * P:(b + 1) * P], cxT[:, b * P:(b + 1) * P], w[:], start=True, stop=True)
                    for b in range(NB):
                        last = nc.tensor.matmul(bank[:, 256 + b * P:256 + (b + 1) * P],
                                                cxL[:, b].rearrange("c j k -> c (j k)"), w[:], start=True, stop=True)
                    last.then_inc(ring_full, 1)
                elif kind == "q":
                    pe.wait_ge(wq_in, 16)
                    pe.wait_ge(wide_free, fills[("xT", b, 0)][0].turn)
                    for t in range(UT):
                        last = nc.tensor.matmul(bank[:, t * P:(t + 1) * P],
                                                xnT[:, (UT * u + t) * P:(UT * u + t + 1) * P], wq[:], start=True, stop=True)
                    last.then_inc(ring_full, 1)
                elif kind == "kT":
                    pe.wait_ge(ks_ready[u], 2 * NC + 2)
                    for h in range(H):
                        last = nc.tensor.transpose(wide[:, 64 * h:64 * h + 64].bitcast(BF16), ks[:, u * PR + h // 2, h % 2, :],
                                                   idb[:])
                    last.then_inc(wide_full, 1)
                elif kind == "kLT":
                    pe.wait_ge(ksL_ready, NC)
                    pe.wait_ge(ones_ready, 2 * J)
                    for m in range(NB * G):
                        last = nc.tensor.transpose(bank[:, 64 * m:64 * m + 64].bitcast(BF16), ksL[:, m, :], idb[:])
                    last.then_inc(ring_full, 1)
                elif kind == "qT":
                    pe.wait_ge(qs_base, 3 * (u + 1))
                    pe.wait_ge(qs_equal, 3 * (u + 1))
                    pe.wait_ge(cleared_qs, u + 1)
                    for t in range(UT):
                        for r2 in range(PR):
                            at = 64 * (PR * t + r2)
                            last = nc.tensor.transpose(wide[:, at:at + 64].bitcast(BF16),
                                                       qs[:, UT * u + t, r2].rearrange("p c m -> p (c m)"), idb[:])
                    last.then_inc(wide_full, 1)
                elif kind == "max":
                    t, part = UT * u + n // 5, n % 5
                    if n == 0:
                        pe.wait_ge(wide_free, fills[("kT", b, 0)][0].turn)
                        pe.wait_ge(qT_begun, u + 1)
                    if n == 4:
                        pe.wait_ge(ring_free, freed[at_ring[("kLT", 0, 0)]])
                    if n == 5:
                        pe.wait_ge(wide_free, fills[("qT", u, 0)][0].turn)
                    for r2 in ((2 * part, 2 * part + 1) if part < 4 else range(PR)):
                        w = qT[0:STK, r2, t * P:(t + 1) * P]
                        if part < 4:
                            o = bank[:, 256 * (r2 % 2):256 * (r2 % 2) + 256]
                            m = kT[0:STK, b, 2 * r2:2 * r2 + 2, :].rearrange("p h k -> p (h k)")
                        else:
                            o = bank[:, 64 * r2:64 * r2 + 64]
                            m = kLT[0:STK, b, r2 // 2, 64 * (r2 % 2):64 * (r2 % 2) + 64]
                        last = nc.tensor.matmul(o, w, m, start=True, stop=True)
                    last.then_inc(ring_full, 1)
                elif kind == "shift":
                    pe.wait_ge(shift_ready, u + 1)
                    for t in range(UT):
                        last = nc.tensor.transpose(wide[:, 64 * t:64 * t + 64].bitcast(BF16), ms[:, UT * u + t, :], idb[:])
                    last.then_inc(wide_full, 1)
                elif kind == "score":
                    if n == 0:
                        pe.wait_ge(wide_free, fills[("shift", u, 0)][0].turn)
                    if n == 5:
                        pe.wait_ge(shift_spread, u + 1)
                    w, quarter = fills[s][0]
                    g, c = n // 5, n % 5
                    if quarter == 0 and w.before:
                        pe.wait_ge(wide_free, w.before)
                    o = pa[w.place][:, UQ * quarter:UQ * quarter + UQ]
                    if c < J:
                        h = J * g + c
                        last = nc.tensor.matmul(o, kT[:, b, h, :], qT[:, h // 2, uq], start=True, stop=True)
                    else:
                        for half in range(2):
                            last = nc.tensor.matmul(o[64 * half:64 * half + 64, :],
                                                    kLT[:, b, g, 64 * half:64 * half + 64],
                                                    qT[:, 2 * g + half, uq], start=True, stop=True)
                    if quarter == 3:
                        last.then_inc(wide_full, 1)
                elif kind == "pv":
                    pe.wait_ge(wide_free, wide_of(u, n))
                    pe.wait_ge(v_ready, 3 + 2 * J)
                    if pvs[0]:
                        pe.wait_ge(oT_ready, pvs[0])
                    c0 = 5 * (G * u + n)
                    pieces = [pt[:, ((c0 + c) // 4) % NPT, (c0 + c) % 4, :] for c in range(5)]
                    o = pv
                    nc.tensor.matmul(o[:, 0:UQ], vL[:, b, n].rearrange("p j m -> p (j m)"), pieces[4],
                                     start=True, stop=False, skip_group_check=True)
                    for j in range(J):
                        last = nc.tensor.matmul(o[32 * j:32 * j + 32, 0:UQ], v[:, b, J * n + j, :], pieces[j],
                                                start=False, stop=True, skip_group_check=True)
                    last.then_inc(pv_full, 1)
                    pvs[0] += 1
                elif kind == "turn":
                    pe.wait_ge(oT_ready, G * u + n + 1)
                    for t in range(UT):
                        last = nc.tensor.transpose(bank[:, t * P:(t + 1) * P], oT[:, (G * u + n) % 2, t * P:(t + 1) * P], idf[:])
                    last.then_inc(ring_full, 1)
                elif kind == "back":
                    if n == 0:
                        pe.wait_ge(ring_free, freed[at_ring[("turn", u, G - 1)]])
                    for t in range(UT):
                        src = xn[:, UT * u + t, :] if n else ot[:, u % 2, t, :]
                        last = nc.tensor.transpose(bank[:, t * P:(t + 1) * P], src, idf[:])
                    last.then_inc(ring_full, 1)
                elif kind == "check":
                    pe.wait_ge(tally_ready, 1)
                    nc.tensor.matmul(bank[:, 0:1], ones[:], finec[:], start=True, stop=True).then_inc(ring_full, 1)
                elif kind == "out":
                    pe.wait_ge(ring_free, freed[at_ring[("back", u, n)]])
                    pe.wait_ge(wo_in, 16)
                    for t in range(UT):
                        last = nc.tensor.matmul(bank[:, t * C:(t + 1) * C], onT[:, u % 2, t * P:(t + 1) * P], wo[:],
                                                start=True, stop=True)
                    last.then_inc(ring_full, 1)
                elif kind == "normedT":
                    pe.wait_ge(xn2_ready, UT * (U * n + u + 1))
                    for t in range(UT):
                        last = nc.tensor.transpose(bank[:, t * P:(t + 1) * P], xn2[:, UT * u + t, :], idf[:])
                    last.then_inc(ring_full, 1)
                elif kind == "route":
                    if u == U - 1 and n == 0:
                        pe.wait_ge(ring_free, odd_known)
                        is_odd.append(pe.value_load(odd[0:1, 0:1], min_val=0, max_val=P * P))
                    pe.wait_ge(ring_free, freed[at_ring[("normedT", u, n)]])
                    pe.wait_ge(gw_in, 16)
                    for t in range(UT):
                        last = nc.tensor.matmul(bank[:, t * E:(t + 1) * E], xn2T[:, u % 2, t * P:(t + 1) * P], gw[:],
                                                start=True, stop=True)
                    last.then_inc(ring_full, 1)

            for s in steps:
                step(s)
            with pe.If(is_odd[0] > 0):
                pe.wait_ge(oT_ready, U * G)
                pe.wait_ge(ring_free, last_free)
                pe.wait_ge(gp_mean, 1)
                for b in range(NB):
                    with pe.Fori(0, H) as h:
                        pe.wait_ge(gp_dve, h * GD + (b * H * GD + 4))
                        for n, at, src in ((0, 0, xnT[:, b * NQ:(b + 1) * NQ]), (1, NQ, cxT[:, b * P:(b + 1) * P]),
                                           (1, NQ + P, cxL[:, b, 0, 0:KL])):
                            width = src.shape[-1]
                            rows_ = slice(0, C if n == 0 else CK)
                            nc.tensor.matmul(pa[1][0:D, at:at + width], gw_[rows_, n, :], src, start=True, stop=False)
                            last = nc.tensor.matmul(pa[1][0:D, at:at + width], gb[:, n, :], gone[0:1, 0:width],
                                                    start=False, stop=True)
                        last.then_inc(gp_pe, 1)
                        pe.wait_ge(gp_act, h * GA + (b * H * GA + 1))
                        for t in range(TB):
                            last = nc.tensor.matmul(pa[0][:, 256 * t:256 * t + NK], gqk[:, t * P:(t + 1) * P], gqk[:, NQ:],
                                                    start=True, stop=True)
                        last.then_inc(gp_pe, 1)
                        pe.wait_ge(gp_dve, h * GD + (b * H * GD + 13))
                        for t in range(TB):
                            nc.tensor.transpose(pa[1][:, t * P:(t + 1) * P], gs[:, t, 0:P], idf[:])
                            last = nc.tensor.transpose(pa[1][0:KL, NQ + t * P:NQ + (t + 1) * P], gs[:, t, P:], idf[:])
                        last.then_inc(gp_pe, 1)
                        pe.wait_ge(gp_act, h * GA + (b * H * GA + 4))
                        vf = v[:].rearrange("p b h m -> p (b h m)")
                        vlf = vLf[:].rearrange("p b c -> p (b c)")
                        for t in range(TB):
                            nc.tensor.matmul(pv[:, t * D:(t + 1) * D], gpT[:, t * P:(t + 1) * P],
                                             vf[:, bass.ds(h * 32 + b * H * 32, D)], start=True, stop=False)
                            last = nc.tensor.matmul(pv[:, t * D:(t + 1) * D], gpT[0:KL, NQ + t * P:NQ + (t + 1) * P],
                                                    vlf[0:KL, bass.ds(h * D + b * C, D)], start=False, stop=True)
                        last.then_inc(gp_pe, 1)
                pe.wait_ge(gp_dve, NB * H * GD)
                pe.wait_ge(gp_link, 2)
                nc.tensor.matmul(pv[:, 0:1], gone[:, 0:P], gnc[:], start=True, stop=True)
                for b in range(NB):
                    nc.tensor.matmul(ring[0][:, b * C:(b + 1) * C], gmean, v[:, b, :, 0:D], start=True, stop=False)
                    last = nc.tensor.matmul(ring[0][:, b * C:(b + 1) * C], gmean[0:KL, :], vLf[0:KL, b, :],
                                            start=False, stop=True)
                last.then_inc(gp_mean, 1)
                pe.wait_ge(gp_link, 4)
                for s in again:
                    step(s)
                pe.wait_ge(oh_ready, 2 * U)
            pe.wait_ge(oT_ready, U * G)
            pe.wait_ge(consts2, 8)
            pe.wait_ge(oh_ready, U)
            flat = oh[:].rearrange("p t e -> p (t e)")
            nc.tensor.matmul(pv[:, 0:T * E], tri[:], flat, start=True, stop=False, skip_group_check=True)
            for d in range(1, T):
                nc.tensor.matmul(pv[:, d * E:T * E], ones[:], flat[:, 0:(T - d) * E], start=False, stop=True,
                                 skip_group_check=True)
            for t in range(T):
                last = nc.tensor.matmul(pv[:, T * E:T * E + E], ones[:], flat[:, t * E:(t + 1) * E], start=False, stop=True,
                                        skip_group_check=True)
            last.then_inc(rank_ps, 1)
            pe.wait_ge(b1_in, 16)
            pe.wait_ge(ring_free, last_free)
            nc.tensor.transpose(ring[0][:, 0:E * FC], b1r[:], idf[0:E * FC, 0:E * FC]).then_inc(b1_ps, 1)
            stay_warm(pa[0], WARM[0])
            pe.wait_ge(olo_ready, T + 2)
            for t in range(T):
                last = nc.tensor.matmul(ring[1][:, 0:3 * NBLK], olo[:, t, :], rhs[:, t].rearrange("p a i -> p (a i)"),
                                        start=(t == 0), stop=(t == T - 1))
            last.then_inc(inv_ps, 1)
            stay_warm(pa[0], WARM[1])
            pe.wait_ge(index_ready, 1)
            pe.wait_ge(b1_ready, 1)
            pe.wait_ge(w2_in, 16 * E)
            pe.wait_ge(expert_ready, 2)

            def turn_rows(i):
                pe.wait_ge(gathered[i], 16)
                if i >= 2:
                    pe.wait_ge(xgT_ready, i - 1)
                nc.tensor.transpose(turned[i % 2][:, 0:P], xg[:, i, 0:C], idf[:]).then_inc(xgT_ps, 1)

            def first_half(i):
                pe.wait_ge(xgT_ready, i + 1)
                pe.wait_ge(w1c_ready, i + 1)
                if i >= 2:
                    pe.wait_ge(hb_ready, i - 1)
                for c in range(FC):
                    last = nc.tensor.matmul(pa[i % 2][:, c * P:(c + 1) * P], w1c[:, i % 2, c * P:(c + 1) * P], xgT[:, i % 2],
                                            start=True, stop=True)
                last.then_inc(h_ps, 1)

            def second_half(i):
                e = nc.tensor.value_load(be[0:1, i:i + 1], min_val=0, max_val=E - 1)
                pe.wait_ge(hidden_ready, i + 1)
                if i >= 2:
                    pe.wait_ge(y_read, i - 1)
                for c in range(FC):
                    last = nc.tensor.matmul(ring[i % 2][:, 0:C], hT[:, i % 2, c * P:(c + 1) * P],
                                            w2f[:, bass.ds(e * (FC * C) + c * C, C)], start=(c == 0), stop=(c == FC - 1))
                last.then_inc(y_ps, 1)

            w2f = w2[:].rearrange("p e c n -> p (e c n)")
            used = blocks_used(pe)
            turn_rows(0)
            turn_rows(1)
            first_half(0)
            turn_rows(2)
            first_half(1)
            for i in range(NBLK):
                for_block(pe, used, i + 3, turn_rows)
                for_block(pe, used, i + 2, first_half)
                for_block(pe, used, i, second_half)


NAMES = ["x", "ctx_768", "g_xattn", "g_ffn", "L0_xattn_Wq", "L0_xattn_bq", "L0_xattn_Wk", "L0_xattn_bk",
         "L0_xattn_Wv", "L0_xattn_bv", "L0_xattn_Wo", "L0_xattn_bo", "L0_ffn_gate_w", "L0_ffn_w1",
         "L0_ffn_b1", "L0_ffn_w2", "L0_ffn_b2"]


def kernel(**inputs):
    import numpy as np
    import concourse.bacc as bacc
    from concourse.bass_utils import run_bass_kernel_spmd

    nc = bacc.Bacc("TRN2", target_bir_lowering=False, num_devices=1)
    arrays, a = {}, {}
    for name in NAMES:
        arr = np.ascontiguousarray(inputs[name])
        arrays[f"in_{name}"] = arr
        a[name] = nc.dram_tensor(f"in_{name}", arr.shape, mybir.dt.from_np(arr.dtype), kind="ExternalInput").ap()
    out = nc.dram_tensor("out_x", (NB, NQ, C), F32, kind="ExternalOutput").ap()
    program(nc, a, out)
    r = run_bass_kernel_spmd(nc, [arrays], core_ids=[0])
    return r.results[0]["out_x"]
```
